# Optimizing a Trainium2 kernel written in Bass

```python
import numpy as np
import jax
import jax.numpy as jnp

def _softmax(x, axis=-1):
    return jax.nn.softmax(x, axis=axis)

def _gelu(x):
    return jax.nn.gelu(x, approximate=True)

def _silu(x):
    return jax.nn.silu(x)

def _sigmoid(x):
    return jax.nn.sigmoid(x)

def _layernorm(x, axis=-1, eps=1e-05):
    m = jnp.mean(x, axis=axis, keepdims=True)
    v = jnp.var(x, axis=axis, keepdims=True)
    return (x - m) / jnp.sqrt(v + eps)

def _scatter_add(tgt, idx, src, axis=0):
    return tgt.at[idx].add(src)

def _segment_sum(src, seg, n):
    return jax.ops.segment_sum(src, seg, n)
kernel_name = 'mk_sandwich_d1_jaxref_r8_185eba'

def setup_inputs(seed: int=0):
    np.random.seed(seed)
    _w = jnp.asarray

    def _L0_attn_setup():
        import jax, jax.numpy as jnp
        import numpy as np
        import math
        EMBED = 128
        HEADS = 16
        HEAD_DIM = EMBED // HEADS
        HIDDEN = 512
        NUM_BUCKETS = 32
        MAX_DISTANCE = 128
        LN_EPS = 1e-06
        KQ_EPS = 1e-06

        def _rms_norm(xs, weight):
            xf = xs.astype(jnp.float32)
            var = jnp.mean(jnp.square(xf), axis=-1, keepdims=True)
            ys = xs * jax.lax.rsqrt(var + LN_EPS) * weight
            return ys.astype(xs.dtype)

        def _normalize_kq(kq):
            ss = jnp.sum(jnp.square(kq), axis=-1, keepdims=True)
            return kq * jax.lax.rsqrt(ss + KQ_EPS)

        def _rel_position_bucket(rp):
            rp = -jnp.minimum(rp, 0)
            max_exact = NUM_BUCKETS // 2
            is_small = rp < max_exact
            safe = jnp.maximum(rp, 1).astype(jnp.float32)
            large = max_exact + (jnp.log(safe / max_exact) / math.log(MAX_DISTANCE / max_exact) * (NUM_BUCKETS - max_exact)).astype(jnp.int32)
            large = jnp.minimum(large, NUM_BUCKETS - 1)
            return jnp.where(is_small, rp, large)
        key = jax.random.key(seed)
        ks = jax.random.split(key, 8)
        B, S = (2, 256)
        w = 0.02
        return {'x': jax.random.normal(ks[0], (B, S, EMBED), dtype=jnp.float32), 'ln1_w': jnp.ones((EMBED,), jnp.float32), 'Wq': jax.random.normal(ks[1], (EMBED, EMBED), jnp.float32) * w, 'Wk': jax.random.normal(ks[2], (EMBED, EMBED), jnp.float32) * w, 'Wv': jax.random.normal(ks[3], (EMBED, EMBED), jnp.float32) * w, 'rel_bias': jax.random.normal(ks[4], (NUM_BUCKETS, HEADS), jnp.float32) * w, 'scale': jnp.ones((HEADS,), jnp.float32), 'Wo': jax.random.normal(ks[5], (EMBED, EMBED), jnp.float32) * w, 'ln2_w': jnp.ones((EMBED,), jnp.float32), 'W1': jax.random.normal(ks[6], (EMBED, HIDDEN), jnp.float32) * w, 'W2': jax.random.normal(ks[7], (HIDDEN, EMBED), jnp.float32) * w}
    _L0_attn_in = _L0_attn_setup()

    def _L0_ffn_setup():
        import jax, jax.numpy as jnp
        import numpy as np
        H = 128
        I = 352
        E = 8
        TOP_K = 2

        def _moe(hidden_states, router_w, gate_w, up_w, down_w):
            B, S, Hd = hidden_states.shape
            x = hidden_states.reshape(-1, Hd)
            logits = x @ router_w.T
            probs = jax.nn.softmax(logits.astype(jnp.float32), axis=-1)
            top_w, top_idx = jax.lax.top_k(probs, TOP_K)
            top_w = top_w.astype(x.dtype)
            onehot = jax.nn.one_hot(top_idx, E, dtype=x.dtype)
            w_te = jnp.einsum('tk,tke->te', top_w, onehot)
            g = jnp.einsum('th,eih->tei', x, gate_w)
            u = jnp.einsum('th,eih->tei', x, up_w)
            h = jax.nn.silu(g) * u
            y = jnp.einsum('tei,ehi,te->th', h, down_w, w_te)
            return y.reshape(B, S, Hd)
        key = jax.random.key(seed)
        ks = jax.random.split(key, 5)
        s = 0.02
        return {'hidden_states': jax.random.normal(ks[0], (2, 128, H), dtype=jnp.float32), 'router_w': jax.random.normal(ks[1], (E, H), dtype=jnp.float32) * s, 'gate_w': jax.random.normal(ks[2], (E, I, H), dtype=jnp.float32) * s, 'up_w': jax.random.normal(ks[3], (E, I, H), dtype=jnp.float32) * s, 'down_w': jax.random.normal(ks[4], (E, H, I), dtype=jnp.float32) * s}
    _L0_ffn_in = _L0_ffn_setup()
    _d = {'L0_attn_x': _L0_attn_in['x'], 'L0_attn_ln1_w': _L0_attn_in['ln1_w'], 'L0_attn_Wq': _L0_attn_in['Wq'], 'L0_attn_Wk': _L0_attn_in['Wk'], 'L0_attn_Wv': _L0_attn_in['Wv'], 'L0_attn_rel_bias': _L0_attn_in['rel_bias'], 'L0_attn_scale': _L0_attn_in['scale'], 'L0_attn_Wo': _L0_attn_in['Wo'], 'L0_attn_ln2_w': _L0_attn_in['ln2_w'], 'L0_attn_W1': _L0_attn_in['W1'], 'L0_attn_W2': _L0_attn_in['W2'], 'L0_ffn_router_w': _L0_ffn_in['router_w'], 'L0_ffn_gate_w': _L0_ffn_in['gate_w'], 'L0_ffn_up_w': _L0_ffn_in['up_w'], 'L0_ffn_down_w': _L0_ffn_in['down_w']}
    _x0 = _d['L0_attn_x']
    _d['L0_attn_x'] = jax.random.normal(jax.random.fold_in(jax.random.key(seed), 1), (8, 512, 128), dtype=_x0.dtype)
    del _x0
    return _d

def reference(L0_attn_x, L0_attn_ln1_w, L0_attn_Wq, L0_attn_Wk, L0_attn_Wv, L0_attn_rel_bias, L0_attn_scale, L0_attn_Wo, L0_attn_ln2_w, L0_attn_W1, L0_attn_W2, L0_ffn_router_w, L0_ffn_gate_w, L0_ffn_up_w, L0_ffn_down_w):

    def _L0_attn_ref(x, ln1_w, Wq, Wk, Wv, rel_bias, scale, Wo, ln2_w, W1, W2):
        import jax, jax.numpy as jnp
        import numpy as np
        import math
        EMBED = 128
        HEADS = 16
        HEAD_DIM = EMBED // HEADS
        HIDDEN = 512
        NUM_BUCKETS = 32
        MAX_DISTANCE = 128
        LN_EPS = 1e-06
        KQ_EPS = 1e-06

        def _rms_norm(xs, weight):
            xf = xs.astype(jnp.float32)
            var = jnp.mean(jnp.square(xf), axis=-1, keepdims=True)
            ys = xs * jax.lax.rsqrt(var + LN_EPS) * weight
            return ys.astype(xs.dtype)

        def _normalize_kq(kq):
            ss = jnp.sum(jnp.square(kq), axis=-1, keepdims=True)
            return kq * jax.lax.rsqrt(ss + KQ_EPS)

        def _rel_position_bucket(rp):
            rp = -jnp.minimum(rp, 0)
            max_exact = NUM_BUCKETS // 2
            is_small = rp < max_exact
            safe = jnp.maximum(rp, 1).astype(jnp.float32)
            large = max_exact + (jnp.log(safe / max_exact) / math.log(MAX_DISTANCE / max_exact) * (NUM_BUCKETS - max_exact)).astype(jnp.int32)
            large = jnp.minimum(large, NUM_BUCKETS - 1)
            return jnp.where(is_small, rp, large)
        B, S, E = x.shape
        xn = _rms_norm(x, ln1_w)
        q = (xn @ Wq).reshape(B, S, HEADS, HEAD_DIM)
        k = (xn @ Wk).reshape(B, S, HEADS, HEAD_DIM)
        v = (xn @ Wv).reshape(B, S, HEADS, HEAD_DIM)
        q = _normalize_kq(q)
        k = _normalize_kq(k)
        pos = jnp.arange(S, dtype=jnp.int32)
        bucket = _rel_position_bucket(pos[None, :] - pos[:, None])
        bias = rel_bias[bucket]
        bias = jnp.transpose(bias, (2, 0, 1))[None]
        attn = jnp.einsum('bqhd,bkhd->bhqk', q, k) + bias
        attn = attn * scale[None, :, None, None]
        causal = pos[None, :] - pos[:, None] < 0
        attn = jnp.where(causal[None, None], attn, -1000000.0)
        attn = jax.nn.softmax(attn, axis=-1)
        y = jnp.einsum('bhqk,bkhd->bqhd', attn, v).reshape(B, S, E)
        y = y @ Wo + x
        z = _rms_norm(y, ln2_w)
        z = jax.nn.relu(z @ W1) @ W2
        return z + y

    def _L0_ffn_ref(hidden_states, router_w, gate_w, up_w, down_w):
        import jax, jax.numpy as jnp
        import numpy as np
        H = 128
        I = 352
        E = 8
        TOP_K = 2

        def _moe(hidden_states, router_w, gate_w, up_w, down_w):
            B, S, Hd = hidden_states.shape
            x = hidden_states.reshape(-1, Hd)
            logits = x @ router_w.T
            probs = jax.nn.softmax(logits.astype(jnp.float32), axis=-1)
            top_w, top_idx = jax.lax.top_k(probs, TOP_K)
            top_w = top_w.astype(x.dtype)
            onehot = jax.nn.one_hot(top_idx, E, dtype=x.dtype)
            w_te = jnp.einsum('tk,tke->te', top_w, onehot)
            g = jnp.einsum('th,eih->tei', x, gate_w)
            u = jnp.einsum('th,eih->tei', x, up_w)
            h = jax.nn.silu(g) * u
            y = jnp.einsum('tei,ehi,te->th', h, down_w, w_te)
            return y.reshape(B, S, Hd)
        return _moe(hidden_states, router_w, gate_w, up_w, down_w)
    x = L0_attn_x
    x = x + _layernorm(_L0_attn_ref(_layernorm(x, axis=-1), L0_attn_ln1_w, L0_attn_Wq, L0_attn_Wk, L0_attn_Wv, L0_attn_rel_bias, L0_attn_scale, L0_attn_Wo, L0_attn_ln2_w, L0_attn_W1, L0_attn_W2), axis=-1)
    x = x + _layernorm(_L0_ffn_ref(_layernorm(x, axis=-1), L0_ffn_router_w, L0_ffn_gate_w, L0_ffn_up_w, L0_ffn_down_w), axis=-1)
    return x

_drawn_inputs = setup_inputs


def setup_inputs(seed=0):
    import zlib

    import numpy as np

    out = dict(_drawn_inputs(seed))
    spreads = {'L0_attn_ln1_w': (1.0, 0.6), 'L0_attn_scale': (1.0, 0.6), 'L0_attn_ln2_w': (1.0, 0.6)}
    factors = {'L0_attn_Wq': 8.0,
     'L0_attn_Wk': 7.478,
     'L0_attn_Wv': 4.744,
     'L0_attn_rel_bias': 8.0,
     'L0_attn_Wo': 4.157}
    for name, (base, spread) in spreads.items():
        noise = np.random.default_rng([zlib.crc32(name.encode()), seed]).standard_normal(out[name].shape)
        drawn = base * np.exp(spread * noise) if base else spread * noise
        out[name] = jnp.asarray(drawn.astype(out[name].dtype))
    for name, factor in factors.items():
        out[name] = (out[name] * factor).astype(out[name].dtype)
    return out
```

```python
from contextlib import ExitStack

import numpy as np
import concourse.bass as bass
from concourse import mybir

ALU = mybir.AluOpType
ACT = mybir.ActivationFunctionType
AX = mybir.AxisListType.X
F32 = mybir.dt.float32
BF16 = mybir.dt.bfloat16
I32 = mybir.dt.int32

P = 128
NEG = -1.0e30
UNITS = 5
GROUPS = 4
NU = UNITS * GROUPS
LN_EPS = 1e-5
RMS_EPS = 1e-6
KQ_EPS = 1e-6
NO_ROW = 1 << 20
RSQRT_SEED = float(0x5F3759DF)


def bucket_starts(buckets, max_distance):
    exact = buckets // 2
    d = np.arange(1, 4 * max_distance)
    big = exact + (np.log((d / exact).astype(np.float32)) / np.float32(np.log(max_distance / exact))
                   * (buckets - exact)).astype(np.int32)
    of = np.where(d < exact, d, np.minimum(big, buckets - 1))
    return [int(d[np.argmax(of >= r)]) for r in range(exact, buckets)]


def block_kernel(nc, x_d, ln1_d, wq_d, wk_d, wv_d, rel_d, scale_d, wo_d, ln2_d, w1_d, w2_d,
                 router_d, gate_d, up_d, down_d, out_d):
    NB, S, D = x_d.shape
    BUCKETS, H = rel_d.shape
    DH = D // H
    HID = w1_d.shape[1]
    E, I, _ = gate_d.shape
    T = S // P
    NT = NB * T
    NTOK = NB * S
    HC = HID // P
    IC = [(c * P, min(P, I - c * P)) for c in range((I + P - 1) // P)]
    REGION = NTOK + P
    DUMMY = E * REGION
    STILES = (2 * NTOK) // P + E
    ROW = D + 2
    WEXP = 2 * I + len(IC) * P
    starts = bucket_starts(BUCKETS, 128)
    assert (S, D, DH, T, H) == (512, P, 8, 4, 16) and STILES % 4 == 0

    slots_d = nc.dram_tensor("slots", [(E * REGION + P), ROW], F32)
    ytok_d = nc.dram_tensor("ytok", [2 * NTOK, D], F32)
    parts_d = nc.dram_tensor("parts", [2, 2, 3, P, S], BF16)
    toe_d = nc.dram_tensor("toe", [H, P, 3 * P], F32)
    cm_d = nc.dram_tensor("cm", [H, P], F32)
    cfar_d = nc.dram_tensor("cfar", [H, 1], F32)

    with ExitStack() as ctx:
        def sb(name, shape, dt=F32):
            return ctx.enter_context(nc.sbuf_tensor(name, shape, dt))

        def sem(name):
            return ctx.enter_context(nc.semaphore(name))

        X = sb("X", [P, NT, D])
        XA = sb("XA", [P, NT, D])
        arena = sb("arena", [P, 8192 + 6144 + 4096 + 2048 + 5120])
        KS = arena[:, 0:4096].bitcast(BF16).rearrange("p (h t) -> p h t", h=H)
        QS = arena[:, 4096:8192].bitcast(BF16).rearrange("p (h t) -> p h t", h=H)
        TAB = arena[:, 8192:14336].rearrange("p (h c) -> p h c", h=H)
        V2 = [arena[:, 14336 + 2048 * r:14336 + 2048 * (r + 1)].rearrange("p (t c) -> p t c", t=T) for r in range(2)]
        V2F = [arena[:, 18432 + 1024 * r:18432 + 1024 * (r + 1)].rearrange("p (t c) -> p t c", t=2) for r in range(2)]
        EB = [arena[:, 20480 + 1024 * u:20480 + 1024 * (u + 1)] for u in range(UNITS)]
        WALL = arena[:, 0:E * WEXP]
        STG = arena[:, E * WEXP:E * WEXP + 3 * E * I]
        WG_N = STG[:, 0:E * I].rearrange("p (n c) -> p n c", c=P)
        WU_N = STG[:, E * I:2 * E * I].rearrange("p (n c) -> p n c", c=P)
        WD_N = STG[:, 2 * E * I:3 * E * I].rearrange("p (e i) -> p e i", e=E)

        WQKV = sb("WQKV", [P, 3 * D])
        WO = sb("WO", [P, D])
        W1 = sb("W1", [P, HID])
        W2 = sb("W2", [P, HC, D])
        RT = sb("RT", [P, E])
        LNW = sb("LNW", [P, 2])
        SCB = sb("SCB", [P, H])
        IDN = sb("IDN", [P, P])
        TRI = sb("TRI", [P, P])
        ONES = sb("ONES", [P, P])
        ST = sb("ST", [P, NT, 6])
        MV = sb("MV", [P, NT, 2])
        RS0 = sb("RS0", [P, NT])
        RR0 = sb("RR0", [P, NT])
        NWA = sb("NWA", [P, P])
        NWB = sb("NWB", [P, P])
        NWC = sb("NWC", [P, P])
        XAR = sb("XAR", [P, T, D])
        XART = sb("XART", [P, S])
        XSUM = sb("XSUM", [P, NB])
        QK = sb("QK", [P, T, 2 * D])
        SQ = sb("SQ", [P, T, 2 * D])
        SS = sb("SS", [P, T * 2 * H])
        RSQ = sb("RSQ", [P, T * 2 * H])
        PF = sb("PF", [P, 2, S])
        PP = sb("PP", [P, 2, 3, S], BF16)
        OS = sb("OS", [P, 2, S])
        RD = sb("RD", [P, T, H])
        YN = sb("YN", [P, T, D])
        YT = sb("YT", [P, S])
        Y = sb("Y", [P, T, D])
        Z = sb("Z", [P, T, D])
        YQ = Z
        ZT = sb("ZT", [P, S])
        H1T = sb("H1T", [P, HC, S])
        A = sb("A", [P, T, D])
        STP = sb("STP", [P, 2, T, 6])
        MVP = sb("MVP", [P, 2, T, 2])
        SSY = sb("SSY", [P, T])
        RZ = sb("RZ", [P, 4, T])
        MH = sb("MH", [P, T])
        XB = [sb(f"XB{r}", [P, T, 2, ROW]) for r in range(2)]
        XBT = sb("XBT", [P, S])
        LG = sb("LG", [P, T, E])
        LG2 = sb("LG2", [P, T, E])
        OH = sb("OH", [P, 2, T, E])
        EQ = sb("EQ", [P, T, E])
        REV = sb("REV", [P, T, E])
        MX = sb("MX", [P, 4, T])
        EX = sb("EX", [P, T, E + 1])
        MM = sb("MM", [P, T, E])
        TB = sb("TB", [P, T + 1, E])
        POS = sb("POS", [P, T, E])
        PSEL = sb("PSEL", [P, 2, T, E])
        POSF = sb("POSF", [P, 2, T])
        IDX = [sb(f"IDX{r}", [P, 2, T], I32) for r in range(2)]
        PADX = sb("PADX", [P, ROW])
        PADI = sb("PADI", [P, E], I32)
        PADF = sb("PADF", [P, E])
        EROW = sb("EROW", [P, E])
        PCOL = sb("PCOL", [P, 1])
        NTE = sb("NTE", [P, E], I32)
        NTF = sb("NTF", [P, 3, E])
        SIO = sb("SIO", [P, STILES])
        SRF = sb("SRF", [P, 2, STILES])
        SRI = sb("SRI", [P, 2, STILES], I32)
        rows = SQ[0:H, 0:3, :].rearrange("p a b -> p (a b)")
        BR, CMR, RB = rows[:, 0:3 * P], rows[:, 3 * P:4 * P], rows[:, 4 * P:4 * P + BUCKETS]
        GM, SCP = rows[:, 5 * P:5 * P + 1], rows[:, 5 * P + 1:5 * P + 2]
        CF = sb("CF", [P, H])
        WRAW = OS[:, :, :].rearrange("p a b -> p (a b)")[:, 0:3 * D]
        W1R = OS[:, :, :].rearrange("p a b -> p (a b)")[:, 3 * D:3 * D + HID]
        SCM = H1T[:, :, :].rearrange("p a b -> p (a b)")[:, 0:2 * STILES * E].rearrange("p (k s e) -> p k s e", k=2, e=E)
        CMB = H1T[:, :, :].rearrange("p a b -> p (a b)").rearrange("p (h c) -> p h c", h=H)
        XG = [X_ for X_ in (sb("XG0", [P, ROW]), sb("XG1", [P, ROW]), sb("XG2", [P, ROW]), sb("XG3", [P, ROW]))]
        MT = [sb(f"MT{r}", [P, 2]) for r in range(4)]
        XGT = [XART[:, 0:P], XART[:, P:2 * P]]
        SG = [QK[:, 0, :], QK[:, 1, :]]
        SGB = [PF[:, r, 0:I] for r in range(2)]
        HS = [OS[:, r, 0:I] for r in range(2)]
        HTB = [H1T[:, r, 0:len(IC) * P] for r in range(2)]
        YS = [YN[:, r, :] for r in range(4)]

        SC = ctx.enter_context(nc.psum_tensor("SC", [P, 2, 1024], F32))
        OA = ctx.enter_context(nc.psum_tensor("OA", [P, 2, 512], F32))
        M0 = ctx.enter_context(nc.psum_tensor("M0", [P, 512], F32))
        M1 = ctx.enter_context(nc.psum_tensor("M1", [P, 512], F32))

        x_in = [sem(f"x_in{i}") for i in range(4)]
        w_in = sem("w_in")
        w2_in = sem("w2_in")
        const_rdy = sem("const_rdy")
        wq_rdy = sem("wq_rdy")
        bias_rows = sem("bias_rows")
        bias_dram = sem("bias_dram")
        bias_in = sem("bias_in")
        tab_raw = sem("tab_raw")
        tab_exp = sem("tab_exp")
        tab_rdy = sem("tab_rdy")
        v2_const = sem("v2_const")
        ks_zero = sem("ks_zero")
        ln0 = sem("ln0")
        xa_rdy = sem("xa_rdy")
        dve_step = sem("dve_step")
        pool_step = sem("pool_step")
        xar_rdy = sem("xar_rdy")
        m0_full, m0_free = sem("m0_full"), sem("m0_free")
        m1_full, m1_free = sem("m1_full"), sem("m1_free")
        v2f_rdy = sem("v2f_rdy")
        sq_rdy = sem("sq_rdy")
        qk_norm = sem("qk_norm")
        part_dve = sem("part_dve")
        part_pool = sem("part_pool")
        parts_out = sem("parts_out")
        kq_in = [sem("kq_in0"), sem("kq_in1")]
        qk_done = sem("qk_done")
        exp_done = sem("exp_done")
        mul_dve, mul_pool = sem("mul_dve"), sem("mul_pool")
        pv_done = sem("pv_done")
        o_out = sem("o_out")
        ysq = sem("ysq")
        ssy_rdy = sem("ssy_rdy")
        z_rdy = sem("z_rdy")
        a_stat = sem("a_stat")
        a_rstd = sem("a_rstd")
        a_ln = sem("a_ln")
        x1_rdy = sem("x1_rdy")
        x1_stat = sem("x1_stat")
        x1_rstd = sem("x1_rstd")
        xb_rdy = sem("xb_rdy")
        route_d = sem("route_d")
        route_e = sem("route_e")
        route_m = sem("route_m")
        route_w = sem("route_w")
        idx_rdy = sem("idx_rdy")
        dest_rdy = sem("dest_rdy")
        scattered = [sem("scattered0"), sem("scattered1")]
        pool_rem = sem("pool_rem")
        z_root = sem("z_root")
        dummy_out = sem("dummy_out")
        pad_rdy = sem("pad_rdy")
        pad_out = sem("pad_out")
        table_rdy = sem("table_rdy")
        stg_in = sem("stg_in")
        wt_full, wt_free = sem("wt_full"), [sem("wt_free0"), sem("wt_free1")]
        xg_in = [sem(f"xg_in{i}") for i in range(4)]
        xt_full, xt_rdy, meta_rdy = sem("xt_full"), sem("xt_rdy"), sem("meta_rdy")
        gu_full, sg_rdy, h_rdy = sem("gu_full"), sem("sg_rdy"), sem("h_rdy")
        ht_full, ht_rdy = sem("ht_full"), sem("ht_rdy")
        y_full, ys_rdy = sem("y_full"), sem("ys_rdy")
        ys_out = [sem(f"ys_out{i}") for i in range(4)]
        yt_in = [sem("yt_in0"), sem("yt_in1")]
        f_stat, f_rstd, f_ln, f_out = sem("f_stat"), sem("f_rstd"), sem("f_ln"), sem("f_out")
        out_done = [sem("out_done0"), sem("out_done1")]

        block = ctx.enter_context(nc.Block())
        x_v = x_d.rearrange("b (i p) d -> p (b i) d", p=P)
        out_v = out_d.rearrange("b (i p) d -> p (b i) d", p=P)

        N_W, N_W2 = 8, 4
        HX = NT // 4

        USES0 = 7
        USES1 = 14
        (R_O0, R_O1, R_V, R_YT, R_Y, R_ZT, R_H, R_A, R_XT, R_L, R_C) = (0, 1, 2, 3, 4, 5, 6, 10, 11, 12, 13)

        def col(g, j):
            return 8 * (g // 2) + 2 * j + g % 2

        FY = [arena[:, 17152 + 1024 * r:17152 + 1024 * (r + 1)].rearrange("p (k t d) -> p k t d", k=2, t=T) for r in range(2)]

        blocks = []
        for m, src in enumerate((WG_N, WU_N)):
            for n in range(E * I // P):
                blocks.append(("gu", m, n))
        for e in range(E):
            for c in range(len(IC)):
                blocks.append(("d", e, c))
        lots = [blocks[i:i + 4] for i in range(0, len(blocks), 4)]
        NWT = len(lots)

        def pieces(kind, a, c):
            if kind == "d":
                return [(IC[c][1], 0, P, a * WEXP + 2 * I + P * c)]
            out, r0 = [], c * P
            while r0 < (c + 1) * P:
                e, i = divmod(r0, I)
                n = min(I - i, (c + 1) * P - r0)
                out.append((P, r0 - c * P, n, e * WEXP + I * a + i))
                r0 += n
            return out

        def copy_lot(copy, i, lot, eng):
            todo = [(dst, SC[0:k, i % 2, P * j + c0:P * j + c0 + n])
                    for j, blk in enumerate(lot) for k, c0, n, at in pieces(*blk)
                    for dst in [WALL[0:k, at:at + n]]]
            for j, (dst, src) in enumerate(todo):
                ins = copy(dst, src)
            ins.then_inc(wt_free[i % 2], 1)

        def mul_first(eng, g, u):
            e = EB[u].rearrange("p (j c) -> p j c", j=2)
            h0 = col(g, 2 * u)
            tab = TAB[:, h0:h0 + 3:2, :].rearrange("p j (a c) -> p j a c", a=3)[:, :, 0:3:2, :]
            v = e[:, :, 0:256].rearrange("p j (a c) -> p j a c", a=2)
            return eng.tensor_tensor(v, v, tab, ALU.mult)

        def mul_mid(eng, g, u):
            e = EB[2 + u].rearrange("p (j c) -> p j c", j=2)
            h0 = col(g, 2 * u)
            a, z = e[:, :, 0:256], e[:, :, 384:512]
            return [eng.tensor_tensor(a, a, TAB[:, h0:h0 + 3:2, P:3 * P], ALU.mult),
                    eng.tensor_tensor(z, z, TAB[:, h0:h0 + 3:2, P:2 * P], ALU.mult)]

        def store(sp, b):
            sp.wait_ge(f_out, b + 1)
            sp.dma_start(out_v[:, T * b:T * (b + 1), :], X[:, T * b:T * (b + 1), :]).then_inc(out_done[b % 2], 16)

        def expert_weights(pe):
            pe.wait_ge(stg_in, 48)
            pe.wait_ge(exp_done, NU * NB)
            for n, lot in enumerate(lots):
                if n >= 2:
                    pe.wait_ge(wt_free[n % 2], n // 2)
                for i, (kind, a, c) in enumerate(lot):
                    dst = SC[:, n % 2, P * i:P * (i + 1)]
                    if kind == "gu":
                        mm = pe.transpose(dst, (WG_N, WU_N)[a][:, c, :], IDN[:, :])
                    else:
                        i0, k = IC[c]
                        mm = pe.transpose(dst[0:k, :], WD_N[:, a, i0:i0 + k], IDN[:, :])
                mm.then_inc(wt_full, 1)

        @block.sync
        def _(sp):
            for i in range(4):
                sp.dma_start(X[:, HX * i:HX * (i + 1), :], x_v[:, HX * i:HX * (i + 1), :]).then_inc(x_in[i], 16)
            with nc.allow_non_contiguous_dma(reason="small vectors"):
                sp.dma_start(RB[:, :], rel_d.rearrange("r h -> h r")).then_inc(w_in, 16)
                sp.dma_start(SCP[:, :], scale_d.rearrange("(h a) -> h a", a=1)).then_inc(w_in, 16)
                sp.dma_start(LNW[:, 0:1], ln1_d.rearrange("(h a) -> h a", a=1)).then_inc(w_in, 16)
                sp.dma_start(LNW[:, 1:2], ln2_d.rearrange("(h a) -> h a", a=1)).then_inc(w_in, 16)
                sp.dma_start(SCB[:, :], bass.AP(scale_d.tensor, scale_d.offset, [[0, P], [1, H]])).then_inc(w_in, 16)
                for n, w in enumerate((wq_d, wk_d, wv_d)):
                    sp.dma_start(WRAW[:, n * D:(n + 1) * D], w).then_inc(w_in, 16)
                sp.dma_start(W1R, w1_d).then_inc(w2_in, 16)
                sp.dma_start(W2[:, :, :], w2_d.rearrange("(c p) n -> p c n", p=P)).then_inc(w2_in, 16)
                sp.dma_start(RT[:, :], router_d.rearrange("e h -> h e")).then_inc(w2_in, 16)
                sp.dma_start(WO[:, :], wo_d).then_inc(w2_in, 16)
            sp.wait_ge(bias_rows, 1)
            with nc.allow_non_contiguous_dma(reason="broadcasts"):
                sp.dma_start(toe_d.ap(), BR.unsqueeze(1).broadcast_to([H, P, 3 * P])).then_inc(bias_dram, 16)
                sp.dma_start(cm_d.ap(), CMR[:, :]).then_inc(bias_dram, 16)
                sp.dma_start(cfar_d.ap(), BR[:, 3 * P - 1:3 * P]).then_inc(bias_dram, 16)
                sp.wait_ge(bias_dram, 48)
                sp.dma_start(TAB[:, :, P:3 * P], bass.AP(toe_d, P, [[3 * P - 1, P], [3 * P * P, H], [1, 2 * P]])).then_inc(bias_in, 16)
                sp.dma_start(CMB, bass.AP(cm_d, 0, [[0, P], [P, H], [1, P]])).then_inc(bias_in, 16)
                sp.dma_start(CF[:, :], bass.AP(cfar_d, 0, [[0, P], [1, H]])).then_inc(bias_in, 16)
            sp.wait_ge(const_rdy, 1)
            sp.dma_start(slots_d.ap()[DUMMY:DUMMY + P, :], PADX[:, :]).then_inc(dummy_out, 16)

            def stack(b):
                r = b % 2
                for m in range(2):
                    sp.wait_ge(part_pool, 2 * b + m + 1)
                    sp.dma_start(parts_d.ap()[r, m].rearrange("c p t -> p c t"), PP[:, m, :, :]).then_inc(parts_out, 16)
                sp.wait_ge(parts_out, 32 * (b + 1))
                if b == 0:
                    sp.wait_ge(ks_zero, 2)
                for half in range(2):
                    hs = slice(8 * half, 8 * half + 8)
                    if b > 0:
                        sp.wait_ge(qk_done, NU * (b - 1) + NU // 2 * (half + 1))
                    src = parts_d.ap()[r].rearrange("m c (d h) t -> m c d h t", h=H)
                    for c in range(3):
                        sp.dma_start(KS[24 * c:24 * c + 24, hs, :],
                                     parts_d.ap()[r, 1].rearrange("c (d h) t -> (c d) h t", h=H)[:, hs, :]
                                     ).then_inc(kq_in[half], 16)
                        for a in range(3):
                            sp.dma_start(QS[8 * (3 * c + a):8 * (3 * c + a) + 8, hs, :], src[0, c, :, hs, :]
                                         ).then_inc(kq_in[half], 16)

            for b in range(NB):
                stack(b)
            sp.wait_ge(pv_done, 3 * GROUPS * NB)
            sp.dma_start(WG_N, gate_d.rearrange("e i h -> (e i) h").rearrange("(n p) h -> p n h", p=P)).then_inc(stg_in, 16)
            sp.dma_start(WU_N, up_d.rearrange("e i h -> (e i) h").rearrange("(n p) h -> p n h", p=P)).then_inc(stg_in, 16)
            sp.dma_start(WD_N, down_d.rearrange("e h i -> h e i")).then_inc(stg_in, 16)

            sp.wait_ge(table_rdy, 1)
            for r in range(2):
                sp.wait_ge(scattered[r], 16 * NT)
            sp.wait_ge(pad_out, 16 * E)
            sp.wait_ge(dummy_out, 16)

            def load(s, r, row):
                sp.dma_start(XG[r][:, :], slots_d.ap()[bass.ds(row, P), :]).then_inc(xg_in[r], 16)

            for s in range(4):
                row = sp.value_load(SRI[0:1, 0, s:s + 1], min_val=0, max_val=DUMMY)
                load(s, s, row)
            with sp.Fori(1, STILES // 4) as it:
                for r in range(4):
                    row = sp.value_load(SRI[0:1, 0, bass.ds(4 * it + r, 1)], min_val=0, max_val=DUMMY)
                    sp.wait_ge(xt_full, 4 * it + r - 3)
                    sp.wait_ge(meta_rdy, 4 * it + r - 3)
                    load(None, r, row)

            for r in range(4):
                sp.wait_ge(ys_out[r], 16 * STILES // 4)
            yt_v = ytok_d.ap().rearrange("(k n p) d -> k p n d", k=2, p=P)
            for b in range(NB):
                r = b % 2
                if b >= 2:
                    sp.wait_ge(f_stat, b - 1)
                for k in range(2):
                    sp.dma_start(FY[r][:, k, :, :], yt_v[k, :, T * b:T * (b + 1), :]).then_inc(yt_in[r], 16)
                if b >= 1:
                    store(sp, b - 1)
            store(sp, NB - 1)
            for r in range(2):
                sp.wait_ge(out_done[r], 16 * NB // 2)

        @block.tensor
        def _(pe):
            def take0(b, k):
                if USES0 * b + k > 0:
                    pe.wait_ge(m0_free, USES0 * b + k)

            def take1(b, k):
                if USES1 * b + k > 0:
                    pe.wait_ge(m1_free, USES1 * b + k)

            def turn4(bank, src, full):
                for t in range(T):
                    mm = pe.transpose(bank[:, P * t:P * (t + 1)], src[:, t, :], IDN[:, :])
                mm.then_inc(full, 1)

            def pre_xt(b):
                take0(b, 0)
                pe.wait_ge(xar_rdy, b + 1)
                turn4(M0, XAR, m0_full)

            def pre_qkv(b, t):
                take0(b, 1 + t)
                if b == 0 and t == 0:
                    pe.wait_ge(wq_rdy, 1)
                pe.matmul(M0[:, 0:3 * D], XART[:, P * t:P * (t + 1)], WQKV[:, :], start=True, stop=True).then_inc(m0_full, 1)

            def pre_turn(b, m):
                take0(b, 5 + m)
                pe.wait_ge(qk_norm, b + 1)
                for t in range(T):
                    mm = pe.transpose(M0[:, P * t:P * (t + 1)], QK[:, t, D * m:D * (m + 1)], IDN[:, :])
                mm.then_inc(m0_full, 1)

            def scores(b, n):
                g, u = divmod(n, UNITS)
                if NU * b + n >= 2:
                    pe.wait_ge(exp_done, NU * b + n - 1)
                if u == 0 and g % 2 == 0:
                    pe.wait_ge(kq_in[g // 2], 16 * 12 * (b + 1))
                s = SC[:, n % 2, :]
                if u < 2:
                    for i in range(2):
                        h = col(g, 2 * u + i)
                        mm = pe.matmul(s[:, 512 * i:512 * i + 512], KS[:, h, 0:P], QS[:, h, :], start=True, stop=True)
                elif u < 4:
                    for i in range(2):
                        h = col(g, 2 * (u - 2) + i)
                        pe.matmul(s[:, 512 * i:512 * i + 384], KS[:, h, P:2 * P], QS[:, h, P:4 * P], start=True, stop=True)
                        mm = pe.matmul(s[:, 512 * i + 384:512 * i + 512], KS[:, h, 3 * P:4 * P], QS[:, h, 3 * P:4 * P],
                                       start=True, stop=True)
                else:
                    for i in range(4):
                        h = col(g, i)
                        mm = pe.matmul(s[:, 256 * i:256 * i + 256], KS[:, h, 2 * P:3 * P], QS[:, h, 2 * P:4 * P],
                                       start=True, stop=True)
                mm.then_inc(qk_done, 1)

            def pv(b, g, vals, t, q0, n, probs, first=False, last=False):
                for j in range(4):
                    h = col(g, j)
                    mm = pe.matmul(OA[32 * j:32 * j + 32, g // 2, q0:q0 + n], vals[:, t, 32 * h:32 * h + 32], probs(j),
                                   start=first, stop=last, skip_group_check=True)
                return mm

            def pv01(b, g):
                pe.wait_ge(mul_dve, 16 * b + 4 * g + 1)
                pe.wait_ge(mul_pool, 12 * b + 3 * g + 1)
                pe.wait_ge(m0_free, USES0 * b + 5)
                pe.wait_ge(v2f_rdy, b + 1)
                if g % 2 == 0 and b > 0:
                    pe.wait_ge(o_out, 2 * (b - 1) + g // 2 + 1)
                e = lambda q0, n: lambda j: EB[j // 2][:, 512 * (j % 2) + q0:512 * (j % 2) + q0 + n]
                pv(b, g, V2[b % 2], 0, 0, 256, e(0, 256), first=g % 2 == 0)
                pv(b, g, V2F[b % 2], 0, 256, 256, e(256, 256)).then_inc(pv_done, 1)

            def pv23(b, g):
                pe.wait_ge(mul_dve, 16 * b + 4 * g + 3)
                pe.wait_ge(mul_pool, 12 * b + 3 * g + 3)
                e = lambda c, n: lambda j: EB[2 + j // 2][:, 512 * (j % 2) + c:512 * (j % 2) + c + n]
                pv(b, g, V2[b % 2], 1, 128, 256, e(0, 256))
                pv(b, g, V2F[b % 2], 1, 384, 128, e(256, 128))
                pv(b, g, V2[b % 2], 3, 384, 128, e(384, 128)).then_inc(pv_done, 1)

            def pv4(b, g):
                pe.wait_ge(mul_dve, 16 * b + 4 * g + 4)
                e = lambda j: EB[4][:, 256 * j:256 * j + 256]
                pv(b, g, V2[b % 2], 2, 256, 256, e, last=g % 2 == 1).then_inc(pv_done, 1)

            def post(b, k):
                take1(b, k)
                full = m1_full
                if k in (R_O0, R_O1):
                    pe.wait_ge(o_out, 2 * b + 2)
                    for i in range(2):
                        t = 2 * (k - R_O0) + i
                        for bank in range(2):
                            mm = pe.transpose(M1[:, 256 * i + P * bank:256 * i + P * (bank + 1)],
                                              OS[:, bank, P * t:P * (t + 1)], IDN[:, :])
                    mm.then_inc(full, 1)
                elif k == R_V:
                    pe.matmul(M1[0:1, 0:P], XSUM[:, b:b + 1], WQKV[:, 2 * D:3 * D], start=True, stop=True).then_inc(full, 1)
                elif k == R_YT:
                    turn4(M1, YN, full)
                elif k == R_Y:
                    if b == 0:
                        pe.wait_ge(w2_in, 16 * N_W2)
                    for t in range(T):
                        mm = pe.matmul(M1[:, P * t:P * (t + 1)], YT[:, P * t:P * (t + 1)], WO[:, :], start=True, stop=True)
                    mm.then_inc(full, 1)
                elif k == R_ZT:
                    pe.wait_ge(z_rdy, b + 1)
                    turn4(M1, Z, full)
                elif R_H <= k < R_H + HC:
                    c = k - R_H
                    if b == 0 and c == 0:
                        pe.wait_ge(wq_rdy, 2)
                    pe.matmul(M1[:, :], W1[:, P * c:P * (c + 1)], ZT[:, :], start=True, stop=True).then_inc(full, 1)
                elif k == R_A:
                    for t in range(T):
                        for c in range(HC):
                            mm = pe.matmul(M1[:, P * t:P * (t + 1)], H1T[:, c, P * t:P * (t + 1)], W2[:, c, :],
                                           start=c == 0, stop=c == HC - 1)
                    mm.then_inc(full, 1)
                elif k == R_XT:
                    pe.wait_ge(xb_rdy, b + 1)
                    for t in range(T):
                        mm = pe.transpose(M1[:, P * t:P * (t + 1)], XB[b % 2][:, t, 0, 0:D], IDN[:, :])
                    mm.then_inc(full, 1)
                elif k == R_L:
                    for t in range(T):
                        mm = pe.matmul(M1[:, E * t:E * (t + 1)], XBT[:, P * t:P * (t + 1)], RT[:, :], start=True, stop=True)
                    mm.then_inc(full, 1)
                else:
                    pe.wait_ge(route_m, b + 1)
                    mflat = MM[:, :, :].rearrange("p t e -> p (t e)")
                    pe.matmul(M1[:, 0:T * E], TRI[:, :], mflat, start=True, stop=True)
                    pe.matmul(M1[:, T * E:2 * T * E], ONES[:, :], mflat, start=True, stop=True).then_inc(full, 1)

            pe.wait_ge(const_rdy, 1)
            pre_xt(0)
            for t in range(T):
                pre_qkv(0, t)
            for m in range(2):
                pre_turn(0, m)
            PRE = {0: lambda b: pre_xt(b), 2: lambda b: pre_qkv(b, 0), 3: lambda b: pre_qkv(b, 1), 5: lambda b: pre_qkv(b, 2),
                   6: lambda b: pre_qkv(b, 3), 13: lambda b: pre_turn(b, 0), 14: lambda b: pre_turn(b, 1)}
            POST = {5: R_O0, 6: R_O1, 7: R_V, 8: R_YT, 9: R_Y, 12: R_ZT, 13: R_H, 14: R_H + 1, 15: R_H + 2, 16: R_H + 3, 17: R_A}
            ROUTE = {1: R_XT, 2: R_L, 4: R_C}
            for b in range(NB + 2):
                for n in range(NU):
                    g, u = divmod(n, UNITS)
                    if b < NB:
                        scores(b, n)
                    before = (b, g - 1) if g else (b - 1, GROUPS - 1)
                    if 0 <= before[0] < NB and (b < NB or before[0] == NB - 1 and b == NB and g == 0):
                        if u == 1:
                            pv23(*before)
                        if u == 2:
                            pv4(*before)
                    if b < NB and u == 4:
                        pv01(b, g)
                    if b + 1 < NB and n in PRE:
                        PRE[n](b + 1)
                    if 2 <= b and n in ROUTE:
                        post(b - 2, ROUTE[n])
                    if 1 <= b <= NB and n in POST:
                        post(b - 1, POST[n])
                    if b == NB and n == 10:
                        expert_weights(pe)

            def xt(s, r, nload):
                pe.wait_ge(xg_in[r % 4], nload)
                pe.wait_ge(xt_rdy, s)
                pe.transpose(M0[:, 0:P], XG[r % 4][:, 0:D], IDN[:, :]).then_inc(xt_full, 1)

            def gu(s, r, off):
                pe.wait_ge(xt_rdy, s + 1)
                if not isinstance(s, int) or s >= 2:
                    pe.wait_ge(h_rdy, s - 1)
                for m in range(2):
                    mm = pe.matmul(SC[:, r % 2, 512 * m:512 * m + I], XGT[r % 2], WALL[:, bass.ds(off + I * m, I)],
                                   start=True, stop=True)
                mm.then_inc(gu_full, 1)

            def ht(s, r):
                pe.wait_ge(h_rdy, s + 1)
                if not isinstance(s, int) or s >= 2:
                    pe.wait_ge(ht_rdy, s - 1)
                for c, (i0, n) in enumerate(IC):
                    mm = pe.transpose(OA[0:n, r % 2, P * c:P * (c + 1)], HS[r % 2][:, i0:i0 + n], IDN[:, :])
                mm.then_inc(ht_full, 1)

            def down(s, r, off):
                pe.wait_ge(ht_rdy, s + 1)
                if not isinstance(s, int) or s >= 1:
                    pe.wait_ge(ys_rdy, s)
                for c, (i0, n) in enumerate(IC):
                    mm = pe.matmul(M1[:, 0:P], HTB[r % 2][0:n, P * c:P * (c + 1)],
                                   WALL[0:n, bass.ds(off + 2 * I + P * c, P)], start=c == 0, stop=c == len(IC) - 1)
                mm.then_inc(y_full, 1)

            def woff(s):
                at = slice(s, s + 1) if isinstance(s, int) else bass.ds(s, 1)
                return pe.value_load(SRI[0:1, 1, at], min_val=0, max_val=(E - 1) * WEXP)

            def step(s, r, it):
                if not isinstance(s, int) or s + 1 < STILES:
                    xt(s + 1, r + 1, 16 * (it + 1 + (r + 1) // 4))
                if not isinstance(s, int) or s < STILES:
                    gu(s, r, woff(s))
                if not isinstance(s, int) or 1 <= s <= STILES:
                    ht(s - 1, r + 3)
                if not isinstance(s, int) or s >= 2:
                    down(s - 2, r + 2, woff(s - 2))

            pe.wait_ge(table_rdy, 1)
            pe.wait_ge(m0_free, USES0 * NB)
            pe.wait_ge(m1_free, USES1 * NB)
            for r in range(2):
                pe.wait_ge(wt_free[r], (NWT + 1 - r) // 2)
            pe.wait_ge(xg_in[0], 16)
            pe.transpose(M0[:, 0:P], XG[0][:, 0:D], IDN[:, :]).then_inc(xt_full, 1)
            for s in range(8):
                step(s, s % 4, s // 4)
            with pe.Fori(2, STILES // 4 - 1) as it:
                for r in range(4):
                    step(4 * it + r, r, it)
            for s in range(STILES - 4, STILES + 2):
                step(s, s % 4, s // 4)

        @block.scalar
        def _(act):
            def exp_unit(b, n):
                u = n % UNITS
                act.wait_ge(qk_done, NU * b + n + 1)
                done = 3 * (GROUPS * b + n // UNITS) + (-2, -2, -1, -1, 0)[u]
                if done > 0:
                    act.wait_ge(pv_done, done)
                act.activation(EB[u], SC[:, n % 2, :], ACT.Exp).then_inc(exp_done, 1)

            def pre(b, k):
                act.wait_ge(m0_full, USES0 * b + k + 1)
                if k == 0:
                    act.activation(XART[:, :], M0[:, :], ACT.Copy, accum_out=XSUM[:, b:b + 1]).then_inc(m0_free, 1)
                elif k <= T:
                    t = k - 1
                    if k == 1 and b == 0:
                        act.wait_ge(v2_const, 2)
                    if k == 1 and b >= 2:
                        act.wait_ge(pv_done, 12 * (b - 1))
                    act.activation(QK[:, t, :], M0[:, 0:2 * D], ACT.Copy)
                    act.activation(V2[b % 2][:, t, :].rearrange("p (n s) -> p n s", s=64)[:, :, 0:8], M0[:, 2 * D:3 * D].rearrange("p (n a d) -> p n a d", a=2, d=DH)[:, :, 0, :],
                        ACT.Copy)
                    act.activation(V2[b % 2][:, t, :].rearrange("p (n s) -> p n s", s=64)[:, :, 48:56],
                                   M0[:, 2 * D:3 * D].rearrange("p (n a d) -> p n a d", a=2, d=DH)[:, :, 1, :],
                                   ACT.Copy).then_inc(m0_free, 1)
                else:
                    m = k - 5
                    if b > 0:
                        act.wait_ge(part_pool, 2 * (b - 1) + m + 1)
                    act.activation(PF[:, m, :], M0[:, :], ACT.Copy).then_inc(m0_free, 1)

            def out_bank(b, bank):
                act.wait_ge(pv_done, 12 * b + 6 * (bank + 1))
                if b > 0:
                    act.wait_ge(m1_full, USES1 * (b - 1) + R_O1 + 1)
                act.activation(OS[:, bank, :], OA[:, bank, :], ACT.Copy).then_inc(o_out, 1)

            def post(b, k):
                act.wait_ge(m1_full, USES1 * b + k + 1)
                if k == R_YT:
                    act.activation(YT[:, :], M1[:, :], ACT.Copy).then_inc(m1_free, 1)
                elif k == R_ZT:
                    act.activation(ZT[:, :], M1[:, :], ACT.Copy).then_inc(m1_free, 1)
                elif k in (R_H, R_H + 2):
                    act.activation(H1T[:, k - R_H, :], M1[:, :], ACT.Relu).then_inc(m1_free, 1)
                elif k == R_XT:
                    act.activation(XBT[:, :], M1[:, :], ACT.Copy).then_inc(m1_free, 1)

            for k in range(5):
                pre(0, k)
            act.wait_ge(bias_in, 48)
            act.activation(CF[:, :], CF[:, :], ACT.Exp).then_inc(tab_exp, 1)
            act.wait_ge(tab_raw, 1)
            act.activation(TAB, TAB, ACT.Exp).then_inc(tab_exp, 1)
            for k in range(5, USES0):
                pre(0, k)
            PRE = {1: 0, 3: 1, 4: 2, 6: 3, 7: 4, 14: 5, 15: 6}
            POST = {9: R_YT, 13: R_ZT, 14: R_H, 16: R_H + 2}
            for b in range(NB + 2):
                for n in range(NU):
                    if b < NB:
                        exp_unit(b, n)
                    if b + 1 < NB and n in PRE:
                        pre(b + 1, PRE[n])
                    if n == 13 and b < NB:
                        out_bank(b, 0)
                    if n == 3 and 1 <= b <= NB:
                        out_bank(b - 1, 1)
                    if b >= 2 and n == 2:
                        post(b - 2, R_XT)
                    if b >= 2 and n == 5:
                        act.wait_ge(route_d, b - 1)
                        act.activation(EX[:, :, :], EX[:, :, :], ACT.Exp).then_inc(route_e, 1)
                    if 1 <= b <= NB and n in POST:
                        post(b - 1, POST[n])
                    if b == NB and n == 10:
                        for i, lot in enumerate(lots):
                            if i % 2:
                                continue
                            act.wait_ge(wt_full, i + 1)
                            copy_lot(act.copy, i, lot, act)

            def evac_x(s, r):
                act.wait_ge(xt_full, s + 1)
                if not isinstance(s, int) or s >= 2:
                    act.wait_ge(gu_full, s - 1)
                act.activation(XGT[r % 2], M0[:, 0:P], ACT.Copy).then_inc(xt_rdy, 1)

            def silu(s, r):
                act.wait_ge(gu_full, s + 1)
                if not isinstance(s, int) or s >= 2:
                    act.wait_ge(h_rdy, s - 1)
                act.activation(SGB[r % 2], SC[:, r % 2, 0:I], ACT.Silu).then_inc(sg_rdy, 1)

            def evac_y(s, r, it):
                act.wait_ge(y_full, s + 1)
                if not isinstance(s, int) or s >= 4:
                    act.wait_ge(ys_out[r % 4], 16 * it)
                act.wait_ge(meta_rdy, s + 1)
                act.activation(YS[r % 4], M1[:, 0:P], ACT.Copy, scale=MT[r % 4][:, 0:1]).then_inc(ys_rdy, 1)

            def step(s, r, it):
                if not isinstance(s, int) or s + 1 < STILES:
                    evac_x(s + 1, r + 1)
                if not isinstance(s, int) or s < STILES:
                    silu(s, r)
                if not isinstance(s, int) or s >= 2:
                    evac_y(s - 2, r + 2, it - (r < 2))

            evac_x(0, 0)
            for s in range(8):
                step(s, s % 4, s // 4)
            with act.Fori(2, STILES // 4 - 1) as it:
                for r in range(4):
                    step(4 * it + r, r, it)
            for s in range(STILES - 4, STILES + 2):
                step(s, s % 4, s // 4)

        @block.vector
        def _(dve):
            steps = [0]

            def link(ins):
                steps[0] += 1
                ins.then_inc(dve_step, 1)
                dve.wait_ge(dve_step, steps[0])

            def rsqrt(y, a, u):
                link(dve.tensor_scalar(y.bitcast(I32), a.bitcast(I32), 1, None, ALU.logical_shift_right))
                link(dve.tensor_scalar(y.bitcast(I32), y.bitcast(I32), -1.0, RSQRT_SEED, ALU.mult, ALU.add))
                for _ in range(3):
                    link(dve.tensor_tensor(u, y, y, ALU.mult))
                    link(dve.scalar_tensor_tensor(u, u, -0.5, a, ALU.mult, ALU.mult))
                    link(dve.scalar_tensor_tensor(y, u, 1.5, y, ALU.add, ALU.mult))

            def bc(ap, shape):
                return ap.unsqueeze(len(shape) - 1).broadcast_to(shape)

            dve.wait_ge(w_in, 16 * N_W)
            link(dve.tensor_scalar(RB[:, :], RB[:, :], SCP[:, 0:1], None, ALU.mult))
            dve.memset(BR[:, 0:P + 1], NEG)
            exact = BUCKETS // 2
            dve.tensor_copy(BR[:, P + 1:P + exact], RB[:, 1:exact])
            ends = starts[1:] + [2 * P]
            for r in range(exact, BUCKETS):
                a, z = starts[r - exact], ends[r - exact]
                last = dve.tensor_copy(BR[:, P + a:P + z], RB[:, r:r + 1].broadcast_to([H, z - a]))
            link(last)
            link(dve.tensor_reduce(GM[:, :], BR[:, P + 1:3 * P], AX, ALU.max))
            link(dve.tensor_scalar(BR[:, P + 1:3 * P], BR[:, P + 1:3 * P], GM[:, 0:1], None, ALU.subtract))
            dve.memset(CMR[:, 0:1], 0.0)
            dve.tensor_tensor_scan(CMR[:, 1:P], BR[:, P + 1:2 * P], BR[:, P + 1:2 * P], NEG, ALU.max, ALU.max
                                   ).then_inc(bias_rows, 1)
            for m in range(2):
                dve.tensor_scalar(WQKV[:, D * m:D * (m + 1)].rearrange("p (d h) -> p h d", h=H),
                                  WRAW[:, D * m:D * (m + 1)].rearrange("p (h d) -> p h d", h=H), LNW[:, 0:1], None, ALU.mult)
            dve.tensor_scalar(WQKV[:, 2 * D:3 * D], WRAW[:, 2 * D:3 * D], LNW[:, 0:1], None, ALU.mult).then_inc(wq_rdy, 1)
            for i in range(NT):
                if i % HX == 0:
                    dve.wait_ge(x_in[i // HX], 16)
                last = dve.bn_stats(ST[:, i, :], X[:, i, :])
            link(last)
            for i in range(NT):
                last = dve.bn_aggr(MV[:, i, :], ST[:, i, :])
            link(last)
            a, u, w = NWA[:, 0:NT], NWB[:, 0:NT], NWC[:, 0:NT]
            link(dve.tensor_scalar(a, MV[:, :, 1], LN_EPS, None, ALU.add))
            rsqrt(RS0[:, :], a, u)
            link(dve.tensor_tensor(w, RS0[:, :], RS0[:, :], ALU.mult))
            link(dve.tensor_tensor(w, w, MV[:, :, 1], ALU.mult))
            link(dve.tensor_scalar(a, w, RMS_EPS, None, ALU.add))
            rsqrt(w, a, u)
            dve.tensor_tensor(RR0[:, :], w, RS0[:, :], ALU.mult).then_inc(ln0, 1)
            dve.wait_ge(ln0, 1)

            def xar(b):
                if b > 0:
                    dve.wait_ge(m0_full, USES0 * (b - 1) + 1)
                for t in range(T):
                    i = T * b + t
                    last = dve.tensor_scalar(XAR[:, t, :], X[:, i, :], MV[:, i, 0:1], RR0[:, i:i + 1], ALU.subtract, ALU.mult)
                last.then_inc(xar_rdy, 1)

            xar(0)
            dve.memset(arena[64:P, 0:4096], 0.0).then_inc(ks_zero, 1)
            dve.memset(arena[64:P, 4096:8192], 0.0).then_inc(ks_zero, 1)
            dve.wait_ge(bias_in, 48)
            dve.tensor_tensor(TAB[:, :, 0:P], TAB[:, :, P:2 * P], CMB, ALU.subtract).then_inc(tab_raw, 1)
            dve.wait_ge(w2_in, 16 * N_W2)
            dve.tensor_scalar(W1[:, :], W1R, LNW[:, 1:2], None, ALU.mult).then_inc(wq_rdy, 1)
            def norms(b):
                dve.wait_ge(sq_rdy, b + 1)
                link(dve.tensor_reduce(SS[:, :].rearrange("p (g h) -> p g h", h=H),
                                       SQ[:, :, :].rearrange("p t c -> p (t c)").rearrange("p (g d h) -> p g h d", d=DH, h=H), AX, ALU.add))
                link(dve.tensor_scalar(SS[:, :], SS[:, :], KQ_EPS, None, ALU.add))
                rsqrt(RSQ[:, :], SS[:, :], NWA[:, :])
                rs = RSQ[:, :].rearrange("p (t m h) -> p t m h", t=T, m=2)
                link(dve.tensor_tensor(rs[:, :, 0, :], rs[:, :, 0, :], SCB[:, :].unsqueeze(1).broadcast_to([P, T, H]), ALU.mult))
                for t in range(T):
                    v = QK[:, t, :].rearrange("p (m d h) -> p m d h", m=2, h=H)
                    last = dve.tensor_tensor(v, v, rs[:, t].unsqueeze(2).broadcast_to([P, 2, DH, H]), ALU.mult)
                last.then_inc(qk_norm, 1)

            def split(b, m, first):
                if first:
                    dve.wait_ge(m0_free, USES0 * b + 6 + m)
                    if b > 0:
                        dve.wait_ge(parts_out, 32 * b)
                    dve.tensor_copy(PP[:, m, 0, :], PF[:, m, :]).then_inc(part_dve, 1)
                else:
                    dve.wait_ge(pool_rem, 2 * b + m + 1)
                    dve.tensor_copy(PP[:, m, 1, :], PF[:, m, :]).then_inc(part_dve, 1)

            def mul(b, n):
                g, u = divmod(n, UNITS)
                heads = slice(col(g, 0), col(g, 3) + 1, 2)
                if u == 0:
                    mul_first(dve, g, 0).then_inc(mul_dve, 1)
                elif u == 2:
                    for i in mul_mid(dve, g, 0):
                        i.then_inc(mul_dve, 1)
                elif u == 4:
                    e = EB[4].rearrange("p (j c) -> p j c", j=4)
                    dve.tensor_tensor(e, e, TAB[:, heads, P:3 * P], ALU.mult).then_inc(mul_dve, 1)

            def post(b, k):
                dve.wait_ge(m1_full, USES1 * b + k + 1)
                if k in (R_O0, R_O1):
                    t0 = 2 * (k - R_O0)
                    v = M1[:, :].rearrange("p (t n c) -> p t n c", t=2, c=16)
                    link(dve.reciprocal(RD[:, t0:t0 + 2, :], v[:, :, :, DH]))
                    for i in range(2):
                        last = dve.tensor_tensor(YN[:, t0 + i, :].rearrange("p (n d) -> p n d", d=DH), v[:, i, :, 0:DH],
                                                 RD[:, t0 + i, :].unsqueeze(2).broadcast_to([P, H, DH]), ALU.mult)
                    last.then_inc(m1_free, 1)
                elif k == R_V:
                    dve.wait_ge(m1_free, USES1 * b + R_V)
                    dve.tensor_scalar(YN[0:1, 0, :], M1[0:1, 0:P], 1.0 / S, None, ALU.mult).then_inc(m1_free, 1)
                elif k == R_Y:
                    dve.wait_ge(xa_rdy, NT)
                    dve.tensor_tensor(Y[:, :, :].rearrange("p t d -> p (t d)"), M1[:, :],
                                      XA[:, T * b:T * (b + 1), :].rearrange("p t d -> p (t d)"), ALU.add).then_inc(m1_free, 1)
                elif k in (R_H + 1, R_H + 3):
                    dve.tensor_scalar(H1T[:, k - R_H, :], M1[:, :], 0.0, None, ALU.max).then_inc(m1_free, 1)
                elif k == R_A:
                    dve.tensor_tensor(A[:, :, :].rearrange("p t d -> p (t d)"), M1[:, :],
                                      Y[:, :, :].rearrange("p t d -> p (t d)"), ALU.add).then_inc(m1_free, 1)
                    dve.wait_ge(m1_free, USES1 * b + R_A + 1)

            def stats(src, r, done):
                for t in range(T):
                    last = dve.bn_stats(STP[:, r, t, :], src[:, t, :])
                link(last)
                for t in range(T):
                    last = dve.bn_aggr(MVP[:, r, t, :], STP[:, r, t, :])
                last.then_inc(done, 1)

            def top2(b):
                dve.wait_ge(m1_full, USES1 * b + R_L + 1)
                dve.tensor_copy(LG[:, :, :].rearrange("p t e -> p (t e)"), M1[:, 0:T * E]).then_inc(m1_free, 1)
                dve.wait_ge(m1_free, USES1 * b + R_L + 1)
                lg = LG
                for k in range(2):
                    link(dve.tensor_reduce(MX[:, k, :], lg[:, :, :], AX, ALU.max))
                    link(dve.tensor_tensor(EQ[:, :, :], lg[:, :, :], bc(MX[:, k, :], [P, T, E]), ALU.is_equal))
                    link(dve.tensor_tensor(EQ[:, :, :], EQ[:, :, :], REV[:, :, :], ALU.mult))
                    link(dve.tensor_reduce(MX[:, 2, :], EQ[:, :, :], AX, ALU.max))
                    link(dve.tensor_tensor(OH[:, k], EQ[:, :, :], bc(MX[:, 2, :], [P, T, E]), ALU.is_equal))
                    if k == 0:
                        link(dve.scalar_tensor_tensor(LG2[:, :, :], OH[:, 0], NEG, LG[:, :, :], ALU.mult, ALU.add))
                        lg = LG2
                dve.tensor_tensor(MM[:, :, :], OH[:, 0], OH[:, 1], ALU.add).then_inc(route_m, 1)
                dve.tensor_tensor(EX[:, :, 0:E], LG[:, :, :], bc(MX[:, 0, :], [P, T, E]), ALU.subtract)
                dve.tensor_tensor(EX[:, :, E], MX[:, 1, :], MX[:, 0, :], ALU.subtract).then_inc(route_d, 1)

            def place(b):
                r = b % 2
                dve.wait_ge(route_e, b + 1)
                link(dve.tensor_reduce(MX[:, 2, :], EX[:, :, 0:E], AX, ALU.add))
                link(dve.reciprocal(MX[:, 3, :], MX[:, 2, :]))
                dve.tensor_copy(XB[r][:, :, 0, D], MX[:, 3, :])
                dve.tensor_tensor(XB[r][:, :, 1, D], MX[:, 3, :], EX[:, :, E], ALU.mult).then_inc(route_w, 1)
                dve.wait_ge(m1_full, USES1 * b + R_C + 1)
                for t in range(T):
                    link(dve.tensor_tensor(TB[:, t + 1, :], TB[:, t, :], M1[:, E * (T + t):E * (T + t + 1)], ALU.add))
                link(dve.tensor_tensor(POS[:, :, :], M1[:, 0:T * E].rearrange("p (t e) -> p t e", t=T), TB[:, 0:T, :], ALU.add))
                for k in range(2):
                    last = dve.tensor_tensor(PSEL[:, k], OH[:, k], POS[:, :, :], ALU.mult)
                last.then_inc(m1_free, 1)
                dve.wait_ge(m1_free, USES1 * b + R_C + 1)
                dve.tensor_copy(TB[:, 0, :], TB[:, T, :])
                link(dve.tensor_reduce(POSF[:, :, :], PSEL[:, :, :, :], AX, ALU.add))
                if b >= 2:
                    dve.wait_ge(scattered[r], 16 * 2 * T * (b // 2))
                dve.tensor_copy(IDX[r][:, :, :], POSF[:, :, :]).then_inc(idx_rdy, 1)
                dve.wait_ge(idx_rdy, b + 1)

            dve.wait_ge(const_rdy, 1)
            dve.tensor_copy(TB[:, 0, :], EROW[:, :])
            norms(0)
            for m in range(2):
                split(0, m, True)
            for m in range(2):
                split(0, m, False)
            dve.wait_ge(tab_exp, 2)
            dve.memset(TAB[0:1, :, 0:1], 1.0).then_inc(tab_rdy, 1)
            dve.wait_ge(tab_rdy, 1)
            xar(1)
            for b in range(NB + 2):
                for n in range(NU):
                    if b < NB and n % UNITS in (0, 2, 4):
                        dve.wait_ge(exp_done, NU * b + n + 1)
                        mul(b, n)
                    if b + 1 < NB:
                        if n == 10:
                            norms(b + 1)
                        if n == 15:
                            split(b + 1, 0, True)
                            split(b + 1, 1, True)
                        if n == 17:
                            split(b + 1, 0, False)
                            split(b + 1, 1, False)
                    if b + 2 < NB and n == 18:
                        xar(b + 2)
                    if b >= 2:
                        if n == 3:
                            top2(b - 2)
                        if n == 5:
                            place(b - 2)
                    if 1 <= b <= NB:
                        c = b - 1
                        if n in (6, 7, 8):
                            post(c, n - 6)
                        if n == 9:
                            post(c, R_Y)
                            dve.wait_ge(ysq, c + 1)
                            dve.tensor_reduce(SSY[:, :], YQ[:, :, :], AX, ALU.add).then_inc(ssy_rdy, 1)
                        if n == 14:
                            post(c, R_H + 1)
                        if n == 16:
                            post(c, R_H + 3)
                        if n == 17:
                            post(c, R_A)
                            stats(A, 0, a_stat)
                        if n == 18:
                            dve.wait_ge(a_rstd, c + 1)
                            for t in range(T):
                                last = dve.tensor_scalar(A[:, t, :], A[:, t, :], MVP[:, 0, t, 0:1], RZ[:, 1, t:t + 1],
                                                         ALU.subtract, ALU.mult)
                            last.then_inc(a_ln, 1)
                            dve.wait_ge(x1_rdy, c + 1)
                            stats(X[:, T * c:T * (c + 1), :], 1, x1_stat)
                        if n == 19:
                            dve.wait_ge(x1_rstd, c + 1)
                            if c >= 2:
                                dve.wait_ge(scattered[c % 2], 16 * 2 * T * (c // 2))
                            for t in range(T):
                                for k in range(2):
                                    last = dve.tensor_scalar(XB[c % 2][:, t, k, 0:D], X[:, T * c + t, :], MVP[:, 1, t, 0:1],
                                                             RZ[:, 2, t:t + 1], ALU.subtract, ALU.mult)
                            last.then_inc(xb_rdy, 1)
                    if b == NB and n == 10:
                        for i, lot in enumerate(lots):
                            if i % 2:
                                dve.wait_ge(wt_full, i + 1)
                                copy_lot(dve.tensor_copy, i, lot, dve)

            dve.tensor_scalar(PADI[:, :], TB[:, T, :], PCOL[:, 0:1], None, ALU.add).then_inc(pad_rdy, 1)
            link(dve.tensor_tensor(NTF[:, 0, :], TB[:, T, :], EROW[:, :], ALU.subtract))
            link(dve.tensor_scalar(NTE[:, :], NTF[:, 0, :], float(P - 1), None, ALU.add))
            link(dve.tensor_scalar(NTE[:, :], NTE[:, :], 7, None, ALU.logical_shift_right))
            link(dve.tensor_copy(NTF[:, 0, :], NTE[:, :]))
            link(dve.tensor_copy(NTF[:, 1, 0:1], NTF[:, 0, 0:1]))
            for e in range(1, E):
                link(dve.tensor_tensor(NTF[:, 1, e:e + 1], NTF[:, 1, e - 1:e], NTF[:, 0, e:e + 1], ALU.add))
            link(dve.tensor_scalar(NTF[:, 2, :], NTF[:, 0, :], -float(P), float(REGION), ALU.mult, ALU.add))
            sh = [P, STILES, E]
            link(dve.tensor_tensor(SCM[:, 0], SIO[:, :].unsqueeze(2).broadcast_to(sh),
                                   NTF[:, 1, :].unsqueeze(1).broadcast_to(sh), ALU.is_ge))
            link(dve.tensor_tensor(SCM[:, 1], SCM[:, 0], NTF[:, 2, :].unsqueeze(1).broadcast_to(sh), ALU.mult))
            dve.tensor_reduce(SRF[:, 0, :], SCM[:, 1], AX, ALU.add)
            link(dve.tensor_reduce(SRF[:, 1, :], SCM[:, 0], AX, ALU.add))
            link(dve.scalar_tensor_tensor(SRF[:, 0, :], SIO[:, :], float(P), SRF[:, 0, :], ALU.mult, ALU.add))
            dve.tensor_scalar(SRI[:, 0, :], SRF[:, 0, :], float(DUMMY), None, ALU.min)
            dve.tensor_scalar(SRI[:, 1, :], SRF[:, 1, :], float(E - 1), float(WEXP), ALU.min, ALU.mult).then_inc(table_rdy, 1)

            def meta(s, r, it):
                dve.wait_ge(xg_in[r % 4], 16 * (it + 1))
                if not isinstance(s, int) or s >= 4:
                    dve.wait_ge(ys_out[r % 4], 16 * it)
                dve.tensor_copy(MT[r % 4][:, :], XG[r % 4][:, D:D + 2]).then_inc(meta_rdy, 1)

            def hidden(s, r):
                dve.wait_ge(sg_rdy, s + 1)
                if not isinstance(s, int) or s >= 2:
                    dve.wait_ge(ht_full, s - 1)
                dve.tensor_tensor(HS[r % 2], SGB[r % 2], SC[:, r % 2, 512:512 + I], ALU.mult).then_inc(h_rdy, 1)

            def evac_h(s, r):
                dve.wait_ge(ht_full, s + 1)
                if not isinstance(s, int) or s >= 2:
                    dve.wait_ge(y_full, s - 1)
                k = IC[-1][1]
                full = P * (len(IC) - 1)
                dve.tensor_copy(HTB[r % 2][:, 0:full], OA[:, r % 2, 0:full])
                dve.tensor_copy(HTB[r % 2][0:k, full:full + P], OA[0:k, r % 2, full:full + P]).then_inc(ht_rdy, 1)

            def step(s, r, it):
                if not isinstance(s, int) or s + 1 < STILES:
                    meta(s + 1, r + 1, it + (r + 1) // 4)
                if not isinstance(s, int) or s < STILES:
                    hidden(s, r)
                if not isinstance(s, int) or 1 <= s <= STILES:
                    evac_h(s - 1, r + 3)

            meta(0, 0, 0)
            for s in range(8):
                step(s, s % 4, s // 4)
            with dve.Fori(2, STILES // 4 - 1) as it:
                for r in range(4):
                    step(4 * it + r, r, it)
            for s in range(STILES - 4, STILES + 2):
                step(s, s % 4, s // 4)

            for b in range(NB):
                r = b % 2
                dve.wait_ge(yt_in[r], 32 * (b // 2 + 1))
                if b > 0:
                    dve.wait_ge(f_out, b)
                link(dve.tensor_tensor(A[:, :, :], FY[r][:, 0], FY[r][:, 1], ALU.add))
                stats(A, 0, f_stat)
                dve.wait_ge(f_rstd, b + 1)
                for t in range(T):
                    last = dve.tensor_scalar(A[:, t, :], A[:, t, :], MVP[:, 0, t, 0:1], RZ[:, 3, t:t + 1],
                                             ALU.subtract, ALU.mult)
                last.then_inc(f_ln, 1)

        @block.gpsimd
        def _(pool):
            steps = [0]

            def link(ins):
                steps[0] += 1
                ins.then_inc(pool_step, 1)
                pool.wait_ge(pool_step, steps[0])

            pool.memset(IDN[:, :], 0.0)
            pool.memset(TRI[:, :], 1.0)
            pool.memset(ONES[:, :], 1.0)
            pool.memset(MH[:, :], -0.5)
            pool.memset(PADX[:, :], 0.0)
            pool.iota(EROW[:, :], pattern=[[REGION, E]], base=0, channel_multiplier=0, allow_small_or_imprecise_dtypes=True)
            pool.iota(PCOL[:, :], pattern=[[0, 1]], base=0, channel_multiplier=1, allow_small_or_imprecise_dtypes=True)
            pool.iota(REV[:, :, :], pattern=[[0, T], [-1, E]], base=E, channel_multiplier=0, allow_small_or_imprecise_dtypes=True)
            link(pool.iota(SIO[:, :], pattern=[[1, STILES]], base=0, channel_multiplier=0, allow_small_or_imprecise_dtypes=True))
            pool.affine_select(out=IDN[:, :], in_=IDN[:, :], compare_op=ALU.not_equal, fill=1.0, base=0,
                               pattern=[[-1, P]], channel_multiplier=1)
            pool.affine_select(out=TRI[:, :], in_=TRI[:, :], compare_op=ALU.is_gt, fill=0.0, base=0,
                               pattern=[[1, P]], channel_multiplier=-1)
            pool.iota(PADX[:, D + 1:D + 2].bitcast(I32), pattern=[[0, 1]], base=NO_ROW, channel_multiplier=0).then_inc(const_rdy, 1)
            for r in range(2):
                link(pool.memset(V2[r][:, :, :], 0.0))
                v = V2[r].rearrange("p t (n s) -> p t n s", s=64)
                pool.memset(v[:, :, :, 8:16], 1.0)
                pool.memset(v[:, :, :, 56:64], 1.0).then_inc(v2_const, 1)
            pool.wait_ge(ln0, 1)

            def xa(b):
                for t in range(T):
                    i = T * b + t
                    pool.tensor_scalar(XA[:, i, :], X[:, i, :], MV[:, i, 0:1], RS0[:, i:i + 1], ALU.subtract, ALU.mult
                                       ).then_inc(xa_rdy, 1)

            def squares(b):
                pool.wait_ge(m0_free, USES0 * b + 5)
                if b == 0:
                    pool.wait_ge(bias_dram, 48)
                if b > 0:
                    pool.wait_ge(qk_norm, b)
                pool.tensor_tensor(SQ[:, :, :], QK[:, :, :], QK[:, :, :], ALU.mult).then_inc(sq_rdy, 1)

            def far_values(b):
                pool.wait_ge(m0_free, USES0 * b + 5)
                if b == 0:
                    pool.wait_ge(tab_exp, 2)
                if b >= 2:
                    pool.wait_ge(pv_done, 12 * (b - 1))
                for t in range(2):
                    last = pool.tensor_tensor(V2F[b % 2][:, t, :].rearrange("p (h s) -> p h s", h=H),
                                              V2[b % 2][:, t, :].rearrange("p (h s) -> p h s", h=H),
                                              CF[:, :].unsqueeze(2).broadcast_to([P, H, 32]), ALU.mult)
                last.then_inc(v2f_rdy, 1)

            def remainder(b, m):
                pool.wait_ge(part_dve, 4 * b + m + 1)
                pool.tensor_tensor(PF[:, m, :], PF[:, m, :], PP[:, m, 0, :], ALU.subtract).then_inc(pool_rem, 1)

            def third(b, m):
                pool.wait_ge(part_dve, 4 * b + 2 + m + 1)
                pool.tensor_tensor(PP[:, m, 2, :], PF[:, m, :], PP[:, m, 1, :], ALU.subtract).then_inc(part_pool, 1)

            def inv_root(k, src, scale, eps, done):
                link(pool.tensor_scalar(RZ[:, k, :], src, scale, eps, ALU.mult, ALU.add))
                pool.tensor_tensor(RZ[:, k, :], RZ[:, k, :], MH[:, :], ALU.pow).then_inc(done, 1)

            def scatter(b, t):
                r = b % 2
                for k in range(2):
                    pool.indirect_dma_start(out=slots_d.ap(), out_offset=bass.IndirectOffsetOnAxis(ap=IDX[r][:, k, t:t + 1], axis=0),
                                            in_=XB[r][:, t, k, :], in_offset=None).then_inc(scattered[r], 16)

            squares(0)
            far_values(0)
            for m in range(2):
                remainder(0, m)
            for m in range(2):
                third(0, m)
            for b in range(NB):
                xa(b)
            pool.wait_ge(tab_rdy, 1)
            for b in range(NB + 2):
                for n in range(NU):
                    g, u = divmod(n, UNITS)
                    if b < NB and u in (1, 3):
                        pool.wait_ge(exp_done, NU * b + n + 1)
                        if u == 1:
                            mul_first(pool, g, 1).then_inc(mul_pool, 1)
                        else:
                            for i in mul_mid(pool, g, 1):
                                i.then_inc(mul_pool, 1)
                    if b + 1 < NB:
                        if n == 8:
                            squares(b + 1)
                        if n == 9:
                            far_values(b + 1)
                        if n == 15:
                            remainder(b + 1, 0)
                            remainder(b + 1, 1)
                        if n == 17:
                            third(b + 1, 0)
                            third(b + 1, 1)
                    if b >= 2:
                        c = b - 2
                        if n == 5:
                            pool.wait_ge(xb_rdy, c + 1)
                            pool.iota(XB[c % 2][:, :, :, D + 1].bitcast(I32), pattern=[[P, T], [NTOK, 2]], base=S * c,
                                      channel_multiplier=1).then_inc(dest_rdy, 1)
                            pool.wait_ge(dest_rdy, c + 1)
                            pool.wait_ge(idx_rdy, c + 1)
                            pool.wait_ge(route_w, c + 1)
                        if n in (5, 6, 7, 8):
                            scatter(c, n - 5)
                    if 1 <= b <= NB:
                        c = b - 1
                        if n == 9:
                            pool.wait_ge(m1_free, USES1 * c + R_Y + 1)
                            pool.tensor_tensor(YQ[:, :, :], Y[:, :, :], Y[:, :, :], ALU.mult).then_inc(ysq, 1)
                        if n == 10:
                            pool.wait_ge(ssy_rdy, c + 1)
                            inv_root(0, SSY[:, :], 1.0 / D, RMS_EPS, z_root)
                            pool.wait_ge(z_root, c + 1)
                            pool.tensor_tensor(Z[:, :, :], Y[:, :, :], RZ[:, 0, :].unsqueeze(2).broadcast_to([P, T, D]),
                                               ALU.mult).then_inc(z_rdy, 1)
                        if n == 17:
                            pool.wait_ge(a_stat, c + 1)
                            inv_root(1, MVP[:, 0, :, 1], 1.0, LN_EPS, a_rstd)
                        if n == 18:
                            pool.wait_ge(a_ln, c + 1)
                            pool.tensor_tensor(X[:, T * c:T * (c + 1), :], X[:, T * c:T * (c + 1), :], A[:, :, :], ALU.add
                                               ).then_inc(x1_rdy, 1)
                            pool.wait_ge(x1_stat, c + 1)
                            inv_root(2, MVP[:, 1, :, 1], 1.0, LN_EPS, x1_rstd)
            pool.wait_ge(pad_rdy, 1)
            for e in range(E):
                pool.indirect_dma_start(out=slots_d.ap(), out_offset=bass.IndirectOffsetOnAxis(ap=PADI[:, e:e + 1], axis=0),
                                        in_=PADX[:, :], in_offset=None).then_inc(pad_out, 16)

            def put(s, r):
                pool.wait_ge(ys_rdy, s + 1)
                pool.indirect_dma_start(out=ytok_d.ap(),
                                        out_offset=bass.IndirectOffsetOnAxis(ap=MT[r % 4][:, 1:2].bitcast(I32), axis=0),
                                        in_=YS[r % 4], in_offset=None, bounds_check=2 * NTOK - 1, oob_is_err=False
                                        ).then_inc(ys_out[r % 4], 16)

            for s in range(STILES):
                put(s, s % 4)

            for b in range(NB):
                pool.wait_ge(f_stat, b + 1)
                inv_root(3, MVP[:, 0, :, 1], 1.0, LN_EPS, f_rstd)
                pool.wait_ge(f_ln, b + 1)
                pool.tensor_tensor(X[:, T * b:T * (b + 1), :], X[:, T * b:T * (b + 1), :], A[:, :, :], ALU.add).then_inc(f_out, 1)


_INS = ['L0_attn_x', 'L0_attn_ln1_w', 'L0_attn_Wq', 'L0_attn_Wk', 'L0_attn_Wv', 'L0_attn_rel_bias', 'L0_attn_scale',
        'L0_attn_Wo', 'L0_attn_ln2_w', 'L0_attn_W1', 'L0_attn_W2', 'L0_ffn_router_w', 'L0_ffn_gate_w', 'L0_ffn_up_w',
        'L0_ffn_down_w']


def kernel(**inputs):
    import concourse.bacc as bacc
    from concourse.bass_utils import run_bass_kernel_spmd

    nc = bacc.Bacc("TRN2", target_bir_lowering=False, num_devices=1)
    arrays, args = {}, []
    for name in _INS:
        a = np.ascontiguousarray(inputs[name])
        arrays[f"in_{name}"] = a
        args.append(nc.dram_tensor(f"in_{name}", a.shape, mybir.dt.from_np(a.dtype), kind="ExternalInput").ap())
    x = inputs['L0_attn_x']
    out = nc.dram_tensor("out", x.shape, mybir.dt.from_np(np.dtype(x.dtype)), kind="ExternalOutput")
    block_kernel(nc, *args, out.ap())
    r = run_bass_kernel_spmd(nc, [arrays], core_ids=[0])
    return r.results[0]["out"]
```

```python
from contextlib import ExitStack

import numpy as np
import concourse.bass as bass
from concourse import mybir

ALU = mybir.AluOpType
ACT = mybir.ActivationFunctionType
AX = mybir.AxisListType.X
F32 = mybir.dt.float32
BF16 = mybir.dt.bfloat16
I32 = mybir.dt.int32

P = 128
NEG = -1.0e30
RING = 8
UNITS = 5
GROUPS = 4
NU = UNITS * GROUPS
LN_EPS = 1e-5
RMS_EPS = 1e-6
KQ_EPS = 1e-6
NO_ROW = 1 << 20
RSQRT_SEED = float(0x5F3759DF)


PE_AT = (dict(xt=0, qkv0=1, qkv1=2, qkv2=3, qkv3=4, turn0=12, turn1=12, rx=1, logits=2, vsum=3, o0=4, o1=5, yt=6, wo=6, zt=8, h0=9, h1=10, h2=11, h3=12, ffn=13, count=15),
    dict(rx=1, logits=2, vsum=3, o0=4, o1=5, yt=6, wo=6, zt=8, h0=9, h1=10, h2=11, h3=12, ffn=13, count=15))
ACT_AT = (dict(xt=0, qkv0=1, qkv1=2, qkv2=3, qkv3=4, part0=11, part1=12, half0=13, half1=13, out0=13, out1=3, rx=1, rexp=6, yt=6, ysq=9, zt=8, h0=9, h1=10, h2=11, h3=12),
    dict(out1=3, rx=1, rexp=6, yt=6, ysq=9, zt=8, h0=9, h1=10, h2=11, h3=12))
DVE_AT = (dict(xa=5, norm0=7, norm1=9, norm2=10, rem0=11, rem1=12, xar=6, top2=2, vsum=3, o0=4, o1=5, wo=6, ffn=14, place=16, ln=16, xb=18),
    dict(xa=5, top2=2, vsum=3, o0=4, o1=5, wo=6, ffn=14, place=16, ln=16, xb=18))
POOL_AT = (dict(far=5, third0=15, third1=15, yroot=10, aroot=15, xroot=17, sc0=18, sc1=19, sc2=19, sc3=19),
    dict(yroot=10, aroot=15, xroot=17, sc0=18, sc1=19, sc2=19, sc3=19))
WEIGHTS_AT = 6
M1_USES = ("rx", "logits", "vsum", "o0", "o1", "yt", "wo", "zt", "h0", "h1", "h2", "h3", "ffn", "count")
ROUTE_USES = ("rx", "logits", "count")


def bucket_starts(buckets, max_distance):
    exact = buckets // 2
    d = np.arange(1, 4 * max_distance)
    big = exact + (np.log((d / exact).astype(np.float32)) / np.float32(np.log(max_distance / exact))
                   * (buckets - exact)).astype(np.int32)
    of = np.where(d < exact, d, np.minimum(big, buckets - 1))
    return [int(d[np.argmax(of >= r)]) for r in range(exact, buckets)]


def block_kernel(nc, x_d, ln1_d, wq_d, wk_d, wv_d, rel_d, scale_d, wo_d, ln2_d, w1_d, w2_d,
                 router_d, gate_d, up_d, down_d, out_d):
    NB, S, D = x_d.shape
    BUCKETS, H = rel_d.shape
    DH = D // H
    HID = w1_d.shape[1]
    E, I, _ = gate_d.shape
    T = S // P
    NT = NB * T
    NTOK = NB * S
    HC = HID // P
    IC = [(c * P, min(P, I - c * P)) for c in range((I + P - 1) // P)]
    REGION = NTOK + P
    DUMMY = E * REGION
    STILES = (2 * NTOK) // P + E
    ROW = D + 2
    WEXP = 2 * I + len(IC) * P
    starts = bucket_starts(BUCKETS, 128)
    assert (S, D, DH, T, H) == (512, P, 8, 4, 16) and STILES % RING == 0

    slots_d = nc.dram_tensor("slots", [(E * REGION + P), ROW], F32)
    ytok_d = nc.dram_tensor("ytok", [2 * NTOK, D], F32)
    parts_d = nc.dram_tensor("parts", [2, 2, 3, P, S], BF16)
    toe_d = nc.dram_tensor("toe", [H, P, 3 * P], F32)
    cm_d = nc.dram_tensor("cm", [H, P], F32)
    cfar_d = nc.dram_tensor("cfar", [H, 1], F32)

    with ExitStack() as ctx:
        def sb(name, shape, dt=F32):
            return ctx.enter_context(nc.sbuf_tensor(name, shape, dt))

        def sem(name):
            return ctx.enter_context(nc.semaphore(name))

        X = sb("X", [P, NT, D])
        XA = sb("XA", [P, T, D])
        arena = sb("arena", [P, 8192 + 6144 + 4096 + 2048 + 5120])
        KS = arena[:, 0:4096].bitcast(BF16).rearrange("p (h t) -> p h t", h=H)
        QS = arena[:, 4096:8192].bitcast(BF16).rearrange("p (h t) -> p h t", h=H)
        TAB = arena[:, 8192:14336].rearrange("p (h c) -> p h c", h=H)
        V2 = [arena[:, 14336 + 2048 * r:14336 + 2048 * (r + 1)].rearrange("p (t c) -> p t c", t=T) for r in range(2)]
        V2F = [arena[:, 18432 + 1024 * r:18432 + 1024 * (r + 1)].rearrange("p (t c) -> p t c", t=2) for r in range(2)]
        EB = [arena[:, 20480 + 1024 * u:20480 + 1024 * (u + 1)] for u in range(UNITS)]
        WALL = arena[:, 8192:8192 + E * WEXP]
        WG_N = arena[:, 0:E * I].rearrange("p (n c) -> p n c", c=P)
        WU_N = arena[:, E * I:2 * E * I].rearrange("p (n c) -> p n c", c=P)
        WD_N = arena[:, 8192 + E * WEXP:8192 + E * WEXP + E * I].rearrange("p (e i) -> p e i", e=E)
        assert 2 * E * I <= 8192

        WQKV = sb("WQKV", [P, 3 * D])
        WO = sb("WO", [P, D])
        W1 = sb("W1", [P, HID])
        W2 = sb("W2", [P, HC, D])
        RT = sb("RT", [P, E])
        LNW = sb("LNW", [P, 2])
        SCB = sb("SCB", [P, H])
        IDN = sb("IDN", [P, P])
        TRI = sb("TRI", [P, P])
        ONES = sb("ONES", [P, P])
        ST = sb("ST", [P, NT, 6])
        MV = sb("MV", [P, NT, 2])
        RS0 = sb("RS0", [P, NT])
        RR0 = sb("RR0", [P, NT])
        NWA = sb("NWA", [P, P])
        NWB = sb("NWB", [P, P])
        NWC = sb("NWC", [P, P])
        XAR = sb("XAR", [P, T, D])
        XART = sb("XART", [P, S])
        XSUM = sb("XSUM", [P, NB])
        QK = sb("QK", [P, T, 2 * D])
        SQ = sb("SQ", [P, T, 2 * D])
        SS = sb("SS", [P, T * 2 * H])
        RSQ = sb("RSQ", [P, T * 2 * H])
        PF = sb("PF", [P, 2, S])
        PP = sb("PP", [P, 2, 3, S], BF16)
        OS = sb("OS", [P, 2, S])
        RD = sb("RD", [P, T, H])
        YN = sb("YN", [P, T, D])
        YT = sb("YT", [P, S])
        Y = sb("Y", [P, T, D])
        YJ = sb("YJ", [P, T, D])
        VROW = sb("VROW", [1, D])
        ZT = sb("ZT", [P, S])
        H1T = sb("H1T", [P, HC, S])
        A = sb("A", [P, T, D])
        STP = sb("STP", [P, 2, T, 6])
        MVP = sb("MVP", [P, 2, T, 2])
        SSY = sb("SSY", [P, T])
        RZ = sb("RZ", [P, 4, T])
        MH = sb("MH", [P, T])
        XB = [sb(f"XB{r}", [P, T, 2, ROW]) for r in range(2)]
        XBT = sb("XBT", [P, S])
        LG = sb("LG", [P, T, E])
        LG2 = sb("LG2", [P, T, E])
        OH = sb("OH", [P, 2, T, E])
        EQ = sb("EQ", [P, T, E])
        REV = sb("REV", [P, T, E])
        MX = sb("MX", [P, 4, T])
        EX = sb("EX", [P, T, E + 1])
        MM = sb("MM", [P, T, E])
        TB = sb("TB", [P, T + 1, E])
        POS = sb("POS", [P, T, E])
        PSEL = sb("PSEL", [P, 2, T, E])
        POSF = sb("POSF", [P, 2, T])
        IDX = [sb(f"IDX{r}", [P, 2, T], I32) for r in range(2)]
        PADX = sb("PADX", [P, ROW])
        PADI = sb("PADI", [P, E], I32)
        EROW = sb("EROW", [P, E])
        NTE = sb("NTE", [P, E], I32)
        NTF = sb("NTF", [P, 3, E])
        SIO = sb("SIO", [P, STILES])
        SRF = sb("SRF", [P, 2, STILES])
        SRI = sb("SRI", [P, 2, STILES], I32)
        rows = EB[UNITS - 1][0:H, :]
        BR, CMR, RB = rows[:, 0:3 * P], rows[:, 3 * P:4 * P], rows[:, 4 * P:4 * P + BUCKETS]
        GM, SCP = rows[:, 5 * P:5 * P + 1], rows[:, 5 * P + 1:5 * P + 2]
        CF = sb("CF", [P, H])
        WRAW = OS[:, :, :].rearrange("p a b -> p (a b)")[:, 0:3 * D]
        W1R = OS[:, :, :].rearrange("p a b -> p (a b)")[:, 3 * D:3 * D + HID]
        SCM = H1T[:, :, :].rearrange("p a b -> p (a b)")[:, 0:2 * STILES * E].rearrange("p (k s e) -> p k s e", k=2, e=E)
        CMB = H1T[:, :, :].rearrange("p a b -> p (a b)").rearrange("p (h c) -> p h c", h=H)
        XG = [sb(f"XG{r}", [P, ROW]) for r in range(RING)]
        XGT = [XART[:, 0:P], XART[:, P:2 * P]]
        SGB = [PF[:, r, 0:I] for r in range(2)]
        HS = [OS[:, r, 0:I] for r in range(2)]
        HTB = [H1T[:, r, 0:len(IC) * P] for r in range(2)]
        YS = [sb(f"YS{r}", [P, D])[:, :] for r in range(RING)]

        SC = ctx.enter_context(nc.psum_tensor("SC", [P, 2, 1024], F32))
        OA = ctx.enter_context(nc.psum_tensor("OA", [P, 2, 512], F32))
        M0 = ctx.enter_context(nc.psum_tensor("M0", [P, 512], F32))
        M1 = ctx.enter_context(nc.psum_tensor("M1", [P, 512], F32))

        x_in = [sem(f"x_in{i}") for i in range(4)]
        w_in = sem("w_in")
        rel_in = sem("rel_in")
        w2_in = sem("w2_in")
        const_rdy = sem("const_rdy")
        wq_rdy = sem("wq_rdy")
        bias_rows = sem("bias_rows")
        bias_dram = sem("bias_dram")
        bias_in = sem("bias_in")
        tab_raw = sem("tab_raw")
        tab_exp = sem("tab_exp")
        tab_rdy = sem("tab_rdy")
        v2_const = sem("v2_const")
        ks_zero = sem("ks_zero")
        xa_rdy = sem("xa_rdy")
        dve_step = sem("dve_step")
        pool_step = sem("pool_step")
        xar_rdy = sem("xar_rdy")
        m0_full, m0_free = sem("m0_full"), sem("m0_free")
        m1_full, m1_free = sem("m1_full"), sem("m1_free")
        v2f_rdy = sem("v2f_rdy")
        ss_rdy = sem("ss_rdy")
        rs_rdy = sem("rs_rdy")
        qk_norm = sem("qk_norm")
        part1_rdy = sem("part1_rdy")
        part2_rdy = sem("part2_rdy")
        part3_rdy = sem("part3_rdy")
        parts_out = sem("parts_out")
        kq_in = [sem("kq_in0"), sem("kq_in1")]
        qk_done = sem("qk_done")
        exp_done = sem("exp_done")
        mul_dve, mul_pool = sem("mul_dve"), sem("mul_pool")
        pv_done = sem("pv_done")
        o_out = sem("o_out")
        yn_rdy = sem("yn_rdy")
        ssy_rdy = sem("ssy_rdy")
        yroot_rdy = sem("yroot_rdy")
        a_stat = sem("a_stat")
        a_rstd = sem("a_rstd")
        x1_stat = sem("x1_stat")
        x1_rstd = sem("x1_rstd")
        xb_rdy = sem("xb_rdy")
        route_d = sem("route_d")
        route_e = sem("route_e")
        route_m = sem("route_m")
        route_w = sem("route_w")
        idx_rdy = sem("idx_rdy")
        dest_rdy = sem("dest_rdy")
        scattered = [sem("scattered0"), sem("scattered1")]
        dummy_out = sem("dummy_out")
        pad_rdy = sem("pad_rdy")
        pad_out = sem("pad_out")
        table_rdy = sem("table_rdy")
        stg_in = [sem("gate_in"), sem("up_in"), sem("down_in")]
        wt_full, wt_free = sem("wt_full"), [sem("wt_free0"), sem("wt_free1")]
        xg_in = [sem(f"xg_in{i}") for i in range(RING)]
        xt_full, xt_rdy = sem("xt_full"), sem("xt_rdy")
        gu_full, sg_rdy, h_rdy = sem("gu_full"), sem("sg_rdy"), sem("h_rdy")
        ht_full, ht_rdy = sem("ht_full"), sem("ht_rdy")
        y_full, ys_rdy = sem("y_full"), sem("ys_rdy")
        ys_out = [sem(f"ys_out{i}") for i in range(RING)]
        yt_in = [sem(f"yt_in{b}") for b in range(NB)]
        f_stat, f_rstd, f_ln, f_out = sem("f_stat"), sem("f_rstd"), sem("f_ln"), sem("f_out")
        out_done = [sem("out_done0"), sem("out_done1")]

        block = ctx.enter_context(nc.Block())
        x_v = x_d.rearrange("b (i p) d -> p (b i) d", p=P)
        out_v = out_d.rearrange("b (i p) d -> p (b i) d", p=P)

        N_W, N_REL, N_W2 = 5, 3, 4
        HX = NT // 4

        USES0 = 7

        def uses(body):
            return sorted((k for k in M1_USES if (2 <= body <= NB + 1 if k in ROUTE_USES else 1 <= body <= NB)),
                          key=PE_AT[body >= NB].get)

        def use1(body, k):
            return sum(len(uses(c)) for c in range(body)) + uses(body).index(k)

        def drained(body, k):
            return use1(body, k) + 1

        def col(g, j):
            return 8 * (g // 2) + 2 * j + g % 2

        FY = [arena[:, 17152 + 1024 * r:17152 + 1024 * (r + 1)].rearrange("p (k t d) -> p k t d", k=2, t=T) for r in range(NB)]

        blocks = []
        for m in range(2):
            for n in range(E * I // P):
                blocks.append(("gu", m, n))
        for e in range(E):
            for c in range(len(IC)):
                blocks.append(("d", e, c))
        lots = [blocks[i:i + 4] for i in range(0, len(blocks), 4)]
        NWT = len(lots)

        def pieces(kind, a, c):
            if kind == "d":
                return [(IC[c][1], 0, P, a * WEXP + 2 * I + P * c)]
            out, r0 = [], c * P
            while r0 < (c + 1) * P:
                e, i = divmod(r0, I)
                n = min(I - i, (c + 1) * P - r0)
                out.append((P, r0 - c * P, n, e * WEXP + I * a + i))
                r0 += n
            return out

        def copy_lot(copy, i, lot):
            todo = [(dst, SC[0:k, i % 2, P * j + c0:P * j + c0 + n])
                    for j, blk in enumerate(lot) for k, c0, n, at in pieces(*blk)
                    for dst in [WALL[0:k, at:at + n]]]
            for j, (dst, src) in enumerate(todo):
                ins = copy(dst, src)
            ins.then_inc(wt_free[i % 2], 1)

        def mul_first(eng, g, u):
            e = EB[u].rearrange("p (j c) -> p j c", j=2)
            h0 = col(g, 2 * u)
            tab = TAB[:, h0:h0 + 3:2, :].rearrange("p j (a c) -> p j a c", a=3)[:, :, 0:3:2, :]
            v = e[:, :, 0:256].rearrange("p j (a c) -> p j a c", a=2)
            return eng.tensor_tensor(v, v, tab, ALU.mult)

        def mul_mid(eng, g, u):
            e = EB[2 + u].rearrange("p (j c) -> p j c", j=2)
            h0 = col(g, 2 * u)
            a, z = e[:, :, 0:256], e[:, :, 384:512]
            return [eng.tensor_tensor(a, a, TAB[:, h0:h0 + 3:2, P:3 * P], ALU.mult),
                    eng.tensor_tensor(z, z, TAB[:, h0:h0 + 3:2, P:2 * P], ALU.mult)]

        def store(sp, b):
            sp.wait_ge(f_out, b + 1)
            sp.dma_start(out_v[:, T * b:T * (b + 1), :], X[:, T * b:T * (b + 1), :]).then_inc(out_done[b % 2], 16)

        def lots_at(b, n):
            i = 2 * (n - WEIGHTS_AT)
            return [(k, lots[k]) for k in (i, i + 1) if b == NB and 0 <= k < NWT]

        @block.sync
        def _(sp):
            def load_x(i):
                sp.dma_start(X[:, HX * i:HX * (i + 1), :], x_v[:, HX * i:HX * (i + 1), :]).then_inc(x_in[i], 16)

            load_x(0)
            with nc.allow_non_contiguous_dma(reason="small vectors"):
                sp.dma_start(LNW[:, 0:1], ln1_d.rearrange("(h a) -> h a", a=1)).then_inc(w_in, 16)
                sp.dma_start(LNW[:, 1:2], ln2_d.rearrange("(h a) -> h a", a=1)).then_inc(w_in, 16)
                for n, w in enumerate((wq_d, wk_d, wv_d)):
                    sp.dma_start(WRAW[:, n * D:(n + 1) * D], w).then_inc(w_in, 16)
                sp.dma_start(RB[:, :], rel_d.rearrange("r h -> h r")).then_inc(rel_in, 16)
                sp.dma_start(SCP[:, :], scale_d.rearrange("(h a) -> h a", a=1)).then_inc(rel_in, 16)
                sp.dma_start(SCB[:, :], bass.AP(scale_d.tensor, scale_d.offset, [[0, P], [1, H]])).then_inc(rel_in, 16)
                for i in range(1, 4):
                    load_x(i)
                sp.dma_start(W1R, w1_d).then_inc(w2_in, 16)
                sp.dma_start(W2[:, :, :], w2_d.rearrange("(c p) n -> p c n", p=P)).then_inc(w2_in, 16)
                sp.dma_start(RT[:, :], router_d.rearrange("e h -> h e")).then_inc(w2_in, 16)
                sp.dma_start(WO[:, :], wo_d).then_inc(w2_in, 16)
            sp.wait_ge(bias_rows, 1)
            with nc.allow_non_contiguous_dma(reason="broadcasts"):
                sp.dma_start(toe_d.ap(), BR.unsqueeze(1).broadcast_to([H, P, 3 * P])).then_inc(bias_dram, 16)
                sp.dma_start(cm_d.ap(), CMR[:, :]).then_inc(bias_dram, 16)
                sp.dma_start(cfar_d.ap(), BR[:, 3 * P - 1:3 * P]).then_inc(bias_dram, 16)
                sp.wait_ge(bias_dram, 48)
                sp.dma_start(TAB[:, :, P:3 * P], bass.AP(toe_d, P, [[3 * P - 1, P], [3 * P * P, H], [1, 2 * P]])).then_inc(bias_in, 16)
                sp.dma_start(CMB, bass.AP(cm_d, 0, [[0, P], [P, H], [1, P]])).then_inc(bias_in, 16)
                sp.dma_start(CF[:, :], bass.AP(cfar_d, 0, [[0, P], [1, H]])).then_inc(bias_in, 16)
            sp.wait_ge(const_rdy, 1)
            sp.dma_start(slots_d.ap()[DUMMY:DUMMY + P, :], PADX[:, :]).then_inc(dummy_out, 16)

            def stack(b):
                r = b % 2
                for m in range(2):
                    sp.wait_ge(part3_rdy, 2 * b + m + 1)
                    sp.dma_start(parts_d.ap()[r, m].rearrange("c p t -> p c t"), PP[:, m, :, :]).then_inc(parts_out, 16)
                sp.wait_ge(parts_out, 32 * (b + 1))
                if b == 0:
                    sp.wait_ge(ks_zero, 1)
                for half in range(2):
                    hs = slice(8 * half, 8 * half + 8)
                    if b > 0:
                        sp.wait_ge(qk_done, NU * (b - 1) + NU // 2 * (half + 1))
                    src = parts_d.ap()[r].rearrange("m c (d h) t -> m c d h t", h=H)
                    for c in range(3):
                        sp.dma_start(KS[24 * c:24 * c + 24, hs, :],
                                     parts_d.ap()[r, 1].rearrange("c (d h) t -> (c d) h t", h=H)[:, hs, :]
                                     ).then_inc(kq_in[half], 16)
                        for a in range(3):
                            sp.dma_start(QS[8 * (3 * c + a):8 * (3 * c + a) + 8, hs, :], src[0, c, :, hs, :]
                                         ).then_inc(kq_in[half], 16)

            for b in range(NB):
                stack(b)
            sp.wait_ge(qk_done, NU * NB)
            sp.dma_start(WG_N, gate_d.rearrange("e i h -> (e i) h").rearrange("(n p) h -> p n h", p=P)).then_inc(stg_in[0], 16)
            sp.dma_start(WU_N, up_d.rearrange("e i h -> (e i) h").rearrange("(n p) h -> p n h", p=P)).then_inc(stg_in[1], 16)
            sp.wait_ge(pv_done, 3 * GROUPS * NB)
            sp.dma_start(WD_N, down_d.rearrange("e h i -> h e i")).then_inc(stg_in[2], 16)

            sp.wait_ge(pad_rdy, 1)
            for e in range(E):
                row = sp.value_load(PADI[0:1, e:e + 1], min_val=0, max_val=DUMMY)
                sp.dma_start(slots_d.ap()[bass.ds(row, P), :], PADX[:, :]).then_inc(pad_out, 16)

            sp.wait_ge(table_rdy, 1)
            for r in range(2):
                sp.wait_ge(scattered[r], 16 * NT)
            sp.wait_ge(pad_out, 16 * E)
            sp.wait_ge(dummy_out, 16)

            def load(s, r, row):
                sp.dma_start(XG[r][:, :], slots_d.ap()[bass.ds(row, P), :]).then_inc(xg_in[r], 16)

            for s in range(RING):
                row = sp.value_load(SRI[0:1, 0, s:s + 1], min_val=0, max_val=DUMMY)
                load(s, s, row)
            with sp.Fori(1, STILES // RING) as it:
                for r in range(RING):
                    row = sp.value_load(SRI[0:1, 0, bass.ds(RING * it + r, 1)], min_val=0, max_val=DUMMY)
                    sp.wait_ge(ys_out[r], 16 * it)
                    load(None, r, row)

            for r in range(RING):
                sp.wait_ge(ys_out[r], 16 * STILES // RING)
            yt_v = ytok_d.ap().rearrange("(k n p) d -> k p n d", k=2, p=P)
            for b in range(NB):
                for k in range(2):
                    sp.dma_start(FY[b][:, k, :, :], yt_v[k, :, T * b:T * (b + 1), :]).then_inc(yt_in[b], 16)
            for b in range(NB):
                store(sp, b)
            for r in range(2):
                sp.wait_ge(out_done[r], 16 * NB // 2)

        @block.tensor
        def _(pe):
            def take0(b, k):
                if USES0 * b + k > 0:
                    pe.wait_ge(m0_free, USES0 * b + k)

            def take1(body, k):
                if use1(body, k) > 0:
                    pe.wait_ge(m1_free, use1(body, k))

            def turn4(bank, src):
                for t in range(T):
                    mm = pe.transpose(bank[:, P * t:P * (t + 1)], src[:, t, :], IDN[:, :])
                return mm

            def pre_xt(b):
                take0(b, 0)
                pe.wait_ge(xar_rdy, b + 1)
                turn4(M0, XAR).then_inc(m0_full, 1)

            def pre_qkv(b, t):
                take0(b, 1 + t)
                if b == 0 and t == 0:
                    pe.wait_ge(wq_rdy, 1)
                pe.matmul(M0[:, 0:3 * D], XART[:, P * t:P * (t + 1)], WQKV[:, :], start=True, stop=True).then_inc(m0_full, 1)

            def pre_turn(b, m):
                take0(b, 5 + m)
                pe.wait_ge(qk_norm, b + 1)
                for t in range(T):
                    mm = pe.transpose(M0[:, P * t:P * (t + 1)], QK[:, t, D * m:D * (m + 1)], IDN[:, :])
                mm.then_inc(m0_full, 1)

            def scores(b, n):
                g, u = divmod(n, UNITS)
                if NU * b + n >= 2:
                    pe.wait_ge(exp_done, NU * b + n - 1)
                if u == 0 and g % 2 == 0:
                    pe.wait_ge(kq_in[g // 2], 16 * 12 * (b + 1))
                s = SC[:, n % 2, :]
                if u < 2:
                    for i in range(2):
                        h = col(g, 2 * u + i)
                        mm = pe.matmul(s[:, 512 * i:512 * i + 512], KS[:, h, 0:P], QS[:, h, :], start=True, stop=True)
                elif u < 4:
                    for i in range(2):
                        h = col(g, 2 * (u - 2) + i)
                        pe.matmul(s[:, 512 * i:512 * i + 384], KS[:, h, P:2 * P], QS[:, h, P:4 * P], start=True, stop=True)
                        mm = pe.matmul(s[:, 512 * i + 384:512 * i + 512], KS[:, h, 3 * P:4 * P], QS[:, h, 3 * P:4 * P],
                                       start=True, stop=True)
                else:
                    for i in range(4):
                        h = col(g, i)
                        mm = pe.matmul(s[:, 256 * i:256 * i + 256], KS[:, h, 2 * P:3 * P], QS[:, h, 2 * P:4 * P],
                                       start=True, stop=True)
                mm.then_inc(qk_done, 1)

            def pv(b, g, vals, t, q0, n, probs, first=False, last=False):
                for j in range(4):
                    h = col(g, j)
                    mm = pe.matmul(OA[32 * j:32 * j + 32, g // 2, q0:q0 + n], vals[:, t, 32 * h:32 * h + 32], probs(j),
                                   start=first, stop=last, skip_group_check=True)
                return mm

            def pv01(b, g):
                pe.wait_ge(mul_dve, 16 * b + 4 * g + 1)
                pe.wait_ge(mul_pool, 12 * b + 3 * g + 1)
                pe.wait_ge(m0_free, USES0 * b + 5)
                pe.wait_ge(v2f_rdy, b + 1)
                if g % 2 == 0 and b > 0:
                    pe.wait_ge(o_out, 2 * (b - 1) + g // 2 + 1)
                e = lambda q0, n: lambda j: EB[j // 2][:, 512 * (j % 2) + q0:512 * (j % 2) + q0 + n]
                pv(b, g, V2[b % 2], 0, 0, 256, e(0, 256), first=g % 2 == 0)
                pv(b, g, V2F[b % 2], 0, 256, 256, e(256, 256)).then_inc(pv_done, 1)

            def pv23(b, g):
                pe.wait_ge(mul_dve, 16 * b + 4 * g + 3)
                pe.wait_ge(mul_pool, 12 * b + 3 * g + 3)
                e = lambda c, n: lambda j: EB[2 + j // 2][:, 512 * (j % 2) + c:512 * (j % 2) + c + n]
                pv(b, g, V2[b % 2], 1, 128, 256, e(0, 256))
                pv(b, g, V2F[b % 2], 1, 384, 128, e(256, 128))
                pv(b, g, V2[b % 2], 3, 384, 128, e(384, 128)).then_inc(pv_done, 1)

            def pv4(b, g):
                pe.wait_ge(mul_dve, 16 * b + 4 * g + 4)
                e = lambda j: EB[4][:, 256 * j:256 * j + 256]
                pv(b, g, V2[b % 2], 2, 256, 256, e, last=g % 2 == 1).then_inc(pv_done, 1)

            def on_m1(body, k):
                b = body - 2 if k in ROUTE_USES else body - 1
                take1(body, k)
                if k in ("o0", "o1"):
                    pe.wait_ge(o_out, 2 * b + 2)
                    for i in range(2):
                        t = 2 * int(k[1]) + i
                        for bank in range(2):
                            mm = pe.transpose(M1[:, 256 * i + P * bank:256 * i + P * (bank + 1)],
                                              OS[:, bank, P * t:P * (t + 1)], IDN[:, :])
                elif k == "vsum":
                    mm = pe.matmul(M1[0:1, 0:P], XSUM[:, b:b + 1], WQKV[:, 2 * D:3 * D], start=True, stop=True)
                elif k == "yt":
                    pe.wait_ge(yn_rdy, b + 1)
                    mm = turn4(M1, YN)
                elif k == "wo":
                    pe.wait_ge(m1_free, drained(body, "yt"))
                    if b == 0:
                        pe.wait_ge(w2_in, 16 * N_W2)
                    for t in range(T):
                        mm = pe.matmul(M1[:, P * t:P * (t + 1)], YT[:, P * t:P * (t + 1)], WO[:, :], start=True, stop=True)
                elif k == "zt":
                    pe.wait_ge(m1_free, drained(body, "wo"))
                    mm = turn4(M1, Y)
                elif k in ("h0", "h1", "h2", "h3"):
                    c = int(k[1])
                    pe.wait_ge(m1_free, drained(body, "zt"))
                    if b == 0 and c == 0:
                        pe.wait_ge(wq_rdy, 2)
                    mm = pe.matmul(M1[:, :], W1[:, P * c:P * (c + 1)], ZT[:, :], start=True, stop=True)
                elif k == "ffn":
                    pe.wait_ge(m1_free, drained(body, "h3"))
                    for t in range(T):
                        for c in range(HC):
                            mm = pe.matmul(M1[:, P * t:P * (t + 1)], H1T[:, c, P * t:P * (t + 1)], W2[:, c, :],
                                           start=c == 0, stop=c == HC - 1)
                elif k == "rx":
                    pe.wait_ge(xb_rdy, b + 1)
                    for t in range(T):
                        mm = pe.transpose(M1[:, P * t:P * (t + 1)], XB[b % 2][:, t, 0, 0:D], IDN[:, :])
                elif k == "logits":
                    pe.wait_ge(m1_free, drained(body, "rx"))
                    for t in range(T):
                        mm = pe.matmul(M1[:, E * t:E * (t + 1)], XBT[:, P * t:P * (t + 1)], RT[:, :], start=True, stop=True)
                else:
                    pe.wait_ge(route_m, b + 1)
                    mflat = MM[:, :, :].rearrange("p t e -> p (t e)")
                    pe.matmul(M1[:, 0:T * E], TRI[:, :], mflat, start=True, stop=True)
                    mm = pe.matmul(M1[:, T * E:2 * T * E], ONES[:, :], mflat, start=True, stop=True)
                mm.then_inc(m1_full, 1)

            def weights(n, lot):
                if n == 0:
                    pe.wait_ge(exp_done, NU * NB)
                if n >= 2:
                    pe.wait_ge(wt_free[n % 2], n // 2)
                for i, (kind, a, c) in enumerate(lot):
                    dst = SC[:, n % 2, P * i:P * (i + 1)]
                    pe.wait_ge(stg_in[2 if kind == "d" else a], 16)
                    if kind == "gu":
                        mm = pe.transpose(dst, (WG_N, WU_N)[a][:, c, :], IDN[:, :])
                    else:
                        i0, k = IC[c]
                        mm = pe.transpose(dst[0:k, :], WD_N[:, a, i0:i0 + k], IDN[:, :])
                mm.then_inc(wt_full, 1)

            pe.wait_ge(const_rdy, 1)
            pre_xt(0)
            for t in range(T):
                pre_qkv(0, t)
            for m in range(2):
                pre_turn(0, m)
            for b in range(NB + 2):
                at = PE_AT[b >= NB]
                for n in range(NU):
                    g, u = divmod(n, UNITS)
                    if b < NB:
                        scores(b, n)
                    before = (b, g - 1) if g else (b - 1, GROUPS - 1)
                    if 0 <= before[0] < NB and (b < NB or before[0] == NB - 1 and b == NB and g == 0):
                        if u == 1:
                            pv23(*before)
                        if u == 2:
                            pv4(*before)
                    if b < NB and u == 4:
                        pv01(b, g)
                    if b + 1 < NB:
                        if n == at["xt"]:
                            pre_xt(b + 1)
                        for t in range(T):
                            if n == at[f"qkv{t}"]:
                                pre_qkv(b + 1, t)
                        for m in range(2):
                            if n == at[f"turn{m}"]:
                                pre_turn(b + 1, m)
                    for k in uses(b):
                        if n == at[k]:
                            on_m1(b, k)
                    for i, lot in lots_at(b, n):
                        weights(i, lot)

            def xt(s, r, nload):
                pe.wait_ge(xg_in[r % RING], nload)
                pe.wait_ge(xt_rdy, s)
                pe.transpose(M0[:, 0:P], XG[r % RING][:, 0:D], IDN[:, :]).then_inc(xt_full, 1)

            def gu(s, r, off):
                if isinstance(s, int) and s + 1 == STILES:
                    pe.wait_ge(xt_rdy, s + 1)
                for m in range(2):
                    mm = pe.matmul(SC[:, r % 2, 512 * m:512 * m + I], XGT[r % 2], WALL[:, bass.ds(off + I * m, I)],
                                   start=True, stop=True)
                mm.then_inc(gu_full, 1)

            def ht(s, r):
                pe.wait_ge(h_rdy, s + 1)
                for c, (i0, n) in enumerate(IC):
                    mm = pe.transpose(OA[0:n, r % 2, P * c:P * (c + 1)], HS[r % 2][:, i0:i0 + n], IDN[:, :])
                mm.then_inc(ht_full, 1)

            def down(s, r, off):
                pe.wait_ge(ht_rdy, s + 1)
                if not isinstance(s, int) or s >= 1:
                    pe.wait_ge(ys_rdy, s)
                for c, (i0, n) in enumerate(IC):
                    mm = pe.matmul(M1[:, 0:P], HTB[r % 2][0:n, P * c:P * (c + 1)],
                                   WALL[0:n, bass.ds(off + 2 * I + P * c, P)], start=c == 0, stop=c == len(IC) - 1)
                mm.then_inc(y_full, 1)

            def woff(s):
                at = slice(s, s + 1) if isinstance(s, int) else bass.ds(s, 1)
                return pe.value_load(SRI[0:1, 1, at], min_val=0, max_val=(E - 1) * WEXP)

            def step(s, r, it):
                if not isinstance(s, int) or s + 1 < STILES:
                    xt(s + 1, r + 1, 16 * (it + 1 + (r + 1) // RING))
                if not isinstance(s, int) or s < STILES:
                    gu(s, r, woff(s))
                if not isinstance(s, int) or 1 <= s <= STILES:
                    ht(s - 1, r + 1)
                if not isinstance(s, int) or s >= 2:
                    down(s - 2, r, woff(s - 2))

            pe.wait_ge(table_rdy, 1)
            pe.wait_ge(m0_free, USES0 * NB)
            pe.wait_ge(m1_free, drained(NB + 1, uses(NB + 1)[-1]))
            for r in range(2):
                pe.wait_ge(wt_free[r], (NWT + 1 - r) // 2)
            pe.wait_ge(xg_in[0], 16)
            pe.transpose(M0[:, 0:P], XG[0][:, 0:D], IDN[:, :]).then_inc(xt_full, 1)
            for s in range(RING):
                step(s, s, 0)
            with pe.Fori(1, STILES // RING - 1) as it:
                for r in range(RING):
                    step(RING * it + r, r, it)
            for s in range(STILES - RING, STILES + 2):
                step(s, s % RING, s // RING)

        @block.scalar
        def _(act):
            def exp_unit(b, n):
                u = n % UNITS
                act.wait_ge(qk_done, NU * b + n + 1)
                done = 3 * (GROUPS * b + n // UNITS) + (-2, -2, -1, -1, 0)[u]
                if done > 0:
                    act.wait_ge(pv_done, done)
                act.activation(EB[u], SC[:, n % 2, :], ACT.Exp).then_inc(exp_done, 1)

            def pre_copy(b, k):
                act.wait_ge(m0_full, USES0 * b + k + 1)
                if k == 0:
                    act.activation(XART[:, :], M0[:, :], ACT.Copy, accum_out=XSUM[:, b:b + 1]).then_inc(m0_free, 1)
                    return
                t = k - 1
                if k == 1 and b == 0:
                    act.wait_ge(v2_const, 2)
                if k == 1 and b >= 1:
                    act.wait_ge(ss_rdy, b)
                if k == 1 and b >= 2:
                    act.wait_ge(pv_done, 12 * (b - 1))
                act.activation(QK[:, t, :], M0[:, 0:2 * D], ACT.Copy)
                act.activation(SQ[:, t, :], M0[:, 0:2 * D], ACT.Square)
                v2 = V2[b % 2][:, t, :].rearrange("p (n s) -> p n s", s=64)
                v = M0[:, 2 * D:3 * D].rearrange("p (n a d) -> p n a d", a=2, d=DH)
                act.activation(v2[:, :, 0:8], v[:, :, 0, :], ACT.Copy)
                act.activation(v2[:, :, 48:56], v[:, :, 1, :], ACT.Copy).then_inc(m0_free, 1)

            def first_part(b, m):
                act.wait_ge(m0_full, USES0 * b + 6 + m)
                if b > 0:
                    act.wait_ge(parts_out, 32 * b)
                act.activation(PP[:, m, 0, :], M0[:, :], ACT.Copy).then_inc(part1_rdy, 1)

            def second_part(b, m):
                act.wait_ge(m0_free, USES0 * b + 6 + m)
                act.activation(PP[:, m, 1, :], PF[:, m, :], ACT.Copy).then_inc(part2_rdy, 1)

            def out_bank(b, bank):
                act.wait_ge(pv_done, 12 * b + 6 * (bank + 1))
                if b > 0:
                    act.wait_ge(m1_full, use1(b, "o1") + 1)
                act.activation(OS[:, bank, :], OA[:, bank, :], ACT.Copy).then_inc(o_out, 1)

            def evac(body, k):
                act.wait_ge(m1_full, use1(body, k) + 1)
                dst, func = {"yt": (YT[:, :], ACT.Copy), "zt": (ZT[:, :], ACT.Copy),
                             "rx": (XBT[:, :], ACT.Copy)}.get(k) or (H1T[:, int(k[1]), :], ACT.Relu)
                act.activation(dst, M1[:, :], func).then_inc(m1_free, 1)

            for k in range(5):
                pre_copy(0, k)
            for m in range(2):
                first_part(0, m)
                second_part(0, m)
            act.wait_ge(bias_in, 48)
            act.activation(CF[:, :], CF[:, :], ACT.Exp).then_inc(tab_exp, 1)
            act.wait_ge(tab_raw, 1)
            act.activation(TAB, TAB, ACT.Exp).then_inc(tab_exp, 1)
            for b in range(NB + 2):
                at = ACT_AT[b >= NB]
                for n in range(NU):
                    if b < NB:
                        exp_unit(b, n)
                    if b + 1 < NB:
                        for k, step in enumerate(("xt", "qkv0", "qkv1", "qkv2", "qkv3")):
                            if n == at[step]:
                                pre_copy(b + 1, k)
                        for m in range(2):
                            if n == at[f"part{m}"]:
                                first_part(b + 1, m)
                        for m in range(2):
                            if n == at[f"half{m}"]:
                                second_part(b + 1, m)
                    if b < NB and n == at["out0"]:
                        out_bank(b, 0)
                    if n == at["out1"] and 1 <= b <= NB:
                        out_bank(b - 1, 1)
                    if n == at["ysq"] and 1 <= b <= NB:
                        act.wait_ge(m1_free, drained(b, "wo"))
                        if b >= 2:
                            act.wait_ge(yroot_rdy, b - 1)
                        for t in range(T):
                            ins = act.activation(YJ[:, t, :], Y[:, t, :], ACT.Square, accum_out=SSY[:, t:t + 1])
                        ins.then_inc(ssy_rdy, 1)
                    for k in uses(b):
                        if k in at and n == at[k]:
                            evac(b, k)
                    if b >= 2 and n == at["rexp"]:
                        act.wait_ge(route_d, b - 1)
                        act.activation(EX[:, :, :], EX[:, :, :], ACT.Exp).then_inc(route_e, 1)
                    for i, lot in lots_at(b, n):
                        if i % 2 == 0:
                            act.wait_ge(wt_full, i + 1)
                            act.wait_ge(pv_done, 3 * GROUPS * NB)
                            copy_lot(act.copy, i, lot)

            def evac_x(s, r):
                act.wait_ge(xt_full, s + 1)
                act.activation(XGT[r % 2], M0[:, 0:P], ACT.Copy).then_inc(xt_rdy, 1)

            def silu(s, r):
                act.wait_ge(gu_full, s + 1)
                act.activation(SGB[r % 2], SC[:, r % 2, 0:I], ACT.Silu).then_inc(sg_rdy, 1)

            def evac_y(s, r):
                act.wait_ge(y_full, s + 1)
                act.activation(YS[r % RING], M1[:, 0:P], ACT.Copy, scale=XG[r % RING][:, D:D + 1]).then_inc(ys_rdy, 1)

            def step(s, r):
                if not isinstance(s, int) or s + 1 < STILES:
                    evac_x(s + 1, r + 1)
                if not isinstance(s, int) or s < STILES:
                    silu(s, r)
                if not isinstance(s, int) or s >= 2:
                    evac_y(s - 2, r - 2)

            evac_x(0, 0)
            for s in range(RING):
                step(s, s)
            with act.Fori(1, STILES // RING - 1) as it:
                for r in range(RING):
                    step(RING * it + r, r)
            for s in range(STILES - RING, STILES + 2):
                step(s, s % RING)

        @block.vector
        def _(dve):
            steps = [0]

            def link(ins):
                steps[0] += 1
                ins.then_inc(dve_step, 1)
                dve.wait_ge(dve_step, steps[0])

            def rsqrt(y, a, u):
                link(dve.tensor_scalar(y.bitcast(I32), a.bitcast(I32), 1, None, ALU.logical_shift_right))
                link(dve.tensor_scalar(y.bitcast(I32), y.bitcast(I32), -1.0, RSQRT_SEED, ALU.mult, ALU.add))
                for _ in range(3):
                    link(dve.tensor_tensor(u, y, y, ALU.mult))
                    link(dve.scalar_tensor_tensor(u, u, -0.5, a, ALU.mult, ALU.mult))
                    link(dve.scalar_tensor_tensor(y, u, 1.5, y, ALU.add, ALU.mult))

            def bc(ap, shape):
                return ap.unsqueeze(len(shape) - 1).broadcast_to(shape)

            def statistics(i0, n):
                for i in range(i0, i0 + n):
                    last = dve.bn_stats(ST[:, i, :], X[:, i, :])
                link(last)
                for i in range(i0, i0 + n):
                    last = dve.bn_aggr(MV[:, i, :], ST[:, i, :])
                link(last)
                a, u, w = NWA[:, 0:n], NWB[:, 0:n], NWC[:, 0:n]
                var, rs = MV[:, i0:i0 + n, 1], RS0[:, i0:i0 + n]
                link(dve.tensor_scalar(a, var, LN_EPS, None, ALU.add))
                rsqrt(rs, a, u)
                link(dve.tensor_tensor(w, rs, rs, ALU.mult))
                link(dve.tensor_tensor(w, w, var, ALU.mult))
                link(dve.tensor_scalar(a, w, RMS_EPS, None, ALU.add))
                rsqrt(w, a, u)
                link(dve.tensor_tensor(RR0[:, i0:i0 + n], w, rs, ALU.mult))

            def xar(b):
                if b > 0:
                    dve.wait_ge(m0_full, USES0 * (b - 1) + 1)
                for t in range(T):
                    i = T * b + t
                    last = dve.tensor_scalar(XAR[:, t, :], X[:, i, :], MV[:, i, 0:1], RR0[:, i:i + 1], ALU.subtract, ALU.mult)
                last.then_inc(xar_rdy, 1)

            def xa(b):
                if b > 0:
                    dve.wait_ge(m1_free, drained(b, "wo"))
                for t in range(T):
                    i = T * b + t
                    last = dve.tensor_scalar(XA[:, t, :], X[:, i, :], MV[:, i, 0:1], RS0[:, i:i + 1], ALU.subtract, ALU.mult)
                last.then_inc(xa_rdy, 1)

            dve.wait_ge(x_in[0], 16)
            statistics(0, T)
            xar(0)
            dve.wait_ge(w_in, 16 * N_W)
            for m in range(2):
                dve.tensor_scalar(WQKV[:, D * m:D * (m + 1)].rearrange("p (d h) -> p h d", h=H),
                                  WRAW[:, D * m:D * (m + 1)].rearrange("p (h d) -> p h d", h=H), LNW[:, 0:1], None, ALU.mult)
            dve.tensor_scalar(WQKV[:, 2 * D:3 * D], WRAW[:, 2 * D:3 * D], LNW[:, 0:1], None, ALU.mult).then_inc(wq_rdy, 1)
            dve.wait_ge(rel_in, 16 * N_REL)
            link(dve.tensor_scalar(RB[:, :], RB[:, :], SCP[:, 0:1], None, ALU.mult))
            dve.memset(BR[:, 0:P + 1], NEG)
            exact = BUCKETS // 2
            dve.tensor_copy(BR[:, P + 1:P + exact], RB[:, 1:exact])
            ends = starts[1:] + [2 * P]
            for r in range(exact, BUCKETS):
                a, z = starts[r - exact], ends[r - exact]
                last = dve.tensor_copy(BR[:, P + a:P + z], RB[:, r:r + 1].broadcast_to([H, z - a]))
            link(last)
            link(dve.tensor_reduce(GM[:, :], BR[:, P + 1:3 * P], AX, ALU.max))
            link(dve.tensor_scalar(BR[:, P + 1:3 * P], BR[:, P + 1:3 * P], GM[:, 0:1], None, ALU.subtract))
            dve.memset(CMR[:, 0:1], 0.0)
            dve.tensor_tensor_scan(CMR[:, 1:P], BR[:, P + 1:2 * P], BR[:, P + 1:2 * P], NEG, ALU.max, ALU.max
                                   ).then_inc(bias_rows, 1)

            def norm_sums(b):
                dve.wait_ge(m0_free, USES0 * b + 5)
                link(dve.tensor_reduce(SS[:, :].rearrange("p (g h) -> p g h", h=H),
                                       SQ[:, :, :].rearrange("p t c -> p (t c)").rearrange("p (g d h) -> p g h d", d=DH, h=H), AX, ALU.add))
                dve.tensor_scalar(SS[:, :], SS[:, :], KQ_EPS, None, ALU.add).then_inc(ss_rdy, 1)

            def norm_roots(b):
                dve.wait_ge(ss_rdy, b + 1)
                rsqrt(RSQ[:, :], SS[:, :], NWA[:, :])
                rs = RSQ[:, :].rearrange("p (t m h) -> p t m h", t=T, m=2)
                dve.tensor_tensor(rs[:, :, 0, :], rs[:, :, 0, :], SCB[:, :].unsqueeze(1).broadcast_to([P, T, H]), ALU.mult
                                  ).then_inc(rs_rdy, 1)

            def norm_apply(b):
                dve.wait_ge(rs_rdy, b + 1)
                rs = RSQ[:, :].rearrange("p (t m h) -> p t m h", t=T, m=2)
                for t in range(T):
                    v = QK[:, t, :].rearrange("p (m d h) -> p m d h", m=2, h=H)
                    last = dve.tensor_tensor(v, v, rs[:, t].unsqueeze(2).broadcast_to([P, 2, DH, H]), ALU.mult)
                last.then_inc(qk_norm, 1)

            def remainder(b, m):
                dve.wait_ge(part1_rdy, 2 * b + m + 1)
                if b > 0:
                    dve.wait_ge(part3_rdy, 2 * (b - 1) + m + 1)
                dve.tensor_tensor(PF[:, m, :], M0[:, :], PP[:, m, 0, :], ALU.subtract).then_inc(m0_free, 1)

            def mul(b, n):
                g, u = divmod(n, UNITS)
                heads = slice(col(g, 0), col(g, 3) + 1, 2)
                if u == 0:
                    mul_first(dve, g, 0).then_inc(mul_dve, 1)
                elif u == 2:
                    for i in mul_mid(dve, g, 0):
                        i.then_inc(mul_dve, 1)
                elif u == 4:
                    e = EB[4].rearrange("p (j c) -> p j c", j=4)
                    dve.tensor_tensor(e, e, TAB[:, heads, P:3 * P], ALU.mult).then_inc(mul_dve, 1)

            def post(body, k):
                b = body - 1
                dve.wait_ge(m1_full, use1(body, k) + 1)
                if k in ("o0", "o1"):
                    t0 = 2 * int(k[1])
                    v = M1[:, :].rearrange("p (t n c) -> p t n c", t=2, c=16)
                    link(dve.reciprocal(RD[:, t0:t0 + 2, :], v[:, :, :, DH]))
                    for i in range(2):
                        last = dve.tensor_tensor(YN[:, t0 + i, :].rearrange("p (n d) -> p n d", d=DH), v[:, i, :, 0:DH],
                                                 RD[:, t0 + i, :].unsqueeze(2).broadcast_to([P, H, DH]), ALU.mult)
                    last.then_inc(m1_free, 1)
                    if k == "o1":
                        dve.wait_ge(m1_free, use1(body, k) + 1)
                        dve.tensor_copy(YN[0:1, 0, :], VROW[0:1, :]).then_inc(yn_rdy, 1)
                elif k == "vsum":
                    dve.tensor_scalar(VROW[0:1, :], M1[0:1, 0:P], 1.0 / S, None, ALU.mult).then_inc(m1_free, 1)
                    dve.wait_ge(m1_free, use1(body, k) + 1)
                elif k == "wo":
                    dve.wait_ge(xa_rdy, b + 1)
                    dve.tensor_tensor(Y[:, :, :].rearrange("p t d -> p (t d)"), M1[:, :],
                                      XA[:, :, :].rearrange("p t d -> p (t d)"), ALU.add).then_inc(m1_free, 1)
                elif k == "ffn":
                    dve.wait_ge(yroot_rdy, b + 1)
                    for t in range(T):
                        last = dve.scalar_tensor_tensor(A[:, t, :], M1[:, P * t:P * (t + 1)], RZ[:, 0, t:t + 1], Y[:, t, :],
                                                        ALU.mult, ALU.add)
                    last.then_inc(m1_free, 1)
                    dve.wait_ge(m1_free, use1(body, k) + 1)

            def stats(src, r, done):
                for t in range(T):
                    last = dve.bn_stats(STP[:, r, t, :], src[:, t, :])
                link(last)
                for t in range(T):
                    last = dve.bn_aggr(MVP[:, r, t, :], STP[:, r, t, :])
                last.then_inc(done, 1)

            def top2(b):
                dve.wait_ge(m1_full, use1(b + 2, "logits") + 1)
                dve.tensor_copy(LG[:, :, :].rearrange("p t e -> p (t e)"), M1[:, 0:T * E]).then_inc(m1_free, 1)
                dve.wait_ge(m1_free, use1(b + 2, "logits") + 1)
                lg = LG
                for k in range(2):
                    link(dve.tensor_reduce(MX[:, k, :], lg[:, :, :], AX, ALU.max))
                    link(dve.tensor_tensor(EQ[:, :, :], lg[:, :, :], bc(MX[:, k, :], [P, T, E]), ALU.is_equal))
                    link(dve.tensor_tensor(EQ[:, :, :], EQ[:, :, :], REV[:, :, :], ALU.mult))
                    link(dve.tensor_reduce(MX[:, 2, :], EQ[:, :, :], AX, ALU.max))
                    link(dve.tensor_tensor(OH[:, k], EQ[:, :, :], bc(MX[:, 2, :], [P, T, E]), ALU.is_equal))
                    if k == 0:
                        link(dve.scalar_tensor_tensor(LG2[:, :, :], OH[:, 0], NEG, LG[:, :, :], ALU.mult, ALU.add))
                        lg = LG2
                dve.tensor_tensor(MM[:, :, :], OH[:, 0], OH[:, 1], ALU.add).then_inc(route_m, 1)
                dve.tensor_tensor(EX[:, :, 0:E], LG[:, :, :], bc(MX[:, 0, :], [P, T, E]), ALU.subtract)
                dve.tensor_tensor(EX[:, :, E], MX[:, 1, :], MX[:, 0, :], ALU.subtract).then_inc(route_d, 1)

            def place(b):
                r = b % 2
                dve.wait_ge(route_e, b + 1)
                link(dve.tensor_reduce(MX[:, 2, :], EX[:, :, 0:E], AX, ALU.add))
                link(dve.reciprocal(MX[:, 3, :], MX[:, 2, :]))
                dve.tensor_copy(XB[r][:, :, 0, D], MX[:, 3, :])
                dve.tensor_tensor(XB[r][:, :, 1, D], MX[:, 3, :], EX[:, :, E], ALU.mult).then_inc(route_w, 1)
                dve.wait_ge(m1_full, use1(b + 2, "count") + 1)
                for t in range(T):
                    link(dve.tensor_tensor(TB[:, t + 1, :], TB[:, t, :], M1[:, E * (T + t):E * (T + t + 1)], ALU.add))
                link(dve.tensor_tensor(POS[:, :, :], M1[:, 0:T * E].rearrange("p (t e) -> p t e", t=T), TB[:, 0:T, :], ALU.add))
                for k in range(2):
                    last = dve.tensor_tensor(PSEL[:, k], OH[:, k], POS[:, :, :], ALU.mult)
                last.then_inc(m1_free, 1)
                dve.wait_ge(m1_free, use1(b + 2, "count") + 1)
                dve.tensor_copy(TB[:, 0, :], TB[:, T, :])
                link(dve.tensor_reduce(POSF[:, :, :], PSEL[:, :, :, :], AX, ALU.add))
                if b >= 2:
                    dve.wait_ge(scattered[r], 16 * 2 * T * (b // 2))
                dve.tensor_copy(IDX[r][:, :, :], POSF[:, :, :]).then_inc(idx_rdy, 1)
                dve.wait_ge(idx_rdy, b + 1)

            norm_sums(0)
            norm_roots(0)
            norm_apply(0)
            for m in range(2):
                remainder(0, m)
            dve.wait_ge(bias_in, 48)
            dve.tensor_tensor(TAB[:, :, 0:P], TAB[:, :, P:2 * P], CMB, ALU.subtract).then_inc(tab_raw, 1)
            statistics(T, HX - T)
            xar(1)
            dve.wait_ge(tab_exp, 2)
            dve.memset(TAB[0:1, :, 0:1], 1.0).then_inc(tab_rdy, 1)
            dve.wait_ge(tab_rdy, 1)
            dve.wait_ge(w2_in, 16 * N_W2)
            dve.tensor_scalar(W1[:, :], W1R, LNW[:, 1:2], None, ALU.mult).then_inc(wq_rdy, 1)
            dve.wait_ge(const_rdy, 1)
            dve.tensor_copy(TB[:, 0, :], EROW[:, :])
            for b in range(NB + 2):
                at = DVE_AT[b >= NB]
                for n in range(NU):
                    if b < NB and n % UNITS in (0, 2, 4):
                        dve.wait_ge(exp_done, NU * b + n + 1)
                        mul(b, n)
                    if b + 1 < NB:
                        if n == at["norm0"]:
                            norm_sums(b + 1)
                        if n == at["norm1"]:
                            norm_roots(b + 1)
                        if n == at["norm2"]:
                            norm_apply(b + 1)
                        for m in range(2):
                            if n == at[f"rem{m}"]:
                                remainder(b + 1, m)
                    if b < NB and n == at["xar"]:
                        if b % 2 == 0 and b + 2 < NB:
                            dve.wait_ge(x_in[(b + 2) // 2], 16)
                            statistics(T * (b + 2), HX)
                        if b + 2 < NB:
                            xar(b + 2)
                    if b >= 2:
                        if n == at["top2"]:
                            top2(b - 2)
                        if n == at["place"]:
                            place(b - 2)
                    if 1 <= b <= NB:
                        c = b - 1
                        if n == at["xa"]:
                            xa(c)
                        for k in ("vsum", "o0", "o1", "wo"):
                            if n == at[k]:
                                post(b, k)
                        if n == at["ffn"]:
                            post(b, "ffn")
                            stats(A, 0, a_stat)
                        if n == at["ln"]:
                            dve.wait_ge(a_rstd, c + 1)
                            for t in range(T):
                                last = dve.tensor_scalar(A[:, t, :], A[:, t, :], MVP[:, 0, t, 0:1], RZ[:, 1, t:t + 1],
                                                         ALU.subtract, ALU.mult)
                            link(last)
                            x1 = X[:, T * c:T * (c + 1), :]
                            link(dve.tensor_tensor(x1, x1, A[:, :, :], ALU.add))
                            stats(x1, 1, x1_stat)
                        if n == at["xb"]:
                            dve.wait_ge(x1_rstd, c + 1)
                            if c >= 2:
                                dve.wait_ge(scattered[c % 2], 16 * 2 * T * (c // 2))
                            for t in range(T):
                                for k in range(2):
                                    last = dve.tensor_scalar(XB[c % 2][:, t, k, 0:D], X[:, T * c + t, :], MVP[:, 1, t, 0:1],
                                                             RZ[:, 2, t:t + 1], ALU.subtract, ALU.mult)
                            last.then_inc(xb_rdy, 1)
                    for i, lot in lots_at(b, n):
                        if i % 2 == 1:
                            dve.wait_ge(wt_full, i + 1)
                            dve.wait_ge(pv_done, 3 * GROUPS * NB)
                            copy_lot(dve.tensor_copy, i, lot)

            dve.tensor_copy(PADI[:, :], TB[:, T, :]).then_inc(pad_rdy, 1)
            link(dve.tensor_tensor(NTF[:, 0, :], TB[:, T, :], EROW[:, :], ALU.subtract))
            link(dve.tensor_scalar(NTE[:, :], NTF[:, 0, :], float(P - 1), None, ALU.add))
            link(dve.tensor_scalar(NTE[:, :], NTE[:, :], 7, None, ALU.logical_shift_right))
            link(dve.tensor_copy(NTF[:, 0, :], NTE[:, :]))
            link(dve.tensor_copy(NTF[:, 1, 0:1], NTF[:, 0, 0:1]))
            for e in range(1, E):
                link(dve.tensor_tensor(NTF[:, 1, e:e + 1], NTF[:, 1, e - 1:e], NTF[:, 0, e:e + 1], ALU.add))
            link(dve.tensor_scalar(NTF[:, 2, :], NTF[:, 0, :], -float(P), float(REGION), ALU.mult, ALU.add))
            sh = [P, STILES, E]
            link(dve.tensor_tensor(SCM[:, 0], SIO[:, :].unsqueeze(2).broadcast_to(sh),
                                   NTF[:, 1, :].unsqueeze(1).broadcast_to(sh), ALU.is_ge))
            link(dve.tensor_tensor(SCM[:, 1], SCM[:, 0], NTF[:, 2, :].unsqueeze(1).broadcast_to(sh), ALU.mult))
            dve.tensor_reduce(SRF[:, 0, :], SCM[:, 1], AX, ALU.add)
            link(dve.tensor_reduce(SRF[:, 1, :], SCM[:, 0], AX, ALU.add))
            link(dve.scalar_tensor_tensor(SRF[:, 0, :], SIO[:, :], float(P), SRF[:, 0, :], ALU.mult, ALU.add))
            dve.tensor_scalar(SRI[:, 0, :], SRF[:, 0, :], float(DUMMY), None, ALU.min)
            dve.tensor_scalar(SRI[:, 1, :], SRF[:, 1, :], float(E - 1), float(WEXP), ALU.min, ALU.mult).then_inc(table_rdy, 1)

            def hidden(s, r):
                dve.wait_ge(sg_rdy, s + 1)
                dve.tensor_tensor(HS[r % 2], SGB[r % 2], SC[:, r % 2, 512:512 + I], ALU.mult).then_inc(h_rdy, 1)

            def evac_h(s, r):
                dve.wait_ge(ht_full, s + 1)
                k = IC[-1][1]
                full = P * (len(IC) - 1)
                dve.tensor_copy(HTB[r % 2][:, 0:full], OA[:, r % 2, 0:full])
                dve.tensor_copy(HTB[r % 2][0:k, full:full + P], OA[0:k, r % 2, full:full + P]).then_inc(ht_rdy, 1)

            def step(s, r):
                if not isinstance(s, int) or s < STILES:
                    hidden(s, r)
                if not isinstance(s, int) or 1 <= s <= STILES:
                    evac_h(s - 1, r + 1)

            for s in range(RING):
                step(s, s)
            with dve.Fori(1, STILES // RING - 1) as it:
                for r in range(RING):
                    step(RING * it + r, r)
            for s in range(STILES - RING, STILES + 1):
                step(s, s % RING)

            for b in range(NB + 1):
                if b < NB:
                    dve.wait_ge(yt_in[b], 32)
                    link(dve.tensor_tensor(FY[b][:, 0], FY[b][:, 0], FY[b][:, 1], ALU.add))
                    stats(FY[b][:, 0], b % 2, f_stat)
                if b >= 1:
                    c = b - 1
                    dve.wait_ge(f_rstd, c + 1)
                    for t in range(T):
                        last = dve.tensor_scalar(FY[c][:, 0, t, :], FY[c][:, 0, t, :], MVP[:, c % 2, t, 0:1],
                                                 RZ[:, c % 2, t:t + 1], ALU.subtract, ALU.mult)
                    last.then_inc(f_ln, 1)

        @block.gpsimd
        def _(pool):
            steps = [0]

            def link(ins):
                steps[0] += 1
                ins.then_inc(pool_step, 1)
                pool.wait_ge(pool_step, steps[0])

            pool.memset(IDN[:, :], 0.0)
            pool.memset(TRI[:, :], 1.0)
            pool.memset(ONES[:, :], 1.0)
            pool.memset(MH[:, :], -0.5)
            pool.memset(PADX[:, :], 0.0)
            pool.iota(EROW[:, :], pattern=[[REGION, E]], base=0, channel_multiplier=0, allow_small_or_imprecise_dtypes=True)
            pool.iota(REV[:, :, :], pattern=[[0, T], [-1, E]], base=E, channel_multiplier=0, allow_small_or_imprecise_dtypes=True)
            link(pool.iota(SIO[:, :], pattern=[[1, STILES]], base=0, channel_multiplier=0, allow_small_or_imprecise_dtypes=True))
            pool.affine_select(out=IDN[:, :], in_=IDN[:, :], compare_op=ALU.not_equal, fill=1.0, base=0,
                               pattern=[[-1, P]], channel_multiplier=1)
            pool.affine_select(out=TRI[:, :], in_=TRI[:, :], compare_op=ALU.is_gt, fill=0.0, base=0,
                               pattern=[[1, P]], channel_multiplier=-1)
            pool.iota(PADX[:, D + 1:D + 2].bitcast(I32), pattern=[[0, 1]], base=NO_ROW, channel_multiplier=0).then_inc(const_rdy, 1)
            for r in range(2):
                link(pool.memset(V2[r][:, :, :], 0.0))
                v = V2[r].rearrange("p t (n s) -> p t n s", s=64)
                pool.memset(v[:, :, :, 8:16], 1.0)
                pool.memset(v[:, :, :, 56:64], 1.0).then_inc(v2_const, 1)
            pool.wait_ge(v2_const, 2)
            pool.memset(arena[64:P, 0:4096], 0.0)
            pool.memset(arena[64:P, 4096:8192], 0.0).then_inc(ks_zero, 1)
            pool.wait_ge(ks_zero, 1)

            def far_values(b):
                pool.wait_ge(m0_free, USES0 * b + 5)
                if b == 0:
                    pool.wait_ge(tab_exp, 1)
                if b >= 2:
                    pool.wait_ge(pv_done, 12 * (b - 1))
                for t in range(2):
                    last = pool.tensor_tensor(V2F[b % 2][:, t, :].rearrange("p (h s) -> p h s", h=H),
                                              V2[b % 2][:, t, :].rearrange("p (h s) -> p h s", h=H),
                                              CF[:, :].unsqueeze(2).broadcast_to([P, H, 32]), ALU.mult)
                last.then_inc(v2f_rdy, 1)

            def third(b, m):
                pool.wait_ge(part2_rdy, 2 * b + m + 1)
                pool.tensor_tensor(PP[:, m, 2, :], PF[:, m, :], PP[:, m, 1, :], ALU.subtract).then_inc(part3_rdy, 1)

            def inv_root(k, src, scale, eps, done):
                link(pool.tensor_scalar(RZ[:, k, :], src, scale, eps, ALU.mult, ALU.add))
                pool.tensor_tensor(RZ[:, k, :], RZ[:, k, :], MH[:, :], ALU.pow).then_inc(done, 1)

            def scatter(b, t):
                r = b % 2
                for k in range(2):
                    pool.indirect_dma_start(out=slots_d.ap(), out_offset=bass.IndirectOffsetOnAxis(ap=IDX[r][:, k, t:t + 1], axis=0),
                                            in_=XB[r][:, t, k, :], in_offset=None).then_inc(scattered[r], 16)

            for m in range(2):
                third(0, m)
            far_values(0)
            pool.wait_ge(tab_rdy, 1)
            for b in range(NB + 2):
                at = POOL_AT[b >= NB]
                for n in range(NU):
                    g, u = divmod(n, UNITS)
                    if b < NB and u in (1, 3):
                        pool.wait_ge(exp_done, NU * b + n + 1)
                        if u == 1:
                            mul_first(pool, g, 1).then_inc(mul_pool, 1)
                        else:
                            for i in mul_mid(pool, g, 1):
                                i.then_inc(mul_pool, 1)
                    if b + 1 < NB:
                        if n == at["far"]:
                            far_values(b + 1)
                        for m in range(2):
                            if n == at[f"third{m}"]:
                                third(b + 1, m)
                    if 1 <= b <= NB:
                        c = b - 1
                        if n == at["yroot"]:
                            pool.wait_ge(ssy_rdy, c + 1)
                            inv_root(0, SSY[:, :], 1.0 / D, RMS_EPS, yroot_rdy)
                        if n == at["aroot"]:
                            pool.wait_ge(a_stat, c + 1)
                            inv_root(1, MVP[:, 0, :, 1], 1.0, LN_EPS, a_rstd)
                        if n == at["xroot"]:
                            pool.wait_ge(x1_stat, c + 1)
                            inv_root(2, MVP[:, 1, :, 1], 1.0, LN_EPS, x1_rstd)
                    if b >= 2:
                        c = b - 2
                        if n == at["sc0"]:
                            pool.wait_ge(xb_rdy, c + 1)
                            pool.iota(XB[c % 2][:, :, :, D + 1].bitcast(I32), pattern=[[P, T], [NTOK, 2]], base=S * c,
                                      channel_multiplier=1).then_inc(dest_rdy, 1)
                            pool.wait_ge(dest_rdy, c + 1)
                            pool.wait_ge(idx_rdy, c + 1)
                            pool.wait_ge(route_w, c + 1)
                        for t in range(T):
                            if n == at[f"sc{t}"]:
                                scatter(c, t)
            def put(s, r):
                pool.wait_ge(ys_rdy, s + 1)
                pool.indirect_dma_start(out=ytok_d.ap(),
                                        out_offset=bass.IndirectOffsetOnAxis(ap=XG[r][:, D + 1:D + 2].bitcast(I32), axis=0),
                                        in_=YS[r], in_offset=None, bounds_check=2 * NTOK - 1, oob_is_err=False
                                        ).then_inc(ys_out[r], 16)

            for s in range(STILES):
                put(s, s % RING)

            for b in range(NB + 1):
                if b < NB:
                    pool.wait_ge(f_stat, b + 1)
                    if b >= 2:
                        pool.wait_ge(f_ln, b - 1)
                    inv_root(b % 2, MVP[:, b % 2, :, 1], 1.0, LN_EPS, f_rstd)
                if b >= 1:
                    c = b - 1
                    pool.wait_ge(f_ln, c + 1)
                    x1 = X[:, T * c:T * (c + 1), :]
                    pool.tensor_tensor(x1, x1, FY[c][:, 0], ALU.add).then_inc(f_out, 1)


_INS = ['L0_attn_x', 'L0_attn_ln1_w', 'L0_attn_Wq', 'L0_attn_Wk', 'L0_attn_Wv', 'L0_attn_rel_bias', 'L0_attn_scale',
        'L0_attn_Wo', 'L0_attn_ln2_w', 'L0_attn_W1', 'L0_attn_W2', 'L0_ffn_router_w', 'L0_ffn_gate_w', 'L0_ffn_up_w',
        'L0_ffn_down_w']


def kernel(**inputs):
    import concourse.bacc as bacc
    from concourse.bass_utils import run_bass_kernel_spmd

    nc = bacc.Bacc("TRN2", target_bir_lowering=False, num_devices=1)
    arrays, args = {}, []
    for name in _INS:
        a = np.ascontiguousarray(inputs[name])
        arrays[f"in_{name}"] = a
        args.append(nc.dram_tensor(f"in_{name}", a.shape, mybir.dt.from_np(a.dtype), kind="ExternalInput").ap())
    x = inputs['L0_attn_x']
    out = nc.dram_tensor("out", x.shape, mybir.dt.from_np(np.dtype(x.dtype)), kind="ExternalOutput")
    block_kernel(nc, *args, out.ap())
    r = run_bass_kernel_spmd(nc, [arrays], core_ids=[0])
    return r.results[0]["out"]
```

```python
from contextlib import ExitStack

import numpy as np
import concourse.bass as bass
from concourse import mybir

ALU = mybir.AluOpType
ACT = mybir.ActivationFunctionType
AX = mybir.AxisListType.X
F32 = mybir.dt.float32
BF16 = mybir.dt.bfloat16
I32 = mybir.dt.int32

P = 128
NEG = -1.0e30
RING = 8
UNITS = 5
GROUPS = 4
NU = UNITS * GROUPS
LN_EPS = 1e-5
RMS_EPS = 1e-6
KQ_EPS = 1e-6
NO_ROW = 1 << 20
RSQRT_SEED = float(0x5F3759DF)


PE_AT = (dict(xt=0, qkv0=2, qkv1=2, qkv2=3, qkv3=5, turn0=12, turn1=13, rx=1, logits=2, vsum=3, o0=4, o1=5, yt=6, wo=7, zt=8, h0=9, h1=10, h2=11, h3=12, ffn_a=14, ffn=14, count=17),
    dict(rx=0, logits=1, vsum=3, count=3, o0=4, o1=5, yt=6, wo=7, zt=8, h0=9, h1=10, h2=11, h3=12, ffn_a=13, ffn=13))
ACT_AT = (dict(xt=0, qkv0=2, qkv1=2, qkv2=3, qkv3=5, part0=12, part1=13, half0=13, half1=13, out0=16, out1=3, rx=1, rexp=8, yt=6, ysq=11, zt=8, h0=9, h1=10, h2=11, h3=12, xb2=7),
    dict(out1=3, rx=0, xb2=1, rexp=3, yt=6, zt=8, ysq=9, h0=9, h1=10, h2=11, h3=12))
DVE_AT = (dict(xa=0, norm0=8, norm1=9, norm2=10, rem0=11, rem1=13, xar=6, top2=2, vsum=2, o0=4, o1=5, wo=6, ffn=14, place=15, ln=15, xb=17),
    dict(top2=2, vsum=2, place=3, tab0=8, tab1=9, o0=4, o1=5, xa=6, wo=7, ffn=14, ln=16, xb=19))
POOL_AT = (dict(far=4, third0=15, third1=15, yroot=12, aroot=15, xroot=18, sc0=21, sc1=21, sc2=23, sc3=24),
    dict(yroot=10, aroot=15, xroot=17, sc0=4, sc1=5, sc2=5, sc3=5))
WEIGHTS_AT = 4
EARLY = 16
EARLY_AT = 15
M1_USES = ("rx", "logits", "vsum", "o0", "o1", "yt", "wo", "zt", "h0", "h1", "h2", "h3", "ffn", "count")
ROUTE_USES = ("rx", "logits", "count")


def bucket_starts(buckets, max_distance):
    exact = buckets // 2
    d = np.arange(1, 4 * max_distance)
    big = exact + (np.log((d / exact).astype(np.float32)) / np.float32(np.log(max_distance / exact))
                   * (buckets - exact)).astype(np.int32)
    of = np.where(d < exact, d, np.minimum(big, buckets - 1))
    return [int(d[np.argmax(of >= r)]) for r in range(exact, buckets)]


def block_kernel(nc, x_d, ln1_d, wq_d, wk_d, wv_d, rel_d, scale_d, wo_d, ln2_d, w1_d, w2_d,
                 router_d, gate_d, up_d, down_d, out_d):
    NB, S, D = x_d.shape
    BUCKETS, H = rel_d.shape
    DH = D // H
    HID = w1_d.shape[1]
    E, I, _ = gate_d.shape
    T = S // P
    NT = NB * T
    NTOK = NB * S
    HC = HID // P
    IC = [(c * P, min(P, I - c * P)) for c in range((I + P - 1) // P)]
    REGION = NTOK + P
    DUMMY = E * REGION
    STILES = (2 * NTOK) // P + E
    ROW = D + 2
    WEXP = 2 * I + len(IC) * P
    starts = bucket_starts(BUCKETS, 128)
    assert (S, D, DH, T, H) == (512, P, 8, 4, 16) and STILES % RING == 0

    slots_d = nc.dram_tensor("slots", [(E * REGION + P), ROW], F32)
    ytok_d = nc.dram_tensor("ytok", [2 * NTOK, D], F32)
    parts_d = nc.dram_tensor("parts", [2, 2, 3, P, S], BF16)
    toe_d = nc.dram_tensor("toe", [H, P, 3 * P], F32)
    cm_d = nc.dram_tensor("cm", [H, P], F32)
    cfar_d = nc.dram_tensor("cfar", [H, 1], F32)

    with ExitStack() as ctx:
        def sb(name, shape, dt=F32):
            return ctx.enter_context(nc.sbuf_tensor(name, shape, dt))

        def sem(name):
            return ctx.enter_context(nc.semaphore(name))

        X = sb("X", [P, NT, D])
        XA = sb("XA", [P, T, D])
        arena = sb("arena", [P, 8192 + 6144 + 4096 + 2048 + 5120])
        KS = arena[:, 0:4096].bitcast(BF16).rearrange("p (h t) -> p h t", h=H)
        QS = arena[:, 4096:8192].bitcast(BF16).rearrange("p (h t) -> p h t", h=H)
        TAB = arena[:, 8192:14336].rearrange("p (h c) -> p h c", h=H)
        V2 = [arena[:, 14336 + 2048 * r:14336 + 2048 * (r + 1)].rearrange("p (t c) -> p t c", t=T) for r in range(2)]
        V2F = [arena[:, 18432 + 1024 * r:18432 + 1024 * (r + 1)].rearrange("p (t c) -> p t c", t=2) for r in range(2)]
        EB = [arena[:, 20480 + 1024 * u:20480 + 1024 * (u + 1)] for u in range(UNITS)]
        WALL = arena[:, 8192:8192 + E * WEXP]
        WG_N = arena[:, 0:E * I].rearrange("p (n c) -> p n c", c=P)
        WU_N = arena[:, E * I:2 * E * I].rearrange("p (n c) -> p n c", c=P)
        WD_N = arena[:, 8192 + E * WEXP:8192 + E * WEXP + E * I].rearrange("p (e i) -> p e i", e=E)
        assert 2 * E * I <= 8192

        WQKV = sb("WQKV", [P, 3 * D])
        WO = sb("WO", [P, D])
        W1 = sb("W1", [P, HID])
        W2 = sb("W2", [P, HC, D])
        RT = sb("RT", [P, E])
        LNW = sb("LNW", [P, 2])
        SCB = sb("SCB", [P, H])
        IDN = sb("IDN", [P, P])
        TRI = sb("TRI", [P, P])
        ONES = sb("ONES", [P, P])
        ST = sb("ST", [P, NT, 6])
        MV = sb("MV", [P, NT, 2])
        RS0 = sb("RS0", [P, NT])
        RR0 = sb("RR0", [P, NT])
        NWA = sb("NWA", [P, P])
        NWB = sb("NWB", [P, P])
        NWC = sb("NWC", [P, P])
        XAR = sb("XAR", [P, T, D])
        XART = sb("XART", [P, S])
        XSUM = sb("XSUM", [P, NB])
        QK = sb("QK", [P, T, 2 * D])
        SQ = sb("SQ", [P, T, 2 * D])
        SS = sb("SS", [P, T * 2 * H])
        RSQ = sb("RSQ", [P, T * 2 * H])
        PF = sb("PF", [P, 2, S])
        PP = sb("PP", [P, 2, 3, S], BF16)
        OS = sb("OS", [P, 2, S])
        RD = sb("RD", [P, T, H])
        YN = sb("YN", [P, T, D])
        YT = sb("YT", [P, S])
        Y = sb("Y", [P, T, D])
        YJ = sb("YJ", [P, T, D])
        VROW = sb("VROW", [1, D])
        ZT = sb("ZT", [P, S])
        H1T = sb("H1T", [P, HC, S])
        A = sb("A", [P, T, D])
        STP = sb("STP", [P, 2, T, 6])
        MVP = sb("MVP", [P, 2, T, 2])
        SSY = sb("SSY", [P, T])
        RZ = sb("RZ", [P, 4, T])
        NM = sb("NM", [P, 2, T])
        MH = sb("MH", [P, T])
        XB = [sb(f"XB{r}", [P, T, 2, ROW]) for r in range(2)]
        XBT = sb("XBT", [P, S])
        LG = sb("LG", [P, T, E])
        LG2 = sb("LG2", [P, T, E])
        OH = sb("OH", [P, 2, T, E])
        EQ = sb("EQ", [P, T, E])
        REV = sb("REV", [P, T, E])
        MX = sb("MX", [P, 4, T])
        EX = sb("EX", [P, T, E + 1])
        MM = sb("MM", [P, T, E])
        TB = sb("TB", [P, T + 1, E])
        POS = sb("POS", [P, T, E])
        PSEL = sb("PSEL", [P, 2, T, E])
        POSF = sb("POSF", [P, 2, T])
        IDX = [sb(f"IDX{r}", [P, 2, T], I32) for r in range(2)]
        PADX = sb("PADX", [P, ROW])
        PADI = sb("PADI", [P, E], I32)
        EROW = sb("EROW", [P, E])
        AE = sb("AE", [P, E + 1])
        NTE = sb("NTE", [P, E], I32)
        NTF = sb("NTF", [P, 4, E])
        SIO = sb("SIO", [P, STILES])
        SRF = sb("SRF", [P, 2, STILES])
        SRI = sb("SRI", [P, 2, STILES], I32)
        rows = EB[UNITS - 1][0:H, :]
        BR, CMR, RB = rows[:, 0:3 * P], rows[:, 3 * P:4 * P], rows[:, 4 * P:4 * P + BUCKETS]
        GM, SCP = rows[:, 5 * P:5 * P + 1], rows[:, 5 * P + 1:5 * P + 2]
        CF = sb("CF", [P, H])
        WRAW = OS[:, :, :].rearrange("p a b -> p (a b)")[:, 0:3 * D]
        W1R = OS[:, :, :].rearrange("p a b -> p (a b)")[:, 3 * D:3 * D + HID]
        SCM = SQ[:, :, :].rearrange("p a b -> p (a b)")[:, 0:2 * (STILES - EARLY) * E].rearrange("p (k s e) -> p k s e", k=2, e=E)
        CMB = H1T[:, :, :].rearrange("p a b -> p (a b)").rearrange("p (h c) -> p h c", h=H)
        XG = [sb(f"XG{r}", [P, ROW]) for r in range(RING)]
        XGT = [XART[:, 0:P], XART[:, P:2 * P]]
        NIC = len(IC)
        CHUNKS = [(P, 0, P * (NIC - 1)), (IC[-1][1], P * (NIC - 1), P * NIC)]
        WSEL = [arena[:, 2 * I * r:2 * I * (r + 1)] for r in range(2)]
        SGB = [PF[:, r, 0:NIC * P] for r in range(2)]
        HTB = [QK[:, 2 * r:2 * r + 2, :].rearrange("p a b -> p (a b)")[:, 0:NIC * P] for r in range(2)]
        YS = [sb(f"YS{r}", [P, D])[:, :] for r in range(RING)]

        SC = ctx.enter_context(nc.psum_tensor("SC", [P, 2, 1024], F32))
        OA = ctx.enter_context(nc.psum_tensor("OA", [P, 2, 512], F32))
        M0 = ctx.enter_context(nc.psum_tensor("M0", [P, 512], F32))
        M1 = ctx.enter_context(nc.psum_tensor("M1", [P, 512], F32))

        x_in = [sem(f"x_in{i}") for i in range(4)]
        w_in = sem("w_in")
        rel_in = sem("rel_in")
        w2_in = sem("w2_in")
        const_rdy = sem("const_rdy")
        wq_rdy = sem("wq_rdy")
        bias_rows = sem("bias_rows")
        bias_dram = sem("bias_dram")
        bias_in = sem("bias_in")
        tab_raw = sem("tab_raw")
        tab_exp = sem("tab_exp")
        tab_rdy = sem("tab_rdy")
        v2_const = sem("v2_const")
        ks_zero = sem("ks_zero")
        xa_rdy = sem("xa_rdy")
        dve_step = sem("dve_step")
        pool_step = sem("pool_step")
        xar_rdy = sem("xar_rdy")
        m0_full, m0_free = sem("m0_full"), sem("m0_free")
        m1_full, m1_free = sem("m1_full"), sem("m1_free")
        v2f_rdy = sem("v2f_rdy")
        ss_rdy = sem("ss_rdy")
        rs_rdy = sem("rs_rdy")
        qk_norm = sem("qk_norm")
        part1_rdy = sem("part1_rdy")
        part2_rdy = sem("part2_rdy")
        part3_rdy = sem("part3_rdy")
        parts_out = sem("parts_out")
        kq_in = [sem("kq_in0"), sem("kq_in1")]
        qk_done = sem("qk_done")
        exp_done = sem("exp_done")
        mul_dve, mul_pool = sem("mul_dve"), sem("mul_pool")
        pv_done = sem("pv_done")
        o_out = sem("o_out")
        yn_rdy = sem("yn_rdy")
        ssy_rdy = sem("ssy_rdy")
        yroot_rdy = sem("yroot_rdy")
        a_stat = sem("a_stat")
        a_rstd = sem("a_rstd")
        x1_stat = sem("x1_stat")
        x1_rstd = sem("x1_rstd")
        xb_rdy = sem("xb_rdy")
        xb2_rdy = sem("xb2_rdy")
        route_d = sem("route_d")
        route_e = sem("route_e")
        route_m = sem("route_m")
        route_w = sem("route_w")
        idx_rdy = sem("idx_rdy")
        dest_rdy = sem("dest_rdy")
        scattered = [sem("scattered0"), sem("scattered1")]
        dummy_out = sem("dummy_out")
        pad_rdy = sem("pad_rdy")
        pad_out = sem("pad_out")
        table_rdy = sem("table_rdy")
        stg_in = [sem("gate_in"), sem("up_in"), sem("down_in")]
        wt_full, wt_free = sem("wt_full"), [sem("wt_free0"), sem("wt_free1")]
        xg_in = [sem(f"xg_in{i}") for i in range(RING)]
        xt_full, xt_rdy = sem("xt_full"), sem("xt_rdy")
        wsel_rdy = sem("wsel_rdy")
        gu_full, sg_rdy, h_rdy = sem("gu_full"), sem("sg_rdy"), sem("h_rdy")
        y_full, ys_rdy = sem("y_full"), sem("ys_rdy")
        ys_out = [sem(f"ys_out{i}") for i in range(RING)]
        yt_in = [sem(f"yt_in{b}") for b in range(NB)]
        f_stat, f_rstd, f_ln = sem("f_stat"), sem("f_rstd"), sem("f_ln")
        f_out = [sem("f_out0"), sem("f_out1")]
        out_done = [sem("out_done0"), sem("out_done1")]

        assert EARLY % RING == 0 and EARLY * P <= 2 * (NTOK - S) - E * (P - 1)

        block = ctx.enter_context(nc.Block())
        x_v = x_d.rearrange("b (i p) d -> p (b i) d", p=P)
        out_v = out_d.rearrange("b (i p) d -> p (b i) d", p=P)

        N_W, N_REL, N_W2 = 5, 3, 4
        HX = NT // 4

        USES0 = 7

        def uses(body):
            return sorted((k for k in M1_USES if (2 <= body <= NB + 1 if k in ROUTE_USES else 1 <= body <= NB)),
                          key=PE_AT[body >= NB].get)

        def use1(body, k):
            return sum(len(uses(c)) for c in range(body)) + uses(body).index(k)

        def drained(body, k):
            return use1(body, k) + 1

        def col(g, j):
            return 8 * (g // 2) + 2 * j + g % 2

        FY = [arena[:, 17152 + 1024 * r:17152 + 1024 * (r + 1)].rearrange("p (k t d) -> p k t d", k=2, t=T) for r in range(NB)]

        blocks = []
        for m in range(2):
            for n in range(E * I // P):
                blocks.append(("gu", m, n))
        for e in range(E):
            for c in range(len(IC)):
                blocks.append(("d", e, c))
        lots = [blocks[i:i + 4] for i in range(0, len(blocks), 4)]
        NWT = len(lots)

        def pieces(kind, a, c):
            if kind == "d":
                return [(IC[c][1], 0, P, a * WEXP + 2 * I + P * c)]
            out, r0 = [], c * P
            while r0 < (c + 1) * P:
                e, i = divmod(r0, I)
                n = min(I - i, (c + 1) * P - r0)
                out.append((P, r0 - c * P, n, e * WEXP + I * a + i))
                r0 += n
            return out

        def copy_lot(copy, i, lot):
            todo = [(dst, SC[0:k, i % 2, P * j + c0:P * j + c0 + n])
                    for j, blk in enumerate(lot) for k, c0, n, at in pieces(*blk)
                    for dst in [WALL[0:k, at:at + n]]]
            for j, (dst, src) in enumerate(todo):
                ins = copy(dst, src)
            ins.then_inc(wt_free[i % 2], 1)

        def mul_first(eng, g, u):
            e = EB[u].rearrange("p (j c) -> p j c", j=2)
            h0 = col(g, 2 * u)
            tab = TAB[:, h0:h0 + 3:2, :].rearrange("p j (a c) -> p j a c", a=3)[:, :, 0:3:2, :]
            v = e[:, :, 0:256].rearrange("p j (a c) -> p j a c", a=2)
            return eng.tensor_tensor(v, v, tab, ALU.mult)

        def mul_mid(eng, g, u):
            e = EB[2 + u].rearrange("p (j c) -> p j c", j=2)
            h0 = col(g, 2 * u)
            a, z = e[:, :, 0:256], e[:, :, 384:512]
            return [eng.tensor_tensor(a, a, TAB[:, h0:h0 + 3:2, P:3 * P], ALU.mult),
                    eng.tensor_tensor(z, z, TAB[:, h0:h0 + 3:2, P:2 * P], ALU.mult)]

        def store(sp, b):
            sp.wait_ge(f_out[b % 2], b // 2 + 1)
            sp.dma_start(out_v[:, T * b:T * (b + 1), :], X[:, T * b:T * (b + 1), :]).then_inc(out_done[b % 2], 16)

        def lots_at(b, n):
            i = 2 * (n - WEIGHTS_AT)
            return [(k, lots[k]) for k in (i, i + 1) if b == NB and 0 <= k < NWT]

        def early_tile(b, n):
            s = n + NU * (b - NB) - EARLY_AT
            return [s] if b >= NB and 0 <= s < EARLY else []

        def weights_offset(eng, s):
            at = slice(s, s + 1) if isinstance(s, int) else bass.ds(s, 1)
            return eng.value_load(SRI[0:1, 1, at], min_val=0, max_val=(E - 1) * WEXP)

        @block.sync
        def _(sp):
            def load_x(i):
                sp.dma_start(X[:, HX * i:HX * (i + 1), :], x_v[:, HX * i:HX * (i + 1), :]).then_inc(x_in[i], 16)

            load_x(0)
            with nc.allow_non_contiguous_dma(reason="small vectors"):
                sp.dma_start(LNW[:, 0:1], ln1_d.rearrange("(h a) -> h a", a=1)).then_inc(w_in, 16)
                sp.dma_start(LNW[:, 1:2], ln2_d.rearrange("(h a) -> h a", a=1)).then_inc(w_in, 16)
                for n, w in enumerate((wq_d, wk_d, wv_d)):
                    sp.dma_start(WRAW[:, n * D:(n + 1) * D], w).then_inc(w_in, 16)
                sp.dma_start(RB[:, :], rel_d.rearrange("r h -> h r")).then_inc(rel_in, 16)
                sp.dma_start(SCP[:, :], scale_d.rearrange("(h a) -> h a", a=1)).then_inc(rel_in, 16)
                sp.dma_start(SCB[:, :], bass.AP(scale_d.tensor, scale_d.offset, [[0, P], [1, H]])).then_inc(rel_in, 16)
                for i in range(1, 4):
                    load_x(i)
                sp.dma_start(W1R, w1_d).then_inc(w2_in, 16)
                sp.dma_start(W2[:, :, :], w2_d.rearrange("(c p) n -> p c n", p=P)).then_inc(w2_in, 16)
                sp.dma_start(RT[:, :], router_d.rearrange("e h -> h e")).then_inc(w2_in, 16)
                sp.dma_start(WO[:, :], wo_d).then_inc(w2_in, 16)
            sp.wait_ge(bias_rows, 1)
            with nc.allow_non_contiguous_dma(reason="broadcasts"):
                sp.dma_start(toe_d.ap(), BR.unsqueeze(1).broadcast_to([H, P, 3 * P])).then_inc(bias_dram, 16)
                sp.dma_start(cm_d.ap(), CMR[:, :]).then_inc(bias_dram, 16)
                sp.dma_start(cfar_d.ap(), BR[:, 3 * P - 1:3 * P]).then_inc(bias_dram, 16)
                sp.wait_ge(bias_dram, 48)
                sp.dma_start(TAB[:, :, P:3 * P], bass.AP(toe_d, P, [[3 * P - 1, P], [3 * P * P, H], [1, 2 * P]])).then_inc(bias_in, 16)
                sp.dma_start(CMB, bass.AP(cm_d, 0, [[0, P], [P, H], [1, P]])).then_inc(bias_in, 16)
                sp.dma_start(CF[:, :], bass.AP(cfar_d, 0, [[0, P], [1, H]])).then_inc(bias_in, 16)
            sp.wait_ge(const_rdy, 1)
            sp.dma_start(slots_d.ap()[DUMMY:DUMMY + P, :], PADX[:, :]).then_inc(dummy_out, 16)

            def stack(b):
                r = b % 2
                for m in range(2):
                    sp.wait_ge(part3_rdy, 2 * b + m + 1)
                    sp.dma_start(parts_d.ap()[r, m].rearrange("c p t -> p c t"), PP[:, m, :, :]).then_inc(parts_out, 16)
                sp.wait_ge(parts_out, 32 * (b + 1))
                if b == 0:
                    sp.wait_ge(ks_zero, 1)
                for half in range(2):
                    hs = slice(8 * half, 8 * half + 8)
                    if b > 0:
                        sp.wait_ge(qk_done, NU * (b - 1) + NU // 2 * (half + 1))
                    for c in range(3):
                        sp.dma_start(KS[24 * c:24 * c + 24, hs, :],
                                     parts_d.ap()[r, 1].rearrange("c (d h) t -> (c d) h t", h=H)[:, hs, :]
                                     ).then_inc(kq_in[half], 16)
                        sp.dma_start(QS[24 * c:24 * c + 24, hs, :],
                                     bass.AP(parts_d, ((2 * r * 3 + c) * P + 8 * half) * S, [[0, 3], [H * S, DH], [1, 8 * S]])
                                     ).then_inc(kq_in[half], 16)

            for b in range(NB):
                stack(b)
            sp.wait_ge(qk_done, NU * NB)
            sp.dma_start(WG_N, gate_d.rearrange("e i h -> (e i) h").rearrange("(n p) h -> p n h", p=P)).then_inc(stg_in[0], 16)
            sp.dma_start(WU_N, up_d.rearrange("e i h -> (e i) h").rearrange("(n p) h -> p n h", p=P)).then_inc(stg_in[1], 16)
            sp.wait_ge(pv_done, 3 * GROUPS * NB)
            sp.dma_start(WD_N, down_d.rearrange("e h i -> h e i")).then_inc(stg_in[2], 16)

            def load(s, r, it):
                at = slice(s, s + 1) if isinstance(s, int) else bass.ds(s, 1)
                row = sp.value_load(SRI[0:1, 0, at], min_val=0, max_val=DUMMY)
                if not isinstance(s, int) or s >= RING:
                    sp.wait_ge(ys_out[r], 16 * it)
                sp.dma_start(XG[r][:, :], slots_d.ap()[bass.ds(row, P), :]).then_inc(xg_in[r], 16)

            sp.wait_ge(table_rdy, 1)
            for r in range(2):
                sp.wait_ge(scattered[r], 16 * (NT - (2 * T if r == (NB - 1) % 2 else 0)))
            for s in range(EARLY):
                load(s, s % RING, s // RING)
            sp.wait_ge(pad_rdy, 1)
            for e in range(E):
                row = sp.value_load(PADI[0:1, e:e + 1], min_val=0, max_val=DUMMY)
                sp.dma_start(slots_d.ap()[bass.ds(row, P), :], PADX[:, :]).then_inc(pad_out, 16)
            sp.wait_ge(table_rdy, 2)
            for r in range(2):
                sp.wait_ge(scattered[r], 16 * NT)
            sp.wait_ge(pad_out, 16 * E)
            sp.wait_ge(dummy_out, 16)
            with sp.Fori(EARLY // RING, STILES // RING) as it:
                for r in range(RING):
                    load(RING * it + r, r, it)

            for r in range(RING):
                sp.wait_ge(ys_out[r], 16 * STILES // RING)
            yt_v = ytok_d.ap().rearrange("(k n p) d -> k p n d", k=2, p=P)
            for b in range(NB):
                for k in range(2):
                    sp.dma_start(FY[b][:, k, :, :], yt_v[k, :, T * b:T * (b + 1), :]).then_inc(yt_in[b], 16)
            for b in range(NB):
                store(sp, b)
            for r in range(2):
                sp.wait_ge(out_done[r], 16 * NB // 2)

        @block.tensor
        def _(pe):
            def take0(b, k):
                if USES0 * b + k > 0:
                    pe.wait_ge(m0_free, USES0 * b + k)

            def take1(body, k):
                if use1(body, k) > 0:
                    pe.wait_ge(m1_free, use1(body, k))

            def turn4(bank, src):
                for t in range(T):
                    mm = pe.transpose(bank[:, P * t:P * (t + 1)], src[:, t, :], IDN[:, :])
                return mm

            def pre_xt(b):
                take0(b, 0)
                pe.wait_ge(xar_rdy, b + 1)
                turn4(M0, XAR).then_inc(m0_full, 1)

            def pre_qkv(b, t):
                take0(b, 1 + t)
                if b == 0 and t == 0:
                    pe.wait_ge(wq_rdy, 1)
                pe.matmul(M0[:, 0:3 * D], XART[:, P * t:P * (t + 1)], WQKV[:, :], start=True, stop=True).then_inc(m0_full, 1)

            def pre_turn(b, m):
                take0(b, 5 + m)
                pe.wait_ge(qk_norm, b + 1)
                for t in range(T):
                    mm = pe.transpose(M0[:, P * t:P * (t + 1)], QK[:, t, D * m:D * (m + 1)], IDN[:, :])
                mm.then_inc(m0_full, 1)

            def scores(b, n):
                g, u = divmod(n, UNITS)
                if NU * b + n >= 2:
                    pe.wait_ge(exp_done, NU * b + n - 1)
                if u == 0 and g % 2 == 0:
                    pe.wait_ge(kq_in[g // 2], 16 * 6 * (b + 1))
                s = SC[:, n % 2, :]
                if u < 2:
                    for i in range(2):
                        h = col(g, 2 * u + i)
                        mm = pe.matmul(s[:, 512 * i:512 * i + 512], KS[:, h, 0:P], QS[:, h, :], start=True, stop=True)
                elif u < 4:
                    for i in range(2):
                        h = col(g, 2 * (u - 2) + i)
                        pe.matmul(s[:, 512 * i:512 * i + 384], KS[:, h, P:2 * P], QS[:, h, P:4 * P], start=True, stop=True)
                        mm = pe.matmul(s[:, 512 * i + 384:512 * i + 512], KS[:, h, 3 * P:4 * P], QS[:, h, 3 * P:4 * P],
                                       start=True, stop=True)
                else:
                    for i in range(4):
                        h = col(g, i)
                        mm = pe.matmul(s[:, 256 * i:256 * i + 256], KS[:, h, 2 * P:3 * P], QS[:, h, 2 * P:4 * P],
                                       start=True, stop=True)
                mm.then_inc(qk_done, 1)

            def pv(b, g, vals, t, q0, n, probs, first=False, last=False):
                for j in range(4):
                    h = col(g, j)
                    mm = pe.matmul(OA[32 * j:32 * j + 32, g // 2, q0:q0 + n], vals[:, t, 32 * h:32 * h + 32], probs(j),
                                   start=first, stop=last, skip_group_check=True)
                return mm

            def pv01(b, g):
                pe.wait_ge(mul_dve, 16 * b + 4 * g + 1)
                pe.wait_ge(mul_pool, 12 * b + 3 * g + 1)
                pe.wait_ge(m0_free, USES0 * b + 5)
                pe.wait_ge(v2f_rdy, b + 1)
                if g % 2 == 0 and b > 0:
                    pe.wait_ge(o_out, 2 * (b - 1) + g // 2 + 1)
                e = lambda q0, n: lambda j: EB[j // 2][:, 512 * (j % 2) + q0:512 * (j % 2) + q0 + n]
                pv(b, g, V2[b % 2], 0, 0, 256, e(0, 256), first=g % 2 == 0)
                pv(b, g, V2F[b % 2], 0, 256, 256, e(256, 256)).then_inc(pv_done, 1)

            def pv23(b, g):
                pe.wait_ge(mul_dve, 16 * b + 4 * g + 3)
                pe.wait_ge(mul_pool, 12 * b + 3 * g + 3)
                e = lambda c, n: lambda j: EB[2 + j // 2][:, 512 * (j % 2) + c:512 * (j % 2) + c + n]
                pv(b, g, V2[b % 2], 1, 128, 256, e(0, 256))
                pv(b, g, V2F[b % 2], 1, 384, 128, e(256, 128))
                pv(b, g, V2[b % 2], 3, 384, 128, e(384, 128)).then_inc(pv_done, 1)

            def pv4(b, g):
                pe.wait_ge(mul_dve, 16 * b + 4 * g + 4)
                e = lambda j: EB[4][:, 256 * j:256 * j + 256]
                pv(b, g, V2[b % 2], 2, 256, 256, e, last=g % 2 == 1).then_inc(pv_done, 1)

            def ffn(body, tiles):
                take1(body, "ffn")
                pe.wait_ge(m1_free, drained(body, "h3"))
                for t in tiles:
                    for c in range(HC):
                        mm = pe.matmul(M1[:, P * t:P * (t + 1)], H1T[:, c, P * t:P * (t + 1)], W2[:, c, :],
                                       start=c == 0, stop=c == HC - 1)
                return mm

            def on_m1(body, k):
                b = body - 2 if k in ROUTE_USES else body - 1
                take1(body, k)
                if k in ("o0", "o1"):
                    pe.wait_ge(o_out, 2 * b + 2)
                    for i in range(2):
                        t = 2 * int(k[1]) + i
                        for bank in range(2):
                            mm = pe.transpose(M1[:, 256 * i + P * bank:256 * i + P * (bank + 1)],
                                              OS[:, bank, P * t:P * (t + 1)], IDN[:, :])
                elif k == "vsum":
                    mm = pe.matmul(M1[0:1, 0:P], XSUM[:, b:b + 1], WQKV[:, 2 * D:3 * D], start=True, stop=True)
                elif k == "yt":
                    pe.wait_ge(yn_rdy, b + 1)
                    mm = turn4(M1, YN)
                elif k == "wo":
                    pe.wait_ge(m1_free, drained(body, "yt"))
                    if b == 0:
                        pe.wait_ge(w2_in, 16 * N_W2)
                    for t in range(T):
                        mm = pe.matmul(M1[:, P * t:P * (t + 1)], YT[:, P * t:P * (t + 1)], WO[:, :], start=True, stop=True)
                elif k == "zt":
                    pe.wait_ge(m1_free, drained(body, "wo"))
                    mm = turn4(M1, Y)
                elif k in ("h0", "h1", "h2", "h3"):
                    c = int(k[1])
                    pe.wait_ge(m1_free, drained(body, "zt"))
                    if b == 0 and c == 0:
                        pe.wait_ge(wq_rdy, 2)
                    mm = pe.matmul(M1[:, :], W1[:, P * c:P * (c + 1)], ZT[:, :], start=True, stop=True)
                elif k == "ffn":
                    mm = ffn(body, range(T // 2, T))
                elif k == "rx":
                    pe.wait_ge(xb_rdy, b + 1)
                    for t in range(T):
                        mm = pe.transpose(M1[:, P * t:P * (t + 1)], XB[b % 2][:, t, 0, 0:D], IDN[:, :])
                elif k == "logits":
                    pe.wait_ge(m1_free, drained(body, "rx"))
                    for t in range(T):
                        mm = pe.matmul(M1[:, E * t:E * (t + 1)], XBT[:, P * t:P * (t + 1)], RT[:, :], start=True, stop=True)
                else:
                    pe.wait_ge(route_m, b + 1)
                    mflat = MM[:, :, :].rearrange("p t e -> p (t e)")
                    pe.matmul(M1[:, 0:T * E], TRI[:, :], mflat, start=True, stop=True)
                    mm = pe.matmul(M1[:, T * E:2 * T * E], ONES[:, :], mflat, start=True, stop=True)
                mm.then_inc(m1_full, 1)

            def weights(n, lot):
                if n == 0:
                    pe.wait_ge(exp_done, NU * NB)
                if n >= 2:
                    pe.wait_ge(wt_free[n % 2], n // 2)
                for i, (kind, a, c) in enumerate(lot):
                    dst = SC[:, n % 2, P * i:P * (i + 1)]
                    pe.wait_ge(stg_in[2 if kind == "d" else a], 16)
                    if kind == "gu":
                        mm = pe.transpose(dst, (WG_N, WU_N)[a][:, c, :], IDN[:, :])
                    else:
                        i0, k = IC[c]
                        mm = pe.transpose(dst[0:k, :], WD_N[:, a, i0:i0 + k], IDN[:, :])
                mm.then_inc(wt_full, 1)

            def xt(s, r, nload):
                pe.wait_ge(xg_in[r % RING], nload)
                pe.wait_ge(xt_rdy, s)
                pe.transpose(M0[:, 0:P], XG[r % RING][:, 0:D], IDN[:, :]).then_inc(xt_full, 1)

            def gu(s, r):
                pe.wait_ge(wsel_rdy, s + 1)
                if isinstance(s, int) and s + 1 in (EARLY, STILES):
                    pe.wait_ge(xt_rdy, s + 1)
                for m in range(2):
                    for c, (i0, n) in enumerate(IC):
                        mm = pe.matmul(SC[0:n, r % 2, 512 * m + P * c:512 * m + P * (c + 1)], WSEL[r % 2][:, I * m + i0:I * m + i0 + n],
                                       XGT[r % 2], start=True, stop=True)
                mm.then_inc(gu_full, 1)

            def down(s, r, off):
                pe.wait_ge(h_rdy, s + 1)
                if not isinstance(s, int) or s >= 1:
                    pe.wait_ge(ys_rdy, s)
                for c, (i0, n) in enumerate(IC):
                    mm = pe.matmul(OA[:, 0, 0:P], HTB[r % 2][0:n, P * c:P * (c + 1)],
                                   WALL[0:n, bass.ds(off + 2 * I + P * c, P)], start=c == 0, stop=c == NIC - 1)
                mm.then_inc(y_full, 1)

            def woff(s):
                return weights_offset(pe, s)

            def step(s, r, it):
                if not isinstance(s, int) or s + 1 not in (EARLY, STILES, STILES + 1):
                    xt(s + 1, r + 1, 16 * (it + 1 + (r + 1) // RING))
                if not isinstance(s, int) or s < STILES:
                    gu(s, r)
                if not isinstance(s, int) or s >= 1:
                    down(s - 1, r + 1, woff(s - 1))

            def early(s):
                if s == 0:
                    pe.wait_ge(table_rdy, 1)
                    pe.wait_ge(m0_free, USES0 * NB)
                    pe.wait_ge(o_out, 2 * NB)
                    for r in range(2):
                        pe.wait_ge(wt_free[r], (NWT + 1 - r) // 2)
                    pe.wait_ge(xg_in[0], 16)
                    pe.transpose(M0[:, 0:P], XG[0][:, 0:D], IDN[:, :]).then_inc(xt_full, 1)
                step(s, s % RING, s // RING)

            pe.wait_ge(const_rdy, 1)
            pre_xt(0)
            for t in range(T):
                pre_qkv(0, t)
            for m in range(2):
                pre_turn(0, m)
            for b in range(NB + 2):
                at = PE_AT[b >= NB]
                for n in range(NU):
                    g, u = divmod(n, UNITS)
                    if b < NB:
                        scores(b, n)
                    before = (b, g - 1) if g else (b - 1, GROUPS - 1)
                    if 0 <= before[0] < NB and (b < NB or before[0] == NB - 1 and b == NB and g == 0):
                        if u == 1:
                            pv23(*before)
                        if u == 2:
                            pv4(*before)
                    if b < NB and u == 4:
                        pv01(b, g)
                    if b + 1 < NB:
                        if n == at["xt"]:
                            pre_xt(b + 1)
                        for t in range(T):
                            if n == at[f"qkv{t}"]:
                                pre_qkv(b + 1, t)
                        for m in range(2):
                            if n == at[f"turn{m}"]:
                                pre_turn(b + 1, m)
                    for k in uses(b):
                        if k == "ffn" and n == at["ffn_a"]:
                            ffn(b, range(T // 2))
                        if n == at[k]:
                            on_m1(b, k)
                    for i, lot in lots_at(b, n):
                        weights(i, lot)
                    for s in early_tile(b, n):
                        early(s)

            pe.wait_ge(table_rdy, 2)
            xt(EARLY, 0, 16 * (EARLY // RING + 1))
            with pe.Fori(EARLY // RING, STILES // RING - 1) as it:
                for r in range(RING):
                    step(RING * it + r, r, it)
            for s in range(STILES - RING, STILES + 1):
                step(s, s % RING, s // RING)

        @block.scalar
        def _(act):
            def exp_unit(b, n):
                u = n % UNITS
                act.wait_ge(qk_done, NU * b + n + 1)
                done = 3 * (GROUPS * b + n // UNITS) + (-2, -2, -1, -1, 0)[u]
                if done > 0:
                    act.wait_ge(pv_done, done)
                act.activation(EB[u], SC[:, n % 2, :], ACT.Exp).then_inc(exp_done, 1)

            def pre_copy(b, k):
                act.wait_ge(m0_full, USES0 * b + k + 1)
                if k == 0:
                    act.activation(XART[:, :], M0[:, :], ACT.Copy, accum_out=XSUM[:, b:b + 1]).then_inc(m0_free, 1)
                    return
                t = k - 1
                if k == 1 and b == 0:
                    act.wait_ge(v2_const, 2)
                if k == 1 and b >= 1:
                    act.wait_ge(ss_rdy, b)
                if k == 1 and b >= 2:
                    act.wait_ge(pv_done, 12 * (b - 1))
                act.activation(QK[:, t, :], M0[:, 0:2 * D], ACT.Copy)
                act.activation(SQ[:, t, :], M0[:, 0:2 * D], ACT.Square)
                v2 = V2[b % 2][:, t, :].rearrange("p (n s) -> p n s", s=64)
                v = M0[:, 2 * D:3 * D].rearrange("p (n a d) -> p n a d", a=2, d=DH)
                act.activation(v2[:, :, 0:8], v[:, :, 0, :], ACT.Copy)
                act.activation(v2[:, :, 48:56], v[:, :, 1, :], ACT.Copy).then_inc(m0_free, 1)

            def first_part(b, m):
                act.wait_ge(m0_full, USES0 * b + 6 + m)
                if b > 0:
                    act.wait_ge(parts_out, 32 * b)
                act.activation(PP[:, m, 0, :], M0[:, :], ACT.Copy).then_inc(part1_rdy, 1)

            def second_part(b, m):
                act.wait_ge(m0_free, USES0 * b + 6 + m)
                act.activation(PP[:, m, 1, :], PF[:, m, :], ACT.Copy).then_inc(part2_rdy, 1)

            def out_bank(b, bank):
                act.wait_ge(pv_done, 12 * b + 6 * (bank + 1))
                if b > 0:
                    act.wait_ge(m1_full, use1(b, "o1") + 1)
                act.activation(OS[:, bank, :], OA[:, bank, :], ACT.Copy).then_inc(o_out, 1)

            def evac(body, k):
                act.wait_ge(m1_full, use1(body, k) + 1)
                dst, func = {"yt": (YT[:, :], ACT.Copy), "zt": (ZT[:, :], ACT.Copy),
                             "rx": (XBT[:, :], ACT.Copy)}.get(k) or (H1T[:, int(k[1]), :], ACT.Relu)
                act.activation(dst, M1[:, :], func).then_inc(m1_free, 1)

            def evac_x(s, r):
                act.wait_ge(xt_full, s + 1)
                act.activation(XGT[r % 2], M0[:, 0:P], ACT.Copy).then_inc(xt_rdy, 1)

            def silu(s, r):
                act.wait_ge(gu_full, s + 1)
                for k, c0, c1 in CHUNKS:
                    ins = act.activation(SGB[r % 2][0:k, c0:c1], SC[0:k, r % 2, c0:c1], ACT.Silu)
                ins.then_inc(sg_rdy, 1)

            def evac_y(s, r):
                act.wait_ge(y_full, s + 1)
                act.activation(YS[r % RING], OA[:, 0, 0:P], ACT.Copy, scale=XG[r % RING][:, D:D + 1]).then_inc(ys_rdy, 1)

            def step(s, r):
                if not isinstance(s, int) or s + 1 not in (EARLY, STILES, STILES + 1):
                    evac_x(s + 1, r + 1)
                if not isinstance(s, int) or s < STILES:
                    silu(s, r)
                if not isinstance(s, int) or s >= 1:
                    evac_y(s - 1, r - 1)

            for k in range(5):
                pre_copy(0, k)
            for m in range(2):
                first_part(0, m)
                second_part(0, m)
            act.wait_ge(bias_in, 48)
            act.activation(CF[:, :], CF[:, :], ACT.Exp).then_inc(tab_exp, 1)
            act.wait_ge(tab_raw, 1)
            act.activation(TAB, TAB, ACT.Exp).then_inc(tab_exp, 1)
            for b in range(NB + 2):
                at = ACT_AT[b >= NB]
                for n in range(NU):
                    if b < NB:
                        exp_unit(b, n)
                    if b + 1 < NB:
                        for k, name in enumerate(("xt", "qkv0", "qkv1", "qkv2", "qkv3")):
                            if n == at[name]:
                                pre_copy(b + 1, k)
                        for m in range(2):
                            if n == at[f"part{m}"]:
                                first_part(b + 1, m)
                        for m in range(2):
                            if n == at[f"half{m}"]:
                                second_part(b + 1, m)
                    if b < NB and n == at["out0"]:
                        out_bank(b, 0)
                    if n == at["out1"] and 1 <= b <= NB:
                        out_bank(b - 1, 1)
                    if n == at["ysq"] and 1 <= b <= NB:
                        act.wait_ge(m1_free, drained(b, "wo"))
                        if b >= 2:
                            act.wait_ge(yroot_rdy, b - 1)
                        for t in range(T):
                            ins = act.activation(YJ[:, t, :], Y[:, t, :], ACT.Square, accum_out=SSY[:, t:t + 1])
                        ins.then_inc(ssy_rdy, 1)
                    for k in uses(b):
                        if k in at and n == at[k]:
                            evac(b, k)
                    if b >= 2 and n == at["xb2"]:
                        act.wait_ge(xb_rdy, b - 1)
                        x2 = XB[b % 2]
                        act.activation(x2[:, :, 1, 0:D], x2[:, :, 0, 0:D], ACT.Copy).then_inc(xb2_rdy, 1)
                    if b >= 2 and n == at["rexp"]:
                        act.wait_ge(route_d, b - 1)
                        act.activation(EX[:, :, :], EX[:, :, :], ACT.Exp).then_inc(route_e, 1)
                    for i, lot in lots_at(b, n):
                        if i % 2 == 0:
                            act.wait_ge(wt_full, i + 1)
                            act.wait_ge(pv_done, 3 * GROUPS * NB)
                            copy_lot(act.copy, i, lot)
                    for s in early_tile(b, n):
                        if s == 0:
                            evac_x(0, 0)
                        step(s, s % RING)

            evac_x(EARLY, 0)
            with act.Fori(EARLY // RING, STILES // RING - 1) as it:
                for r in range(RING):
                    step(RING * it + r, r)
            for s in range(STILES - RING, STILES + 1):
                step(s, s % RING)

            for b in range(NB):
                act.wait_ge(f_rstd, b + 1)
                for t in range(T):
                    y = FY[b][:, 0, t, :]
                    ins = act.activation(y, y, ACT.Identity, bias=NM[:, b % 2, t:t + 1], scale=RZ[:, b % 2, t:t + 1])
                ins.then_inc(f_ln, 1)

        @block.vector
        def _(dve):
            steps = [0]

            def link(ins):
                steps[0] += 1
                ins.then_inc(dve_step, 1)
                dve.wait_ge(dve_step, steps[0])

            def rsqrt(y, a, u):
                link(dve.tensor_scalar(y.bitcast(I32), a.bitcast(I32), 1, None, ALU.logical_shift_right))
                link(dve.tensor_scalar(y.bitcast(I32), y.bitcast(I32), -1.0, RSQRT_SEED, ALU.mult, ALU.add))
                for _ in range(3):
                    link(dve.tensor_tensor(u, y, y, ALU.mult))
                    link(dve.scalar_tensor_tensor(u, u, -0.5, a, ALU.mult, ALU.mult))
                    link(dve.scalar_tensor_tensor(y, u, 1.5, y, ALU.add, ALU.mult))

            def bc(ap, shape):
                return ap.unsqueeze(len(shape) - 1).broadcast_to(shape)

            def statistics(i0, n):
                for i in range(i0, i0 + n):
                    last = dve.bn_stats(ST[:, i, :], X[:, i, :])
                link(last)
                for i in range(i0, i0 + n):
                    last = dve.bn_aggr(MV[:, i, :], ST[:, i, :])
                link(last)
                a, u, w = NWA[:, 0:n], NWB[:, 0:n], NWC[:, 0:n]
                var, rs = MV[:, i0:i0 + n, 1], RS0[:, i0:i0 + n]
                link(dve.tensor_scalar(a, var, LN_EPS, None, ALU.add))
                rsqrt(rs, a, u)
                link(dve.tensor_tensor(w, rs, rs, ALU.mult))
                link(dve.tensor_tensor(w, w, var, ALU.mult))
                link(dve.tensor_scalar(a, w, RMS_EPS, None, ALU.add))
                rsqrt(w, a, u)
                link(dve.tensor_tensor(RR0[:, i0:i0 + n], w, rs, ALU.mult))

            def xar(b):
                if b > 0:
                    dve.wait_ge(m0_full, USES0 * (b - 1) + 1)
                for t in range(T):
                    i = T * b + t
                    last = dve.tensor_scalar(XAR[:, t, :], X[:, i, :], MV[:, i, 0:1], RR0[:, i:i + 1], ALU.subtract, ALU.mult)
                last.then_inc(xar_rdy, 1)

            def xa(b):
                if b > 0:
                    dve.wait_ge(m1_free, drained(b, "wo"))
                for t in range(T):
                    i = T * b + t
                    last = dve.tensor_scalar(XA[:, t, :], X[:, i, :], MV[:, i, 0:1], RS0[:, i:i + 1], ALU.subtract, ALU.mult)
                last.then_inc(xa_rdy, 1)

            dve.wait_ge(x_in[0], 16)
            statistics(0, T)
            xar(0)
            dve.wait_ge(w_in, 16 * N_W)
            for m in range(2):
                dve.tensor_scalar(WQKV[:, D * m:D * (m + 1)].rearrange("p (d h) -> p h d", h=H),
                                  WRAW[:, D * m:D * (m + 1)].rearrange("p (h d) -> p h d", h=H), LNW[:, 0:1], None, ALU.mult)
            dve.tensor_scalar(WQKV[:, 2 * D:3 * D], WRAW[:, 2 * D:3 * D], LNW[:, 0:1], None, ALU.mult).then_inc(wq_rdy, 1)
            dve.wait_ge(rel_in, 16 * N_REL)
            link(dve.tensor_scalar(RB[:, :], RB[:, :], SCP[:, 0:1], None, ALU.mult))
            dve.memset(BR[:, 0:P + 1], NEG)
            exact = BUCKETS // 2
            dve.tensor_copy(BR[:, P + 1:P + exact], RB[:, 1:exact])
            ends = starts[1:] + [2 * P]
            for r in range(exact, BUCKETS):
                a, z = starts[r - exact], ends[r - exact]
                last = dve.tensor_copy(BR[:, P + a:P + z], RB[:, r:r + 1].broadcast_to([H, z - a]))
            link(last)
            link(dve.tensor_reduce(GM[:, :], BR[:, P + 1:3 * P], AX, ALU.max))
            link(dve.tensor_scalar(BR[:, P + 1:3 * P], BR[:, P + 1:3 * P], GM[:, 0:1], None, ALU.subtract))
            dve.memset(CMR[:, 0:1], 0.0)
            dve.tensor_tensor_scan(CMR[:, 1:P], BR[:, P + 1:2 * P], BR[:, P + 1:2 * P], NEG, ALU.max, ALU.max
                                   ).then_inc(bias_rows, 1)

            def norm_sums(b):
                dve.wait_ge(m0_free, USES0 * b + 5)
                link(dve.tensor_reduce(SS[:, :].rearrange("p (g h) -> p g h", h=H),
                                       SQ[:, :, :].rearrange("p t c -> p (t c)").rearrange("p (g d h) -> p g h d", d=DH, h=H), AX, ALU.add))
                dve.tensor_scalar(SS[:, :], SS[:, :], KQ_EPS, None, ALU.add).then_inc(ss_rdy, 1)

            def norm_roots(b):
                dve.wait_ge(ss_rdy, b + 1)
                rsqrt(RSQ[:, :], SS[:, :], NWA[:, :])
                rs = RSQ[:, :].rearrange("p (t m h) -> p t m h", t=T, m=2)
                dve.tensor_tensor(rs[:, :, 0, :], rs[:, :, 0, :], SCB[:, :].unsqueeze(1).broadcast_to([P, T, H]), ALU.mult
                                  ).then_inc(rs_rdy, 1)

            def norm_apply(b):
                dve.wait_ge(rs_rdy, b + 1)
                rs = RSQ[:, :].rearrange("p (t m h) -> p t m h", t=T, m=2)
                for t in range(T):
                    v = QK[:, t, :].rearrange("p (m d h) -> p m d h", m=2, h=H)
                    last = dve.tensor_tensor(v, v, rs[:, t].unsqueeze(2).broadcast_to([P, 2, DH, H]), ALU.mult)
                last.then_inc(qk_norm, 1)

            def remainder(b, m):
                dve.wait_ge(part1_rdy, 2 * b + m + 1)
                if b > 0:
                    dve.wait_ge(part3_rdy, 2 * (b - 1) + m + 1)
                dve.tensor_tensor(PF[:, m, :], M0[:, :], PP[:, m, 0, :], ALU.subtract).then_inc(m0_free, 1)

            def mul(b, n):
                g, u = divmod(n, UNITS)
                heads = slice(col(g, 0), col(g, 3) + 1, 2)
                if u == 0:
                    mul_first(dve, g, 0).then_inc(mul_dve, 1)
                elif u == 2:
                    for i in mul_mid(dve, g, 0):
                        i.then_inc(mul_dve, 1)
                elif u == 4:
                    e = EB[4].rearrange("p (j c) -> p j c", j=4)
                    dve.tensor_tensor(e, e, TAB[:, heads, P:3 * P], ALU.mult).then_inc(mul_dve, 1)

            def post(body, k):
                b = body - 1
                dve.wait_ge(m1_full, use1(body, k) + 1)
                if k in ("o0", "o1"):
                    t0 = 2 * int(k[1])
                    v = M1[:, :].rearrange("p (t n c) -> p t n c", t=2, c=16)
                    link(dve.reciprocal(RD[:, t0:t0 + 2, :], v[:, :, :, DH]))
                    for i in range(2):
                        last = dve.tensor_tensor(YN[:, t0 + i, :].rearrange("p (n d) -> p n d", d=DH), v[:, i, :, 0:DH],
                                                 RD[:, t0 + i, :].unsqueeze(2).broadcast_to([P, H, DH]), ALU.mult)
                    last.then_inc(m1_free, 1)
                    if k == "o1":
                        dve.wait_ge(m1_free, use1(body, k) + 1)
                        dve.tensor_copy(YN[0:1, 0, :], VROW[0:1, :]).then_inc(yn_rdy, 1)
                elif k == "vsum":
                    dve.tensor_scalar(VROW[0:1, :], M1[0:1, 0:P], 1.0 / S, None, ALU.mult).then_inc(m1_free, 1)
                    dve.wait_ge(m1_free, use1(body, k) + 1)
                elif k == "wo":
                    dve.wait_ge(xa_rdy, b + 1)
                    dve.tensor_tensor(Y[:, :, :].rearrange("p t d -> p (t d)"), M1[:, :],
                                      XA[:, :, :].rearrange("p t d -> p (t d)"), ALU.add).then_inc(m1_free, 1)
                elif k == "ffn":
                    dve.wait_ge(yroot_rdy, b + 1)
                    for t in range(T):
                        last = dve.scalar_tensor_tensor(A[:, t, :], M1[:, P * t:P * (t + 1)], RZ[:, 0, t:t + 1], Y[:, t, :],
                                                        ALU.mult, ALU.add)
                    last.then_inc(m1_free, 1)
                    dve.wait_ge(m1_free, use1(body, k) + 1)

            def stats(src, r, done):
                for t in range(T):
                    last = dve.bn_stats(STP[:, r, t, :], src[:, t, :])
                link(last)
                for t in range(T):
                    last = dve.bn_aggr(MVP[:, r, t, :], STP[:, r, t, :])
                last.then_inc(done, 1)

            def top2(b):
                dve.wait_ge(m1_full, use1(b + 2, "logits") + 1)
                dve.tensor_copy(LG[:, :, :].rearrange("p t e -> p (t e)"), M1[:, 0:T * E]).then_inc(m1_free, 1)
                dve.wait_ge(m1_free, use1(b + 2, "logits") + 1)
                lg = LG
                for k in range(2):
                    link(dve.tensor_reduce(MX[:, k, :], lg[:, :, :], AX, ALU.max))
                    link(dve.tensor_tensor(EQ[:, :, :], lg[:, :, :], bc(MX[:, k, :], [P, T, E]), ALU.is_equal))
                    link(dve.tensor_tensor(EQ[:, :, :], EQ[:, :, :], REV[:, :, :], ALU.mult))
                    link(dve.tensor_reduce(MX[:, 2, :], EQ[:, :, :], AX, ALU.max))
                    link(dve.tensor_tensor(OH[:, k], EQ[:, :, :], bc(MX[:, 2, :], [P, T, E]), ALU.is_equal))
                    if k == 0:
                        link(dve.scalar_tensor_tensor(LG2[:, :, :], OH[:, 0], NEG, LG[:, :, :], ALU.mult, ALU.add))
                        lg = LG2
                dve.tensor_tensor(MM[:, :, :], OH[:, 0], OH[:, 1], ALU.add).then_inc(route_m, 1)
                dve.tensor_tensor(EX[:, :, 0:E], LG[:, :, :], bc(MX[:, 0, :], [P, T, E]), ALU.subtract)
                dve.tensor_tensor(EX[:, :, E], MX[:, 1, :], MX[:, 0, :], ALU.subtract).then_inc(route_d, 1)

            def place(b):
                r = b % 2
                dve.wait_ge(route_e, b + 1)
                link(dve.tensor_reduce(MX[:, 2, :], EX[:, :, 0:E], AX, ALU.add))
                link(dve.reciprocal(MX[:, 3, :], MX[:, 2, :]))
                dve.tensor_copy(XB[r][:, :, 0, D], MX[:, 3, :])
                dve.tensor_tensor(XB[r][:, :, 1, D], MX[:, 3, :], EX[:, :, E], ALU.mult).then_inc(route_w, 1)
                dve.wait_ge(m1_full, use1(b + 2, "count") + 1)
                for t in range(T):
                    link(dve.tensor_tensor(TB[:, t + 1, :], TB[:, t, :], M1[:, E * (T + t):E * (T + t + 1)], ALU.add))
                link(dve.tensor_tensor(POS[:, :, :], M1[:, 0:T * E].rearrange("p (t e) -> p t e", t=T), TB[:, 0:T, :], ALU.add))
                for k in range(2):
                    last = dve.tensor_tensor(PSEL[:, k], OH[:, k], POS[:, :, :], ALU.mult)
                last.then_inc(m1_free, 1)
                dve.wait_ge(m1_free, use1(b + 2, "count") + 1)
                dve.tensor_copy(TB[:, 0, :], TB[:, T, :])
                link(dve.tensor_reduce(POSF[:, :, :], PSEL[:, :, :, :], AX, ALU.add))
                if b >= 2:
                    dve.wait_ge(scattered[r], 16 * 2 * T * (b // 2))
                dve.tensor_copy(IDX[r][:, :, :], POSF[:, :, :]).then_inc(idx_rdy, 1)
                dve.wait_ge(idx_rdy, b + 1)

            def expert_tiles(last):
                link(dve.tensor_tensor(NTF[:, 0, :], TB[:, T, :], EROW[:, :], ALU.subtract))
                link(dve.tensor_scalar(NTE[:, :], NTF[:, 0, :], float(P - 1) if last else 0.0, None, ALU.add))
                link(dve.tensor_scalar(NTE[:, :], NTE[:, :], 7, None, ALU.logical_shift_right))
                link(dve.tensor_copy(NTF[:, 0, :], NTE[:, :]))
                link(dve.tensor_tensor(NTF[:, 0, :], NTF[:, 0, :], AE[:, 0:E], ALU.subtract))
                dve.tensor_tensor_scan(NTF[:, 1, :], ONES[:, 0:E], NTF[:, 0, :], 0.0, ALU.mult, ALU.add)
                link(dve.tensor_tensor(NTF[:, 2, :], AE[:, 1:E + 1], AE[:, 0:E], ALU.subtract))
                link(dve.tensor_tensor(NTF[:, 2, :], NTF[:, 2, :], NTF[:, 0, :], ALU.subtract))
                dve.tensor_scalar(NTF[:, 3, 0:1], AE[:, 0:1], float(P), None, ALU.mult)
                link(dve.tensor_scalar(NTF[:, 2, :], NTF[:, 2, :], float(P), float(REGION), ALU.mult, ALU.add))

            def slot_table(s0, n):
                sh = [P, n, E]
                past, up = SCM[:, 0, 0:n], SCM[:, 1, 0:n]
                link(dve.tensor_tensor(past, SIO[:, 0:n].unsqueeze(2).broadcast_to(sh),
                                       NTF[:, 1, :].unsqueeze(1).broadcast_to(sh), ALU.is_ge))
                link(dve.tensor_tensor(up, past, NTF[:, 2, :].unsqueeze(1).broadcast_to(sh), ALU.mult))
                row, exp = SRF[:, 0, s0:s0 + n], SRF[:, 1, s0:s0 + n]
                dve.tensor_reduce(row, up, AX, ALU.add)
                link(dve.tensor_reduce(exp, past, AX, ALU.add))
                link(dve.scalar_tensor_tensor(row, SIO[:, 0:n], float(P), row, ALU.mult, ALU.add))
                link(dve.tensor_scalar(row, row, NTF[:, 3, 0:1], None, ALU.add))
                dve.tensor_scalar(SRI[:, 0, s0:s0 + n], row, float(DUMMY), None, ALU.min)
                dve.tensor_scalar(SRI[:, 1, s0:s0 + n], exp, float(E - 1), float(WEXP), ALU.min, ALU.mult).then_inc(table_rdy, 1)

            def early_counts():
                link(dve.tensor_scalar(NTF[:, 1, :], NTF[:, 1, :], float(EARLY), None, ALU.min))
                dve.tensor_copy(AE[:, 0:1], NTF[:, 1, 0:1])
                link(dve.tensor_tensor(AE[:, 1:E], NTF[:, 1, 1:E], NTF[:, 1, 0:E - 1], ALU.subtract))

            def hidden(s, r):
                dve.wait_ge(sg_rdy, s + 1)
                for k, c0, c1 in CHUNKS:
                    ins = dve.tensor_tensor(HTB[r % 2][0:k, c0:c1], SGB[r % 2][0:k, c0:c1], SC[0:k, r % 2, 512 + c0:512 + c1],
                                            ALU.mult)
                ins.then_inc(h_rdy, 1)

            def select(s, r):
                dve.tensor_copy(WSEL[r % 2], WALL[:, bass.ds(weights_offset(dve, s), 2 * I)]).then_inc(wsel_rdy, 1)

            def step(s, r):
                if not isinstance(s, int) or s + 1 not in (EARLY, STILES):
                    select(s + 1, r + 1)
                hidden(s, r)

            dve.memset(AE[:, :], 0.0)
            norm_sums(0)
            norm_roots(0)
            norm_apply(0)
            for m in range(2):
                remainder(0, m)
            dve.wait_ge(bias_in, 48)
            dve.tensor_tensor(TAB[:, :, 0:P], TAB[:, :, P:2 * P], CMB, ALU.subtract).then_inc(tab_raw, 1)
            statistics(T, HX - T)
            xar(1)
            dve.wait_ge(tab_exp, 2)
            dve.memset(TAB[0:1, :, 0:1], 1.0).then_inc(tab_rdy, 1)
            dve.wait_ge(tab_rdy, 1)
            dve.wait_ge(w2_in, 16 * N_W2)
            dve.tensor_scalar(W1[:, :], W1R, LNW[:, 1:2], None, ALU.mult).then_inc(wq_rdy, 1)
            dve.wait_ge(const_rdy, 1)
            dve.tensor_copy(TB[:, 0, :], EROW[:, :])
            for b in range(NB + 2):
                at = DVE_AT[b >= NB]
                for n in range(NU):
                    if b < NB and n % UNITS in (0, 2, 4):
                        dve.wait_ge(exp_done, NU * b + n + 1)
                        mul(b, n)
                    if b + 1 < NB:
                        if n == at["norm0"]:
                            norm_sums(b + 1)
                        if n == at["norm1"]:
                            norm_roots(b + 1)
                        if n == at["norm2"]:
                            norm_apply(b + 1)
                        for m in range(2):
                            if n == at[f"rem{m}"]:
                                remainder(b + 1, m)
                    if b < NB and n == at["xar"]:
                        if b % 2 == 0 and b + 2 < NB:
                            dve.wait_ge(x_in[(b + 2) // 2], 16)
                            statistics(T * (b + 2), HX)
                        if b + 2 < NB:
                            xar(b + 2)
                    if b >= 2:
                        if n == at["top2"]:
                            top2(b - 2)
                        if n == at["place"]:
                            place(b - 2)
                            if b == NB + 1:
                                dve.tensor_copy(PADI[:, :], TB[:, T, :]).then_inc(pad_rdy, 1)
                    if b >= NB and n == at["tab0"]:
                        expert_tiles(b > NB)
                    if b >= NB and n == at["tab1"]:
                        if b == NB:
                            slot_table(0, EARLY)
                            early_counts()
                        else:
                            slot_table(EARLY, STILES - EARLY)
                    if 1 <= b <= NB:
                        c = b - 1
                        if n == at["xa"]:
                            xa(c)
                        for k in ("vsum", "o0", "o1", "wo"):
                            if n == at[k]:
                                post(b, k)
                        if n == at["ffn"]:
                            post(b, "ffn")
                            stats(A, 0, a_stat)
                        if n == at["ln"]:
                            dve.wait_ge(a_rstd, c + 1)
                            for t in range(T):
                                last = dve.tensor_scalar(A[:, t, :], A[:, t, :], MVP[:, 0, t, 0:1], RZ[:, 1, t:t + 1],
                                                         ALU.subtract, ALU.mult)
                            link(last)
                            x1 = X[:, T * c:T * (c + 1), :]
                            link(dve.tensor_tensor(x1, x1, A[:, :, :], ALU.add))
                            stats(x1, 1, x1_stat)
                        if n == at["xb"]:
                            dve.wait_ge(x1_rstd, c + 1)
                            if c >= 2:
                                dve.wait_ge(scattered[c % 2], 16 * 2 * T * (c // 2))
                            for t in range(T):
                                last = dve.tensor_scalar(XB[c % 2][:, t, 0, 0:D], X[:, T * c + t, :], MVP[:, 1, t, 0:1],
                                                         RZ[:, 2, t:t + 1], ALU.subtract, ALU.mult)
                            last.then_inc(xb_rdy, 1)
                    for i, lot in lots_at(b, n):
                        if i % 2 == 1:
                            dve.wait_ge(wt_full, i + 1)
                            dve.wait_ge(pv_done, 3 * GROUPS * NB)
                            copy_lot(dve.tensor_copy, i, lot)
                    for s in early_tile(b, n):
                        if s == 0:
                            for i in range(2):
                                dve.wait_ge(wt_free[i], (NWT + 1 - i) // 2)
                            dve.wait_ge(table_rdy, 1)
                            select(0, 0)
                        step(s, s % RING)

            dve.wait_ge(table_rdy, 2)
            select(EARLY, 0)
            with dve.Fori(EARLY // RING, STILES // RING - 1) as it:
                for r in range(RING):
                    step(RING * it + r, r)
            for s in range(STILES - RING, STILES):
                step(s, s % RING)

            for b in range(NB + 2):
                if b < NB:
                    dve.wait_ge(yt_in[b], 32)
                    link(dve.tensor_tensor(FY[b][:, 0], FY[b][:, 0], FY[b][:, 1], ALU.add))
                    if b >= 2:
                        dve.wait_ge(f_rstd, b - 1)
                    stats(FY[b][:, 0], b % 2, f_stat)
                if b >= 2 and b % 2 == 0:
                    c = b - 2
                    dve.wait_ge(f_ln, c + 1)
                    x1 = X[:, T * c:T * (c + 1), :]
                    dve.tensor_tensor(x1, x1, FY[c][:, 0], ALU.add).then_inc(f_out[0], 1)

        @block.gpsimd
        def _(pool):
            steps = [0]

            def link(ins):
                steps[0] += 1
                ins.then_inc(pool_step, 1)
                pool.wait_ge(pool_step, steps[0])

            pool.memset(IDN[:, :], 0.0)
            pool.memset(TRI[:, :], 1.0)
            pool.memset(ONES[:, :], 1.0)
            pool.memset(MH[:, :], -0.5)
            pool.memset(PADX[:, :], 0.0)
            pool.iota(EROW[:, :], pattern=[[REGION, E]], base=0, channel_multiplier=0, allow_small_or_imprecise_dtypes=True)
            pool.iota(REV[:, :, :], pattern=[[0, T], [-1, E]], base=E, channel_multiplier=0, allow_small_or_imprecise_dtypes=True)
            link(pool.iota(SIO[:, :], pattern=[[1, STILES]], base=0, channel_multiplier=0, allow_small_or_imprecise_dtypes=True))
            pool.affine_select(out=IDN[:, :], in_=IDN[:, :], compare_op=ALU.not_equal, fill=1.0, base=0,
                               pattern=[[-1, P]], channel_multiplier=1)
            pool.affine_select(out=TRI[:, :], in_=TRI[:, :], compare_op=ALU.is_gt, fill=0.0, base=0,
                               pattern=[[1, P]], channel_multiplier=-1)
            pool.iota(PADX[:, D + 1:D + 2].bitcast(I32), pattern=[[0, 1]], base=NO_ROW, channel_multiplier=0).then_inc(const_rdy, 1)
            for r in range(2):
                link(pool.memset(V2[r][:, :, :], 0.0))
                v = V2[r].rearrange("p t (n s) -> p t n s", s=64)
                pool.memset(v[:, :, :, 8:16], 1.0)
                pool.memset(v[:, :, :, 56:64], 1.0).then_inc(v2_const, 1)
            pool.wait_ge(v2_const, 2)
            pool.memset(arena[64:P, 0:4096], 0.0)
            pool.memset(arena[64:P, 4096:8192], 0.0).then_inc(ks_zero, 1)
            pool.wait_ge(ks_zero, 1)

            def far_values(b):
                pool.wait_ge(m0_free, USES0 * b + 5)
                if b == 0:
                    pool.wait_ge(tab_exp, 1)
                if b >= 2:
                    pool.wait_ge(pv_done, 12 * (b - 1))
                for t in range(2):
                    last = pool.tensor_tensor(V2F[b % 2][:, t, :].rearrange("p (h s) -> p h s", h=H),
                                              V2[b % 2][:, t, :].rearrange("p (h s) -> p h s", h=H),
                                              CF[:, :].unsqueeze(2).broadcast_to([P, H, 32]), ALU.mult)
                last.then_inc(v2f_rdy, 1)

            def third(b, m):
                pool.wait_ge(part2_rdy, 2 * b + m + 1)
                pool.tensor_tensor(PP[:, m, 2, :], PF[:, m, :], PP[:, m, 1, :], ALU.subtract).then_inc(part3_rdy, 1)

            def inv_root(k, src, scale, eps, done):
                link(pool.tensor_scalar(RZ[:, k, :], src, scale, eps, ALU.mult, ALU.add))
                pool.tensor_tensor(RZ[:, k, :], RZ[:, k, :], MH[:, :], ALU.pow).then_inc(done, 1)

            def scatter(b, t):
                r = b % 2
                if t == 0:
                    pool.wait_ge(xb2_rdy, b + 1)
                    pool.wait_ge(xb_rdy, b + 1)
                    pool.iota(XB[r][:, :, :, D + 1].bitcast(I32), pattern=[[P, T], [NTOK, 2]], base=S * b,
                              channel_multiplier=1).then_inc(dest_rdy, 1)
                    pool.wait_ge(dest_rdy, b + 1)
                    pool.wait_ge(idx_rdy, b + 1)
                    pool.wait_ge(route_w, b + 1)
                for k in range(2):
                    pool.indirect_dma_start(out=slots_d.ap(), out_offset=bass.IndirectOffsetOnAxis(ap=IDX[r][:, k, t:t + 1], axis=0),
                                            in_=XB[r][:, t, k, :], in_offset=None).then_inc(scattered[r], 16)

            def put(s, r):
                pool.wait_ge(ys_rdy, s + 1)
                pool.indirect_dma_start(out=ytok_d.ap(),
                                        out_offset=bass.IndirectOffsetOnAxis(ap=XG[r][:, D + 1:D + 2].bitcast(I32), axis=0),
                                        in_=YS[r], in_offset=None, bounds_check=2 * NTOK - 1, oob_is_err=False
                                        ).then_inc(ys_out[r], 16)

            for m in range(2):
                third(0, m)
            far_values(0)
            pool.wait_ge(tab_rdy, 1)
            for b in range(NB + 2):
                at = POOL_AT[b >= NB]
                for n in range(NU):
                    g, u = divmod(n, UNITS)
                    if b < NB and u in (1, 3):
                        pool.wait_ge(exp_done, NU * b + n + 1)
                        if u == 1:
                            mul_first(pool, g, 1).then_inc(mul_pool, 1)
                        else:
                            for i in mul_mid(pool, g, 1):
                                i.then_inc(mul_pool, 1)
                    if b + 1 < NB:
                        if n == at["far"]:
                            far_values(b + 1)
                        for m in range(2):
                            if n == at[f"third{m}"]:
                                third(b + 1, m)
                    if 1 <= b <= NB:
                        c = b - 1
                        if n == at["yroot"]:
                            pool.wait_ge(ssy_rdy, c + 1)
                            inv_root(0, SSY[:, :], 1.0 / D, RMS_EPS, yroot_rdy)
                        if n == at["aroot"]:
                            pool.wait_ge(a_stat, c + 1)
                            inv_root(1, MVP[:, 0, :, 1], 1.0, LN_EPS, a_rstd)
                        if n == at["xroot"]:
                            pool.wait_ge(x1_stat, c + 1)
                            inv_root(2, MVP[:, 1, :, 1], 1.0, LN_EPS, x1_rstd)
                    for body in (b - 1, b):
                        for t in range(T):
                            if body >= 2 and n + NU * (b - body) == POOL_AT[body >= NB][f"sc{t}"]:
                                scatter(body - 2, t)
                    for s in early_tile(b, n):
                        if s >= 1:
                            put(s - 1, (s - 1) % RING)

            for s in range(EARLY - 1, STILES):
                put(s, s % RING)

            for b in range(NB + 1):
                if b < NB:
                    r = b % 2
                    pool.wait_ge(f_stat, b + 1)
                    if b >= 2:
                        pool.wait_ge(f_ln, b - 1)
                    link(pool.tensor_scalar(RZ[:, r, :], MVP[:, r, :, 1], 1.0, LN_EPS, ALU.mult, ALU.add))
                    pool.tensor_scalar(NM[:, r, :], MVP[:, r, :, 0], -1.0, None, ALU.mult)
                    link(pool.tensor_tensor(RZ[:, r, :], RZ[:, r, :], MH[:, :], ALU.pow))
                    pool.tensor_tensor(NM[:, r, :], NM[:, r, :], RZ[:, r, :], ALU.mult).then_inc(f_rstd, 1)
                if b >= 2 and b % 2 == 0:
                    c = b - 1
                    pool.wait_ge(f_ln, c + 1)
                    x1 = X[:, T * c:T * (c + 1), :]
                    pool.tensor_tensor(x1, x1, FY[c][:, 0], ALU.add).then_inc(f_out[1], 1)


_INS = ['L0_attn_x', 'L0_attn_ln1_w', 'L0_attn_Wq', 'L0_attn_Wk', 'L0_attn_Wv', 'L0_attn_rel_bias', 'L0_attn_scale',
        'L0_attn_Wo', 'L0_attn_ln2_w', 'L0_attn_W1', 'L0_attn_W2', 'L0_ffn_router_w', 'L0_ffn_gate_w', 'L0_ffn_up_w',
        'L0_ffn_down_w']


def kernel(**inputs):
    import concourse.bacc as bacc
    from concourse.bass_utils import run_bass_kernel_spmd

    nc = bacc.Bacc("TRN2", target_bir_lowering=False, num_devices=1)
    arrays, args = {}, []
    for name in _INS:
        a = np.ascontiguousarray(inputs[name])
        arrays[f"in_{name}"] = a
        args.append(nc.dram_tensor(f"in_{name}", a.shape, mybir.dt.from_np(a.dtype), kind="ExternalInput").ap())
    x = inputs['L0_attn_x']
    out = nc.dram_tensor("out", x.shape, mybir.dt.from_np(np.dtype(x.dtype)), kind="ExternalOutput")
    block_kernel(nc, *args, out.ap())
    r = run_bass_kernel_spmd(nc, [arrays], core_ids=[0])
    return r.results[0]["out"]
```
